# Optimizing a Trainium2 kernel written in Bass

```python
import numpy as np
import jax
import jax.numpy as jnp

def _softmax(x, axis=-1):
    return jax.nn.softmax(x, axis=axis)

def _gelu(x):
    return jax.nn.gelu(x, approximate=True)

def _silu(x):
    return jax.nn.silu(x)

def _sigmoid(x):
    return jax.nn.sigmoid(x)

def _layernorm(x, axis=-1, eps=1e-05):
    m = jnp.mean(x, axis=axis, keepdims=True)
    v = jnp.var(x, axis=axis, keepdims=True)
    return (x - m) / jnp.sqrt(v + eps)

def _scatter_add(tgt, idx, src, axis=0):
    return tgt.at[idx].add(src)

def _segment_sum(src, seg, n):
    return jax.ops.segment_sum(src, seg, n)
kernel_name = 'mk_vit_tower_d2_tok_img768_r4_e3bd7b'

def setup_inputs(seed: int=0):
    np.random.seed(seed)
    _w = jnp.asarray

    def _rec_inputs():
        import jax
        import jax.numpy as jnp
        _rk = jax.random.key(seed)
        x = -0.00016672 + 0.999947 * jax.random.normal(jax.random.fold_in(_rk, 1), (128, 3, 64, 64), jnp.float32)
        return x
    x = _rec_inputs()

    def _L0_tok_setup():
        import jax, jax.numpy as jnp
        import numpy as np
        BATCH = 64
        IN_CHANS = 3
        EMBED_DIM = 192
        IMG = 96
        OLD_PS = 32
        NEW_PS = 16

        def _compute_pinv(old_ps: int, new_ps: int) -> jnp.ndarray:
            old_hw = old_ps * old_ps
            basis = jnp.eye(old_hw, dtype=jnp.float32).reshape(old_hw, old_ps, old_ps)
            resize = lambda b: jax.image.resize(b, (new_ps, new_ps), method='cubic', antialias=True)
            resize_matrix = jax.vmap(resize)(basis).reshape(old_hw, new_ps * new_ps)
            return jnp.linalg.pinv(resize_matrix)
        key = jax.random.key(seed)
        k_x, k_w, k_b = jax.random.split(key, 3)
        x = jax.random.normal(k_x, (BATCH, IN_CHANS, IMG, IMG), dtype=jnp.float32)
        proj_weight = 0.02 * jax.random.normal(k_w, (EMBED_DIM, IN_CHANS, OLD_PS, OLD_PS), dtype=jnp.float32)
        proj_bias = 0.02 * jax.random.normal(k_b, (EMBED_DIM,), dtype=jnp.float32)
        pinv = _compute_pinv(OLD_PS, NEW_PS)
        return {'x': x, 'patch_size': NEW_PS, 'proj_weight': proj_weight, 'proj_bias': proj_bias, 'pinv': pinv}
    _L0_tok_all = _L0_tok_setup()
    _L0_tok_in = {k: v for k, v in _L0_tok_all.items() if k in ('proj_weight', 'proj_bias', 'pinv')}
    del _L0_tok_all

    def _L0_attn_setup():
        import math
        import jax, jax.numpy as jnp
        import numpy as np
        B, S, IN_DIM, EMB, H, MAX_LEN = (4, 128, 192, 192, 12, 128)
        D = EMB // H
        key = jax.random.key(seed)
        ks = jax.random.split(key, 16)

        def lin(k, fan_in, fan_out):
            lim = math.sqrt(6.0 / (fan_in + fan_out))
            W = jax.random.uniform(k, (fan_in, fan_out), minval=-lim, maxval=lim, dtype=jnp.float32)
            return (W, jnp.zeros((fan_out,), jnp.float32))
        Wq, bq = lin(ks[0], IN_DIM, EMB)
        Wk, bk = lin(ks[1], IN_DIM, EMB)
        Wv, bv = lin(ks[2], IN_DIM, EMB)
        Wpk, bpk = lin(ks[3], IN_DIM, EMB)
        Wpq, bpq = lin(ks[4], IN_DIM, EMB)
        Wo, bo = lin(ks[5], EMB, IN_DIM)
        rel_table = jax.random.normal(ks[6], (2 * MAX_LEN - 1, IN_DIM), jnp.float32)
        x = jax.random.normal(ks[7], (B, S, IN_DIM), jnp.float32)
        return {'x': x, 'Wq': Wq, 'bq': bq, 'Wk': Wk, 'bk': bk, 'Wv': Wv, 'bv': bv, 'rel_table': rel_table, 'Wpk': Wpk, 'bpk': bpk, 'Wpq': Wpq, 'bpq': bpq, 'Wo': Wo, 'bo': bo}
    _L0_attn_all = _L0_attn_setup()
    _L0_attn_in = {k: v for k, v in _L0_attn_all.items() if k in ('Wq', 'bq', 'Wk', 'bk', 'Wv', 'bv', 'rel_table', 'Wpk', 'bpk', 'Wpq', 'bpq', 'Wo', 'bo')}
    del _L0_attn_all

    def _L0_ffn_setup():
        import jax, jax.numpy as jnp
        import numpy as np
        from jax import lax
        DIM = 192
        INTER = 128
        E = 8
        G = 4
        TOPK_G = 2
        TOPK = 2
        ROUTE_SCALE = 1.0

        def _gate(x2, gate_weight, gate_bias):
            T = x2.shape[0]
            scores = jax.nn.sigmoid(x2 @ gate_weight.T)
            s = scores + gate_bias
            sv = s.reshape(T, G, E // G)
            top2, _ = lax.top_k(sv, 2)
            group_scores = top2.sum(-1)
            _, gidx = lax.top_k(group_scores, TOPK_G)
            gmask = jnp.zeros((T, G), bool).at[jnp.arange(T)[:, None], gidx].set(True)
            masked = jnp.where(gmask[:, :, None], sv, -jnp.inf).reshape(T, E)
            _, idx = lax.top_k(masked, TOPK)
            w = jnp.take_along_axis(scores, idx, axis=1)
            w = w / (w.sum(-1, keepdims=True) + 1e-06) * ROUTE_SCALE
            return (w, idx)
        key = jax.random.key(seed)
        ks = jax.random.split(key, 9)
        s = 1.0 / np.sqrt(DIM)
        si = 1.0 / np.sqrt(INTER)
        return {'x': jax.random.normal(ks[0], (4, 1024, DIM), jnp.float32), 'gate_weight': jax.random.uniform(ks[1], (E, DIM), jnp.float32, -s, s), 'gate_bias': jnp.zeros((E,), jnp.float32), 'w1': jax.random.uniform(ks[2], (E, INTER, DIM), jnp.float32, -s, s), 'w2': jax.random.uniform(ks[3], (E, DIM, INTER), jnp.float32, -si, si), 'w3': jax.random.uniform(ks[4], (E, INTER, DIM), jnp.float32, -s, s), 'sw1': jax.random.uniform(ks[5], (INTER, DIM), jnp.float32, -s, s), 'sw2': jax.random.uniform(ks[6], (DIM, INTER), jnp.float32, -si, si), 'sw3': jax.random.uniform(ks[7], (INTER, DIM), jnp.float32, -s, s)}
    _L0_ffn_all = _L0_ffn_setup()
    _L0_ffn_in = {k: v for k, v in _L0_ffn_all.items() if k in ('gate_weight', 'gate_bias', 'w1', 'w2', 'w3', 'sw1', 'sw2', 'sw3')}
    del _L0_ffn_all

    def _L1_attn_setup():
        import jax, jax.numpy as jnp
        import numpy as np
        NUM_HEADS = 12
        Q_BITS = 8

        def fake_quant(x, bits=Q_BITS):
            qmax = 2.0 ** (bits - 1) - 1.0
            scale = jnp.maximum(jnp.max(jnp.abs(x)) / qmax, 1e-08)
            q = jnp.clip(jnp.round(x / scale), -qmax - 1.0, qmax) * scale
            return x + jax.lax.stop_gradient(q - x)
        key = jax.random.key(seed)
        ks = jax.random.split(key, 5)
        B, N, C = (8, 256, 192)
        x = jax.random.normal(ks[0], (B, N, C), dtype=jnp.float32)
        w_qkv = jax.random.normal(ks[1], (C, 3 * C), dtype=jnp.float32) * 0.02
        b_qkv = jax.random.normal(ks[2], (3 * C,), dtype=jnp.float32) * 0.02
        w_proj = jax.random.normal(ks[3], (C, C), dtype=jnp.float32) * 0.02
        b_proj = jax.random.normal(ks[4], (C,), dtype=jnp.float32) * 0.02
        return {'x': x, 'w_qkv': w_qkv, 'b_qkv': b_qkv, 'w_proj': w_proj, 'b_proj': b_proj}
    _L1_attn_all = _L1_attn_setup()
    _L1_attn_in = {k: v for k, v in _L1_attn_all.items() if k in ('w_qkv', 'b_qkv', 'w_proj', 'b_proj')}
    del _L1_attn_all

    def _L1_ffn_setup():
        import jax, jax.numpy as jnp
        import numpy as np
        D_MODEL = 192
        N_EXPERTS = 8
        TOP_K = 2
        D_FF = 4 * D_MODEL
        key = jax.random.key(seed)
        ks = jax.random.split(key, 6)
        B, S = (2, 512)
        x = jax.random.normal(ks[0], (B, S, D_MODEL), dtype=jnp.float32)
        Wr = jax.random.normal(ks[1], (D_MODEL, N_EXPERTS), dtype=jnp.float32) * 0.02
        W1 = jax.random.normal(ks[2], (N_EXPERTS, D_MODEL, D_FF), dtype=jnp.float32) * 0.02
        b1 = jnp.zeros((N_EXPERTS, D_FF), dtype=jnp.float32)
        W2 = jax.random.normal(ks[3], (N_EXPERTS, D_FF, D_MODEL), dtype=jnp.float32) * 0.02
        b2 = jnp.zeros((N_EXPERTS, D_MODEL), dtype=jnp.float32)
        return {'x': x, 'Wr': Wr, 'W1': W1, 'b1': b1, 'W2': W2, 'b2': b2}
    _L1_ffn_all = _L1_ffn_setup()
    _L1_ffn_in = {k: v for k, v in _L1_ffn_all.items() if k in ('Wr', 'W1', 'b1', 'W2', 'b2')}
    del _L1_ffn_all
    return {'x': x, 'L0_tok_proj_weight': _L0_tok_in['proj_weight'], 'L0_tok_proj_bias': _L0_tok_in['proj_bias'], 'L0_tok_pinv': _L0_tok_in['pinv'], 'L0_attn_Wq': _L0_attn_in['Wq'], 'L0_attn_bq': _L0_attn_in['bq'], 'L0_attn_Wk': _L0_attn_in['Wk'], 'L0_attn_bk': _L0_attn_in['bk'], 'L0_attn_Wv': _L0_attn_in['Wv'], 'L0_attn_bv': _L0_attn_in['bv'], 'L0_attn_rel_table': _L0_attn_in['rel_table'], 'L0_attn_Wpk': _L0_attn_in['Wpk'], 'L0_attn_bpk': _L0_attn_in['bpk'], 'L0_attn_Wpq': _L0_attn_in['Wpq'], 'L0_attn_bpq': _L0_attn_in['bpq'], 'L0_attn_Wo': _L0_attn_in['Wo'], 'L0_attn_bo': _L0_attn_in['bo'], 'L0_ffn_gate_weight': _L0_ffn_in['gate_weight'], 'L0_ffn_gate_bias': _L0_ffn_in['gate_bias'], 'L0_ffn_w1': _L0_ffn_in['w1'], 'L0_ffn_w2': _L0_ffn_in['w2'], 'L0_ffn_w3': _L0_ffn_in['w3'], 'L0_ffn_sw1': _L0_ffn_in['sw1'], 'L0_ffn_sw2': _L0_ffn_in['sw2'], 'L0_ffn_sw3': _L0_ffn_in['sw3'], 'L1_attn_w_qkv': _L1_attn_in['w_qkv'], 'L1_attn_b_qkv': _L1_attn_in['b_qkv'], 'L1_attn_w_proj': _L1_attn_in['w_proj'], 'L1_attn_b_proj': _L1_attn_in['b_proj'], 'L1_ffn_Wr': _L1_ffn_in['Wr'], 'L1_ffn_W1': _L1_ffn_in['W1'], 'L1_ffn_b1': _L1_ffn_in['b1'], 'L1_ffn_W2': _L1_ffn_in['W2'], 'L1_ffn_b2': _L1_ffn_in['b2']}

def reference(x, L0_tok_proj_weight, L0_tok_proj_bias, L0_tok_pinv, L0_attn_Wq, L0_attn_bq, L0_attn_Wk, L0_attn_bk, L0_attn_Wv, L0_attn_bv, L0_attn_rel_table, L0_attn_Wpk, L0_attn_bpk, L0_attn_Wpq, L0_attn_bpq, L0_attn_Wo, L0_attn_bo, L0_ffn_gate_weight, L0_ffn_gate_bias, L0_ffn_w1, L0_ffn_w2, L0_ffn_w3, L0_ffn_sw1, L0_ffn_sw2, L0_ffn_sw3, L1_attn_w_qkv, L1_attn_b_qkv, L1_attn_w_proj, L1_attn_b_proj, L1_ffn_Wr, L1_ffn_W1, L1_ffn_b1, L1_ffn_W2, L1_ffn_b2):
    import jax
    import jax.numpy as jnp

    def _L0_tok_ref(x, patch_size, proj_weight, proj_bias, pinv):
        import jax, jax.numpy as jnp
        import numpy as np
        BATCH = 64
        IN_CHANS = 3
        EMBED_DIM = 192
        IMG = 96
        OLD_PS = 32
        NEW_PS = 16

        def _compute_pinv(old_ps: int, new_ps: int) -> jnp.ndarray:
            old_hw = old_ps * old_ps
            basis = jnp.eye(old_hw, dtype=jnp.float32).reshape(old_hw, old_ps, old_ps)
            resize = lambda b: jax.image.resize(b, (new_ps, new_ps), method='cubic', antialias=True)
            resize_matrix = jax.vmap(resize)(basis).reshape(old_hw, new_ps * new_ps)
            return jnp.linalg.pinv(resize_matrix)
        ps = int(patch_size)
        E, C, oh, ow = proj_weight.shape
        w = jnp.einsum('po,eco->ecp', pinv, proj_weight.reshape(E, C, oh * ow))
        w = w.reshape(E, C, ps, ps)
        B, _, H, W = x.shape
        gh, gw = (H // ps, W // ps)
        xp = x.reshape(B, C, gh, ps, gw, ps)
        out = jnp.einsum('bcipjq,ecpq->bije', xp, w) + proj_bias
        return out.reshape(B, gh * gw, E)

    def _L0_attn_ref(x, Wq, bq, Wk, bk, Wv, bv, rel_table, Wpk, bpk, Wpq, bpq, Wo, bo):
        import math
        import jax, jax.numpy as jnp
        import numpy as np
        B, S, IN_DIM, EMB, H, MAX_LEN = (4, 128, 192, 192, 12, 128)
        D = EMB // H
        Bx, Sx, _ = x.shape

        def shape_heads(t):
            return t.reshape(Bx, Sx, H, D).transpose(0, 2, 1, 3)
        q = shape_heads(x @ Wq + bq)
        k = shape_heads(x @ Wk + bk)
        v = shape_heads(x @ Wv + bv)
        pos = jnp.arange(Sx)
        ids = jnp.clip(pos[:, None] - pos[None, :], -(MAX_LEN - 1), MAX_LEN - 1) + (MAX_LEN - 1)
        pos_k = (rel_table @ Wpk + bpk)[ids].reshape(Sx, Sx, H, D)
        pos_q = (rel_table @ Wpq + bpq)[ids].reshape(Sx, Sx, H, D)
        scores = jnp.einsum('bhid,bhjd->bhij', q, k)
        scores = scores + jnp.einsum('bhid,ijhd->bhij', q, pos_k)
        scores = scores + jnp.einsum('ijhd,bhjd->bhij', pos_q, k)
        scores = scores / math.sqrt(D * 3.0)
        attn = jax.nn.softmax(scores, axis=-1)
        out = jnp.einsum('bhij,bhjd->bhid', attn, v)
        out = out.transpose(0, 2, 1, 3).reshape(Bx, Sx, EMB)
        return out @ Wo + bo

    def _L0_ffn_ref(x, gate_weight, gate_bias, w1, w2, w3, sw1, sw2, sw3):
        import jax, jax.numpy as jnp
        import numpy as np
        from jax import lax
        DIM = 192
        INTER = 128
        E = 8
        G = 4
        TOPK_G = 2
        TOPK = 2
        ROUTE_SCALE = 1.0

        def _gate(x2, gate_weight, gate_bias):
            T = x2.shape[0]
            scores = jax.nn.sigmoid(x2 @ gate_weight.T)
            s = scores + gate_bias
            sv = s.reshape(T, G, E // G)
            top2, _ = lax.top_k(sv, 2)
            group_scores = top2.sum(-1)
            _, gidx = lax.top_k(group_scores, TOPK_G)
            gmask = jnp.zeros((T, G), bool).at[jnp.arange(T)[:, None], gidx].set(True)
            masked = jnp.where(gmask[:, :, None], sv, -jnp.inf).reshape(T, E)
            _, idx = lax.top_k(masked, TOPK)
            w = jnp.take_along_axis(scores, idx, axis=1)
            w = w / (w.sum(-1, keepdims=True) + 1e-06) * ROUTE_SCALE
            return (w, idx)
        B, S, D = x.shape
        x2 = x.reshape(-1, D)
        T = x2.shape[0]
        weights, indices = _gate(x2, gate_weight, gate_bias)
        cw = jnp.zeros((T, E), x.dtype).at[jnp.arange(T)[:, None], indices].add(weights)
        h1 = jnp.einsum('td,eid->tei', x2, w1)
        h3 = jnp.einsum('td,eid->tei', x2, w3)
        h = jax.nn.silu(h1) * h3
        y = jnp.einsum('tei,edi,te->td', h, w2, cw)
        z = jax.nn.silu(x2 @ sw1.T) * (x2 @ sw3.T) @ sw2.T
        return (y + z).reshape(B, S, D)

    def _L1_attn_ref(x, w_qkv, b_qkv, w_proj, b_proj):
        import jax, jax.numpy as jnp
        import numpy as np
        NUM_HEADS = 12
        Q_BITS = 8

        def fake_quant(x, bits=Q_BITS):
            qmax = 2.0 ** (bits - 1) - 1.0
            scale = jnp.maximum(jnp.max(jnp.abs(x)) / qmax, 1e-08)
            q = jnp.clip(jnp.round(x / scale), -qmax - 1.0, qmax) * scale
            return x + jax.lax.stop_gradient(q - x)
        B, N, C = x.shape
        H = NUM_HEADS
        hd = C // H
        scale = hd ** (-0.5)
        qkv = fake_quant(x) @ fake_quant(w_qkv) + b_qkv
        qkv = qkv.reshape(B, N, 3, H, hd).transpose(2, 0, 3, 1, 4)
        q, k, v = (qkv[0], qkv[1], qkv[2])
        attn = jnp.einsum('bhnd,bhmd->bhnm', fake_quant(q), fake_quant(k))
        attn = attn * scale
        attn = fake_quant(jax.nn.softmax(attn, axis=-1))
        out = jnp.einsum('bhnm,bhmd->bhnd', attn, fake_quant(v))
        out = out.transpose(0, 2, 1, 3).reshape(B, N, C)
        out = fake_quant(out) @ fake_quant(w_proj) + b_proj
        return out

    def _L1_ffn_ref(x, Wr, W1, b1, W2, b2):
        import jax, jax.numpy as jnp
        import numpy as np
        D_MODEL = 192
        N_EXPERTS = 8
        TOP_K = 2
        D_FF = 4 * D_MODEL
        B, S, D = x.shape
        T = B * S
        x_flat = x.reshape(T, D)
        gate_logits = x_flat @ Wr
        topw, topi = jax.lax.top_k(gate_logits, TOP_K)
        topw = jax.nn.softmax(topw, axis=-1)
        combine = jnp.zeros((T, N_EXPERTS), dtype=x.dtype)
        combine = combine.at[jnp.arange(T)[:, None], topi].add(topw)
        h = jax.nn.relu(jnp.einsum('td,edh->eth', x_flat, W1) + b1[:, None, :])
        y = jnp.einsum('eth,ehd->etd', h, W2) + b2[:, None, :]
        out = jnp.einsum('te,etd->td', combine, y)
        return out.reshape(B, S, D)
    h = _L0_tok_ref(x, 16, L0_tok_proj_weight, L0_tok_proj_bias, L0_tok_pinv)
    h = h + _L0_attn_ref(_layernorm(h, axis=-1), L0_attn_Wq, L0_attn_bq, L0_attn_Wk, L0_attn_bk, L0_attn_Wv, L0_attn_bv, L0_attn_rel_table, L0_attn_Wpk, L0_attn_bpk, L0_attn_Wpq, L0_attn_bpq, L0_attn_Wo, L0_attn_bo)
    h = h + _L0_ffn_ref(_layernorm(h, axis=-1), L0_ffn_gate_weight, L0_ffn_gate_bias, L0_ffn_w1, L0_ffn_w2, L0_ffn_w3, L0_ffn_sw1, L0_ffn_sw2, L0_ffn_sw3)
    h = h + _L1_attn_ref(_layernorm(h, axis=-1), L1_attn_w_qkv, L1_attn_b_qkv, L1_attn_w_proj, L1_attn_b_proj)
    h = h + _L1_ffn_ref(_layernorm(h, axis=-1), L1_ffn_Wr, L1_ffn_W1, L1_ffn_b1, L1_ffn_W2, L1_ffn_b2)
    return h

_drawn_inputs = setup_inputs


def setup_inputs(seed=0):
    import zlib

    import numpy as np

    out = dict(_drawn_inputs(seed))
    spreads = {'L0_attn_bq': (0.0, 0.408),
     'L0_attn_bk': (0.0, 0.534),
     'L0_attn_bv': (0.0, 0.1),
     'L0_attn_bpk': (0.0, 0.8),
     'L0_attn_bpq': (0.0, 0.523),
     'L0_attn_bo': (0.0, 0.1),
     'L0_ffn_gate_bias': (0.0, 0.1),
     'L1_ffn_b1': (0.0, 0.445),
     'L1_ffn_b2': (0.0, 0.1)}
    factors = {'L0_tok_proj_bias': 2.969,
     'L1_attn_w_qkv': 3.183,
     'L1_attn_b_qkv': 8.0,
     'L1_attn_w_proj': 3.11,
     'L1_attn_b_proj': 3.832}
    for name, (base, spread) in spreads.items():
        noise = np.random.default_rng([zlib.crc32(name.encode()), seed]).standard_normal(out[name].shape)
        drawn = base * np.exp(spread * noise) if base else spread * noise
        out[name] = jnp.asarray(drawn.astype(out[name].dtype))
    for name, factor in factors.items():
        out[name] = (out[name] * factor).astype(out[name].dtype)
    return out
```

```python
from contextlib import ExitStack

import concourse.bass as bass
from concourse import mybir

F32 = mybir.dt.float32
BF16 = mybir.dt.bfloat16
ALU = mybir.AluOpType
ACT = mybir.ActivationFunctionType
AX = mybir.AxisListType
RMAX = bass.bass_isa.ReduceOp.max

P = 128
IMAGES, CHANS, SIDE, PATCH, OLD = 128, 3, 64, 16, 32
S = (SIDE // PATCH) ** 2
T = IMAGES * S
NT = T // P
IPT = P // S
BLK = 512
NB = T // BLK
TPB = BLK // P
E = 192
EH = E // 2
H, D = 12, 16
HG = H // 2
KC = CHANS * PATCH * PATCH // P
OC = OLD * OLD // P
REL = 2 * S - 1
NE0, INTER = 8, 128
GROUPS = 4
NE1, FF = 8, 768
FC = FF // P
EPS = 1e-5
SOFT0 = 1.0 / (3.0 * D) ** 0.5
SOFT1 = D ** -0.5
QMAX = 127.0
ROUND = 1.5 * 2.0 ** 23


def ds(start, size):
    return bass.ds(start, size)


def wait(eng, semaphore, count):
    if isinstance(count, int) and count <= 0:
        return
    eng.wait_ge(semaphore, count)


def wait_alone(eng, semaphore, count, passed):
    wait(eng, semaphore, count)
    if not isinstance(count, int):
        eng.sem_inc(passed, 1)


def in_slot(t, u):
    return 8 * (t - u) + 16


def steps(eng, n, stages):
    deepest = max(lag for _, lag in stages)
    head = deepest + 2 + deepest % 2

    def fixed(s):
        for stage, lag in stages:
            if 0 <= s - lag < n:
                stage(s - lag, (s - lag) % 2)

    for s in range(head):
        fixed(s)
    with eng.Fori(head, n - 1, 2) as s0:
        for v in range(2):
            for stage, lag in stages:
                stage(s0 + (v - lag), (v - lag) % 2)
    for s in range(n, n + deepest):
        fixed(s)


def tower(nc, a, out):
    ctx = ExitStack()
    with ctx:
        def sb(name, shape, dt=F32):
            return ctx.enter_context(nc.sbuf_tensor(name, shape, dt))

        def sem(name):
            return ctx.enter_context(nc.semaphore(name))

        h = sb("h", [P, NT, E])
        xnT = sb("xnT", [P, 2 * T])
        qT = sb("qT", [P, 2 * T])
        kT = sb("kT", [P, 2 * T])
        sT = sb("sT", [P, 2 * T])
        big = sb("big", [P, 2 * T + S * E])
        ident = sb("ident", [P, P])
        ident16 = sb("ident16", [P, P], BF16)
        hmask = sb("hmask", [EH, HG])
        hmask16 = sb("hmask16", [EH, HG], BF16)
        lower4 = sb("lower4", [P, GROUPS * GROUPS])
        lower8 = sb("lower8", [P, 64])
        tokb = sb("tokb", [P, E])
        wtok = sb("wtok", [P, KC, E])
        wq = sb("wq", [EH, 2, E])
        wk = sb("wk", [EH, 2, E])
        wv = sb("wv", [EH, 2, E])
        wo = sb("wo", [EH, 2, E])
        wpk = sb("wpk", [EH, 2, E])
        wpq = sb("wpq", [EH, 2, E])
        relr = sb("relr", [EH, 2, REL])
        relf = sb("relf", [EH, 2, REL])
        colb = sb("colb", [EH, 4, 2])
        bv = sb("bv", [P, E])
        bo = sb("bo", [P, E])
        bproj = sb("bproj", [P, E])
        bv1 = sb("bv1", [P, E])
        bqk1 = sb("bqk1", [EH, 2, 2])
        gate0 = sb("gate0", [EH, 2, NE0])
        gate1 = sb("gate1", [EH, 2, NE1])
        gbias = sb("gbias", [P, NE0])
        w13 = sb("w13", [EH, 2, NE0 + 1, 2, INTER])
        w2 = sb("w2", [INTER, NE0 + 1, E])
        b1c = sb("b1c", [P, NE1 * FC])
        b2r = sb("b2r", [NE1, E])
        pkbd = sb("pkbd", [EH, 2, HG, REL])
        pqbd = sb("pqbd", [EH, 2, HG, REL])
        pos = sb("pos", [EH, 2, 2, REL])
        eps = sb("eps", [P, 1])
        rounding = sb("rounding", [P, 2])
        moments = sb("moments", [P, 2, 6])
        meanvar = sb("meanvar", [P, 2, 2])
        sdev = sb("sdev", [P, 2])
        rstd = sb("rstd", [P, 2])
        xn = sb("xn", [P, 2, E])
        xt = sb("xt", [EH, 2, 2, P])
        vt = sb("vt", [P, 2, E])
        kbd = sb("kbd", [EH, 2, 2, IPT * EH])
        vbd = sb("vbd", [EH, 2, 2, IPT, EH])
        st1 = sb("st1", [EH, 2, 2, P])
        ot = sb("ot", [EH, 2, 2, P])
        scores = sb("scores", [P, 2, 2 * E])
        top = sb("top", [P, 2, 2 * H])
        mass = sb("mass", [P, 2, 2 * H])
        logits = sb("logits", [P, NT, NE0])
        comb = sb("comb", [P, NT, NE0 + 1])
        rt = [sb(f"rt{i}", [P, NT, NE0]) for i in range(3)]
        small = sb("small", [P, NT, 2])
        v16 = sb("v16", [P, 2, E], BF16)
        combc = sb("combc", [P, 2, NE1])
        combT = sb("combT", [NE1, 2, P])
        stats = sb("stats", [P, 8, NT])
        peak = sb("peak", [P, 8])
        peaks = sb("peaks", [P, 8])
        qs = sb("qs", [P, 8])
        qi = sb("qi", [P, 8])
        prod = sb("prod", [P, 4])
        bank = [ctx.enter_context(nc.psum_tensor(f"bank{i}", [P, 512], F32)) for i in range(8)]

        def halves(buf, width=T):
            return buf[0:EH, :].rearrange("p (g t) -> p g t", g=2)

        xnT_v = halves(xnT)
        qT_v, kT_v, sT_v = halves(qT), halves(kT), halves(sT)
        pinv_v = big[:, 0:OC * 256].rearrange("p (o k) -> p o k", o=OC)
        pw_v = big[:, OC * 256:OC * 256 + OC * CHANS * E].rearrange("p (o k) -> p o k", o=OC)
        pT_v = big[0:EH, 0:2 * T].rearrange("p (g t) -> p g t", g=2)
        t2 = big[:, 2 * T:2 * T + S * E].rearrange("p (i k) -> p i k", i=S)
        xall = t2
        vall = sT[:, 0:NT * E].rearrange("p (n e) -> p n e", n=NT)
        q16 = xnT[0:EH, 0:2 * P].bitcast(BF16).rearrange("p (u g t) -> p u g t", u=2, g=2)
        k16 = xnT[0:EH, 2 * P:4 * P].bitcast(BF16).rearrange("p (u g t) -> p u g t", u=2, g=2)
        wqkv32 = big[0:EH, 0:6 * E].rearrange("p (c n) -> p c n", c=2)
        wproj32 = big[0:EH, 6 * E:8 * E].rearrange("p (c n) -> p c n", c=2)
        wqkv16 = big[0:EH, 8 * E:11 * E].bitcast(BF16).rearrange("p (c n) -> p c n", c=2)
        wproj16 = big[0:EH, 11 * E:12 * E].bitcast(BF16).rearrange("p (c n) -> p c n", c=2)
        wround = big[0:EH, 12 * E:18 * E].rearrange("p (c n) -> p c n", c=2)
        hidden1 = kT[:, 0:FC * 512].rearrange("p (c t) -> p c t", c=FC)
        w1s = qT[0:EH, 0:2 * 2 * FF].rearrange("p (u c f) -> p u c f", u=2, c=2)
        w2s = sT[:, 0:2 * FC * E].rearrange("p (u c e) -> p u c e", u=2, c=FC)
        hidden0 = qT[:, 0:3 * 512].rearrange("p (u t) -> p u t", u=3)
        silu0 = qT[:, 3 * 512:6 * 512].rearrange("p (u t) -> p u t", u=3)
        pairs = big[:, 0:NT * 64]
        ties = big[:, NT * 64:2 * NT * 64]
        x16 = scores[:, :, :].bitcast(BF16)
        vbd16 = vbd[:, :, :, :, :].rearrange("p u g b k -> p u (g b k)").bitcast(BF16)
        kbd16 = kbd[:, :, :, :].rearrange("p u g k -> p u (g k)").bitcast(BF16)

        v_scr = nc.dram_tensor("v_scratch", [T, E], F32, kind="Internal").ap()
        v_scr16 = nc.dram_tensor("v_scratch16", [T, E], BF16, kind="Internal").ap()

        passed = sem("passed")

        def moments_of(dve, t, u, steps_done, written, written_count):
            wait_alone(dve, written, written_count, passed)
            nc.vector.bn_stats(moments[:, u, :], h[:, ds(t, 1), :].rearrange("p a e -> p (a e)"))\
                .then_inc(steps_done, 1)
            wait_alone(dve, steps_done, 2 * t + 1, passed)
            nc.vector.bn_aggr(meanvar[:, u, :], moments[:, u, :]).then_inc(steps_done, 1)

        def sdev_of(act, t, u, steps_done, sdev_ready, inverted):
            act.wait_ge(steps_done, 2 * t + 2)
            wait(act, inverted, t - 1)
            nc.scalar.activation(sdev[:, u:u + 1], meanvar[:, u, 1:2], ACT.Sqrt, bias=eps[:, 0:1])\
                .then_inc(sdev_ready, 1)

        def normalise(dve, t, u, sdev_ready, inverted, xn_ready, dest):
            dve.wait_ge(sdev_ready, t + 1)
            nc.vector.reciprocal(rstd[:, u:u + 1], sdev[:, u:u + 1]).then_inc(inverted, 1)
            dve.wait_ge(inverted, t + 1)
            nc.vector.tensor_scalar(dest, h[:, ds(t, 1), :].rearrange("p a e -> p (a e)"),
                                    meanvar[:, u, 0:1], rstd[:, u:u + 1], ALU.subtract, ALU.mult)\
                .then_inc(xn_ready, 1)

        consts = sem("consts")
        tokw = [sem(f"tokw{i}") for i in range(4)]
        wtok_ps = sem("wtok_ps")
        wtok_done = sem("wtok_done")
        pos_ps = sem("pos_ps")
        pos_sb = sem("pos_sb")
        pos_bd = sem("pos_bd")
        cleared = sem("cleared")
        LOADS = [(ident, "ident"), (hmask, "hmask"), (lower4, "lower4"), (lower8, "lower8"),
                 (wpk, "L0_attn_Wpk"), (wpq, "L0_attn_Wpq"), (relr, "rel_reversed"), (relf, "rel"),
                 (colb, "L0_attn_columns"), (wq, "L0_attn_Wq"), (wk, "L0_attn_Wk"), (wv, "L0_attn_Wv"),
                 (wo, "L0_attn_Wo"), (gate0, "L0_ffn_gate_weight"), (gate1, "L1_ffn_Wr"),
                 (bqk1, "L1_attn_columns"), (w13, "L0_ffn_w13"), (w2, "L0_ffn_w2"), (b1c, "L1_ffn_b1"),
                 (b2r, "L1_ffn_b2")]
        ROWS = [(tokb, "L0_tok_proj_bias"), (bv, "L0_attn_bv"), (bo, "L0_attn_bo"),
                (bproj, "L1_attn_b_proj"), (bv1, "L1_attn_b_v"), (gbias, "L0_ffn_gate_bias")]

        def whole(buf):
            return buf[(slice(None),) * len(buf.shape)]

        with nc.Block() as block:
            @block.sync
            def _(sp):
                pinv_d = a["L0_tok_pinv"]
                pw_d = a["L0_tok_proj_weight"]
                for i in range(4):
                    sp.dma_start(pinv_v[:, 2 * i:2 * i + 2, :], pinv_d[:, 2 * i:2 * i + 2, :]).then_inc(tokw[i], 16)
                    sp.dma_start(pw_v[:, 2 * i:2 * i + 2, :], pw_d[:, 2 * i:2 * i + 2, :]).then_inc(tokw[i], 16)

            @block.gpsimd
            def _(pool):
                nc.gpsimd.memset(eps[:, :], EPS).then_inc(cleared, 1)
                nc.gpsimd.memset(rounding[:, 0:1], ROUND).then_inc(cleared, 1)
                nc.gpsimd.memset(rounding[:, 1:2], -ROUND).then_inc(cleared, 1)
                nc.gpsimd.memset(comb[:, :, :], 1.0).then_inc(cleared, 1)
                nc.gpsimd.memset(stats[:, :, :], 0.0).then_inc(cleared, 1)

            @block.scalar
            def _(act):
                for buf, name in LOADS:
                    act.dma_start(whole(buf), a[name]).then_inc(consts, 16)
                for buf, name in ROWS:
                    act.dma_start(buf[:, :], a[name].partition_broadcast(P)).then_inc(consts, 16)
                act.wait_ge(consts, 16 * len(LOADS + ROWS))
                for n in range(4):
                    act.wait_ge(pos_ps, 4)
                    nc.scalar.activation(pos[:, n // 2, n % 2, :], bank[6][0:EH, 32 * n:32 * n + REL],
                                         ACT.Identity, bias=colb[:, 2 + n // 2, n % 2:n % 2 + 1]).then_inc(pos_sb, 1)
                nc.scalar.activation(ident16[:, :], ident[:, :], ACT.Copy).then_inc(pos_sb, 1)
                nc.scalar.activation(hmask16[:, :], hmask[:, :], ACT.Copy).then_inc(pos_sb, 1)

            @block.tensor
            def _(pe):
                pe.wait_ge(consts, 16 * len(LOADS + ROWS))
                for n, (w, rel) in enumerate(((wpk, relr), (wpk, relr), (wpq, relf), (wpq, relf))):
                    g = n % 2
                    for c in range(2):
                        mm = nc.tensor.matmul(bank[6][0:EH, 32 * n:32 * n + REL], w[:, c, g * EH:(g + 1) * EH],
                                              rel[:, c, :], start=(c == 0), stop=(c == 1))
                    mm.then_inc(pos_ps, 1)
                for o in range(OC):
                    if o % 2 == 0:
                        pe.wait_ge(tokw[o // 2], 32)
                    for k in range(KC):
                        c, half = k // 2, k % 2
                        mm = nc.tensor.matmul(bank[k][:, 0:E], pinv_v[:, o, half * P:(half + 1) * P],
                                              pw_v[:, o, c * E:(c + 1) * E], start=(o == 0), stop=(o == OC - 1))
                        if o == OC - 1:
                            mm.then_inc(wtok_ps, 1)

            @block.vector
            def _(dve):
                for n in range(4):
                    dve.wait_ge(pos_sb, n + 1)
                    dest = (pkbd, pqbd)[n // 2]
                    nc.vector.tensor_tensor(
                        dest[:, n % 2, :, :],
                        pos[:, n // 2, n % 2, :].unsqueeze(1).broadcast_to([EH, HG, REL]),
                        hmask[:, :].unsqueeze(2).broadcast_to([EH, HG, REL]), ALU.mult).then_inc(pos_bd, 1)
                for k in range(KC):
                    dve.wait_ge(wtok_ps, k + 1)
                    nc.vector.tensor_copy(wtok[:, k, :], bank[k][:, 0:E]).then_inc(wtok_done, 1)

        x_loaded = [sem(f"x_loaded{u}") for u in range(2)]
        embedded, h_done, ln1, sdev1, inv1, xn1, tr1, xt1 = (sem(n) for n in (
            "embedded", "h_done", "ln1", "sdev1", "inv1", "xn1", "tr1", "xt1"))
        qk_ps, v_ps, qk_sb, v_sb, kbd_done, s_ps, s_sb = (sem(n) for n in (
            "qk_ps", "v_ps", "qk_sb", "v_sb", "kbd_done", "s_ps", "s_sb"))
        v_stored = [sem(f"v_stored{u}") for u in range(2)]
        xload = ctx.enter_context(nc.sbuf_tensor("xload", [P, 2, KC * P], F32))

        with nc.Block() as block:
            @block.sync
            def _(sp):
                def load(t, u):
                    wait(sp, embedded, t - 1)
                    sp.dma_start(xload[:, u, :], a["x"][ds(t, 1), :, :].rearrange("a p k -> p (a k)"))\
                        .then_inc(x_loaded[u], 16)

                steps(sp, NT, [(load, 0)])

            @block.gpsimd
            def _(pool):
                def store(t, u):
                    pool.wait_ge(v_sb, t + 1)
                    pool.dma_start(v_scr[ds(t * P, P), :], vt[:, u, :]).then_inc(v_stored[u], 16)

                steps(pool, NT, [(store, 0)])
                for u in range(2):
                    pool.wait_ge(v_stored[u], 8 * NT)

            @block.tensor
            def _(pe):
                def transpose(t, u):
                    pe.wait_ge(xn1, t + 1)
                    wait(pe, xt1, t)
                    for c in range(2):
                        mm = nc.tensor.transpose(bank[2][0:EH, c * P:(c + 1) * P], xn[:, u, c * EH:(c + 1) * EH],
                                                 ident[:, :])
                    mm.then_inc(tr1, 1)

                def embed(t, u):
                    pe.wait_ge(x_loaded[u], in_slot(t, u))
                    wait(pe, h_done, t - 1)
                    for k in range(KC):
                        mm = nc.tensor.matmul(bank[u][:, 0:E], xload[:, u, k * P:(k + 1) * P], wtok[:, k, :],
                                              start=(k == 0), stop=(k == KC - 1))
                    mm.then_inc(embedded, 1)

                def project(t, u):
                    pe.wait_ge(xt1, t + 1)
                    wait(pe, qk_sb, 4 * t)
                    for n, w in enumerate((wq, wq, wk, wk)):
                        for c in range(2):
                            mm = nc.tensor.matmul(bank[3][0:EH, n * P:(n + 1) * P],
                                                  w[:, c, (n % 2) * EH:(n % 2 + 1) * EH], xt[:, u, c, :],
                                                  start=(c == 0), stop=(c == 1))
                    mm.then_inc(qk_ps, 1)
                    wait(pe, v_sb, t)
                    for c in range(2):
                        mm = nc.tensor.matmul(bank[4][:, 0:E], xt[:, u, c, :], wv[:, c, :],
                                              start=(c == 0), stop=(c == 1))
                    mm.then_inc(v_ps, 1)

                def score(t, u):
                    pe.wait_ge(kbd_done, 2 * t + 2)
                    pe.wait_ge(qk_sb, 4 * t + 4)
                    wait(pe, s_sb, t - 1)
                    for g in range(2):
                        for b in range(IPT):
                            mm = nc.tensor.matmul(bank[5 + u][0:EH, g * P + b * S:g * P + (b + 1) * S],
                                                  kbd[:, u, g, b * EH:(b + 1) * EH],
                                                  qT_v[:, g, ds(t * P + b * S, S)], start=True, stop=True)
                    mm.then_inc(s_ps, 1)

                steps(pe, NT, [(score, 5), (project, 3), (transpose, 2), (embed, 0)])

            @block.scalar
            def _(act):
                def copy_x(t, u):
                    act.wait_ge(tr1, t + 1)
                    wait(act, v_ps, t - 1)
                    nc.scalar.activation(xt[:, u, :, :].rearrange("p c t -> p (c t)"), bank[2][0:EH, 0:2 * P],
                                         ACT.Copy).then_inc(xt1, 1)

                def deviation(t, u):
                    sdev_of(act, t, u, ln1, sdev1, inv1)

                def copy_qk(t, u):
                    act.wait_ge(qk_ps, t + 1)
                    for n in range(4):
                        dest = (qT_v, kT_v)[n // 2]
                        nc.scalar.activation(dest[:, n % 2, ds(t * P, P)], bank[3][0:EH, n * P:(n + 1) * P],
                                             ACT.Identity, bias=colb[:, n // 2, n % 2:n % 2 + 1]).then_inc(qk_sb, 1)

                def copy_s(t, u):
                    act.wait_ge(s_ps, t + 1)
                    nc.scalar.activation(sT_v[:, :, ds(t * P, P)],
                                         bank[5 + u][0:EH, 0:2 * P].rearrange("p (g t) -> p g t", g=2),
                                         ACT.Copy).then_inc(s_sb, 1)

                steps(act, NT, [(copy_s, 5), (copy_qk, 3), (copy_x, 2), (deviation, 0)])

            @block.vector
            def _(dve):
                def norm(t, u):
                    wait(dve, tr1, t - 1)
                    normalise(dve, t, u, sdev1, inv1, xn1, xn[:, u, :])

                def residual(t, u):
                    dve.wait_ge(embedded, t + 1)
                    nc.vector.tensor_tensor(h[:, ds(t, 1), :].rearrange("p a e -> p (a e)"), bank[u][:, 0:E],
                                            tokb[:, :], ALU.add).then_inc(h_done, 1)
                    moments_of(dve, t, u, ln1, h_done, t + 1)

                def values(t, u):
                    dve.wait_ge(v_ps, t + 1)
                    wait(dve, v_stored[u], in_slot(t, u) - 16)
                    nc.vector.tensor_tensor(vt[:, u, :], bank[4][:, 0:E], bv[:, :], ALU.add).then_inc(v_sb, 1)

                def keys(t, u):
                    wait(dve, s_ps, t - 1)
                    dve.wait_ge(qk_sb, 4 * t + 4)
                    for g in range(2):
                        nc.vector.tensor_tensor(
                            kbd[:, u, g, :].rearrange("p (b m j) -> p b m j", b=IPT, m=HG),
                            kT_v[:, g, ds(t * P, P)].rearrange("p (b j) -> p b j", b=IPT).unsqueeze(2)
                            .broadcast_to([EH, IPT, HG, S]),
                            hmask[:, :].unsqueeze(1).unsqueeze(3).broadcast_to([EH, IPT, HG, S]),
                            ALU.mult).then_inc(kbd_done, 1)

                steps(dve, NT, [(keys, 4), (values, 3), (norm, 1), (residual, 0)])

        ki_done, t2_ps, t2_sb, qs_done, d_ps, p_done, pt_ps, pt_sb, sm = (sem(n) for n in (
            "ki_done", "t2_ps", "t2_sb", "qs_done", "d_ps", "p_done", "pt_ps", "pt_sb", "sm"))
        ss_done, exp_done, share_done = sem("ss_done"), sem("exp_done"), sem("share_done")
        stage = kbd[:, :, :, :].rearrange("p u g k -> p (u g k)")[:, 0:16 * P]\
            .rearrange("p (u i k g b) -> p u i k g b", u=2, i=2, k=2, g=2)

        def at_position(buf, i):
            return buf.rearrange("p g (b i) -> p g b i", i=S)[:, :, :, ds(i, 1)].rearrange("p g b i -> p g (b i)")

        with nc.Block() as block:
            @block.gpsimd
            def _(pool):
                def keys(j, u):
                    wait(pool, t2_ps, j - 1)
                    nc.gpsimd.tensor_copy(stage[:, u, 0, 0, :, :], at_position(kT_v, j)).then_inc(ki_done, 1)

                steps(pool, S, [(keys, 0)])

                def queries(n, u):
                    if isinstance(n, int) and n < 2:
                        pool.wait_ge(t2_ps, S)
                    wait(pool, d_ps, n - 1)
                    for i in range(2):
                        nc.gpsimd.tensor_copy(stage[:, u, i, 0, :, :], at_position(qT_v, 2 * n + i))\
                            .then_inc(qs_done, 1)

                steps(pool, S // 2, [(queries, 0)])

            @block.tensor
            def _(pe):
                def key_terms(j, u):
                    pe.wait_ge(ki_done, j + 1)
                    wait_alone(pe, t2_sb, j - 1, passed)
                    for g in range(2):
                        mm = nc.tensor.matmul(bank[u][:, g * EH:(g + 1) * EH], stage[:, u, 0, 0, g, :],
                                              pqbd[:, g, :, ds(S - 1 - j, S)], start=True, stop=True)
                    mm.then_inc(t2_ps, 1)

                steps(pe, S, [(key_terms, 0)])

                def query_terms(n, u):
                    pe.wait_ge(qs_done, 2 * n + 2)
                    pe.wait_ge(ss_done, 2 * n + 2)
                    wait_alone(pe, sm, 4 * n - 7, passed)
                    for i in range(2):
                        for g in range(2):
                            region = bank[2 + u][:, i * E + g * EH:i * E + (g + 1) * EH]
                            nc.tensor.matmul(region, stage[:, u, i, 0, g, :],
                                             pkbd[:, g, :, ds(S - 1 - i - 2 * n, S)], start=True, stop=False)
                            mm = nc.tensor.matmul(region, stage[:, u, i, 1, g, :], ident[0:EH, 0:EH],
                                                  start=False, stop=True)
                    mm.then_inc(d_ps, 1)

                def turn(n, u):
                    pe.wait_ge(p_done, n + 1)
                    wait(pe, pt_sb, n - 1)
                    for m in range(4):
                        mm = nc.tensor.transpose(bank[4 + u][0:EH, m * P:(m + 1) * P],
                                                 scores[:, u, m * EH:(m + 1) * EH], ident[:, :])
                    mm.then_inc(pt_ps, 1)

                steps(pe, S // 2, [(turn, 2), (query_terms, 1)])

            @block.scalar
            def _(act):
                def keep_t2(j, u):
                    act.wait_ge(t2_ps, j + 1)
                    nc.scalar.activation(
                        t2.rearrange("p i (m j) -> p i m j", m=H)[:, :, :, ds(j, 1)].rearrange("p i m j -> p i (m j)"),
                        bank[u][:, 0:E].rearrange("p (m i) -> p i m", m=H), ACT.Copy).then_inc(t2_sb, 1)

                steps(act, S, [(keep_t2, 0)])

                def stage_scores(n, u):
                    wait(act, d_ps, n - 1)
                    for i in range(2):
                        nc.scalar.activation(stage[:, u, i, 1, :, :], at_position(sT_v, 2 * n + i), ACT.Copy)\
                            .then_inc(ss_done, 1)

                def exponent(n, u):
                    act.wait_ge(sm, 4 * n + 3)
                    nc.scalar.activation(scores[:, u, :], scores[:, u, :], ACT.Exp, scale=SOFT0).then_inc(exp_done, 1)

                def keep_p(n, u):
                    act.wait_ge(pt_ps, n + 1)
                    for i in range(2):
                        dest = pT_v.rearrange("p g (b i) -> p g b i", i=S)[:, :, :, ds(2 * n + i, 1)]\
                            .rearrange("p g b i -> p g (b i)")
                        ins = nc.scalar.activation(
                            dest, bank[4 + u][0:EH, i * 2 * P:(i + 1) * 2 * P].rearrange("p (g b) -> p g b", g=2),
                            ACT.Copy)
                    ins.then_inc(pt_sb, 1)

                steps(act, S // 2, [(keep_p, 3), (stage_scores, 0), (exponent, 1)])

            @block.vector
            def _(dve):
                dve.wait_ge(t2_sb, S)

                def by_head(buf):
                    return buf.rearrange("p (m j) -> p m j", j=S)

                def spread(buf):
                    return buf.unsqueeze(2).broadcast_to([P, 2 * H, S])

                def shift(n, u):
                    dve.wait_ge(d_ps, n + 1)
                    wait(dve, pt_ps, n - 1)
                    nc.vector.tensor_tensor(scores[:, u, :], bank[2 + u][:, 0:2 * E],
                                            t2[:, ds(2 * n, 2), :].rearrange("p i k -> p (i k)"),
                                            ALU.add).then_inc(sm, 1)
                    dve.wait_ge(sm, 4 * n + 1)
                    nc.vector.tensor_reduce(top[:, u, :], by_head(scores[:, u, :]), AX.X, ALU.max).then_inc(sm, 1)
                    dve.wait_ge(sm, 4 * n + 2)
                    nc.vector.tensor_tensor(by_head(scores[:, u, :]), by_head(scores[:, u, :]),
                                            spread(top[:, u, :]), ALU.subtract).then_inc(sm, 1)

                def share(n, u):
                    dve.wait_ge(exp_done, n + 1)
                    nc.vector.tensor_reduce(mass[:, u, :], by_head(scores[:, u, :]), AX.X, ALU.add).then_inc(sm, 1)
                    dve.wait_ge(sm, 4 * n + 4)
                    nc.vector.reciprocal(top[:, u, :], mass[:, u, :]).then_inc(share_done, 1)
                    dve.wait_ge(share_done, n + 1)
                    nc.vector.tensor_tensor(by_head(scores[:, u, :]), by_head(scores[:, u, :]),
                                            spread(top[:, u, :]), ALU.mult).then_inc(p_done, 1)

                steps(dve, S // 2, [(share, 2), (shift, 1)])

        def tail_sems(tag):
            return {n: sem(n + tag) for n in (
                "moments", "sdev", "inverse", "xn", "turned", "xt", "gathered", "gate_ps", "gate_sb")}

        def tail_on_pe(pe, s, gate_w):
            def turn(t, u):
                pe.wait_ge(s["xn"], t + 1)
                wait(pe, s["xt"], t - 1)
                for c in range(2):
                    mm = nc.tensor.transpose(bank[4 + u][0:EH, c * P:(c + 1) * P],
                                             xn[:, u, c * EH:(c + 1) * EH], ident[:, :])
                mm.then_inc(s["turned"], 1)

            def gate(t, u):
                pe.wait_ge(s["xt"], t + 1)
                wait(pe, s["gate_sb"], t - 1)
                for c in range(2):
                    mm = nc.tensor.matmul(bank[6 + u][:, 0:NE0], xt[:, u, c, :], gate_w[:, c, :],
                                          start=(c == 0), stop=(c == 1))
                mm.then_inc(s["gate_ps"], 1)

            return turn, gate

        def tail_on_act(act, s):
            def copy_x(t, u):
                act.wait_ge(s["turned"], t + 1)
                wait(act, s["gate_ps"], t - 1)
                wait(act, s["gathered"], t - 1)
                nc.scalar.activation(xt[:, u, :, :].rearrange("p c t -> p (c t)"), bank[4 + u][0:EH, 0:2 * P],
                                     ACT.Copy).then_inc(s["xt"], 1)

            def deviation(t, u):
                sdev_of(act, t, u, s["moments"], s["sdev"], s["inverse"])

            return copy_x, deviation

        def tail_on_pool(pool, s):
            def gather(t, u):
                pool.wait_ge(s["xt"], t + 1)
                nc.gpsimd.tensor_copy(xnT_v[:, :, ds(t * P, P)], xt[:, u, :, :]).then_inc(s["gathered"], 1)

            return gather

        def tail_on_dve(dve, s):
            def norm(t, u):
                wait(dve, s["turned"], t - 1)
                normalise(dve, t, u, s["sdev"], s["inverse"], s["xn"], xn[:, u, :])

            def keep_gate(t, u):
                dve.wait_ge(s["gate_ps"], t + 1)
                nc.vector.tensor_copy(logits[:, ds(t, 1), :].rearrange("p a e -> p (a e)"),
                                      bank[6 + u][:, 0:NE0]).then_inc(s["gate_sb"], 1)

            return norm, keep_gate

        tail2 = tail_sems("2")
        pv_ps, ot_sb, o_ps, h2 = (sem(n) for n in ("pv_ps", "ot_sb", "o_ps", "h2"))
        v_loaded = [sem(f"v_loaded{u}") for u in range(2)]
        vbd_done = [sem(f"vbd_done{g}") for g in range(2)]
        vrep = kT[0:EH, 0:2 * IPT * E].rearrange("p (u b e) -> p u b e", u=2, b=IPT)

        def spread_values(eng, t, u, g):
            eng.wait_ge(v_loaded[u], HG * in_slot(t, u))
            wait(eng, pv_ps, t - 1)
            shape = [EH, IPT, HG, D]
            eng.tensor_tensor(vbd[:, u, g, :, :].rearrange("p b (m d) -> p b m d", m=HG),
                              vrep[:, u, :, g * EH:(g + 1) * EH].rearrange("p b (m d) -> p b m d", m=HG),
                              hmask[:, :].unsqueeze(1).unsqueeze(3).broadcast_to(shape), ALU.mult)\
                .then_inc(vbd_done[g], 1)

        with nc.Block() as block:
            @block.sync
            def _(sp):
                src = v_scr.rearrange("(b j) e -> j b e", j=S)

                def load(t, u):
                    wait(sp, vbd_done[0], t - 1)
                    wait(sp, vbd_done[1], t - 1)
                    for m in range(HG):
                        sp.dma_start(vrep[m * S:(m + 1) * S, u, :, :], src[:, ds(t * IPT, IPT), :])\
                            .then_inc(v_loaded[u], 16)

                steps(sp, NT, [(load, 0)])

            @block.tensor
            def _(pe):
                def attend(t, u):
                    pe.wait_ge(vbd_done[0], t + 1)
                    pe.wait_ge(vbd_done[1], t + 1)
                    wait(pe, ot_sb, t - 1)
                    for g in range(2):
                        for b in range(IPT):
                            mm = nc.tensor.matmul(bank[u][0:EH, g * P + b * S:g * P + (b + 1) * S],
                                                  vbd[:, u, g, b, :], pT_v[:, g, ds(t * P + b * S, S)],
                                                  start=True, stop=True)
                    mm.then_inc(pv_ps, 1)

                def project(t, u):
                    pe.wait_ge(ot_sb, t + 1)
                    wait(pe, h2, 2 * t - 2)
                    for g in range(2):
                        mm = nc.tensor.matmul(bank[2 + u][:, 0:E], ot[:, u, g, :], wo[:, g, :],
                                              start=(g == 0), stop=(g == 1))
                    mm.then_inc(o_ps, 1)

                turn, gate = tail_on_pe(pe, tail2, gate0)
                steps(pe, NT, [(gate, 5), (turn, 4), (project, 2), (attend, 1)])

            @block.scalar
            def _(act):
                def keep_o(t, u):
                    act.wait_ge(pv_ps, t + 1)
                    wait(act, o_ps, t - 1)
                    nc.scalar.activation(ot[:, u, :, :].rearrange("p g t -> p (g t)"), bank[u][0:EH, 0:2 * P],
                                         ACT.Copy).then_inc(ot_sb, 1)

                copy_x, deviation = tail_on_act(act, tail2)
                steps(act, NT, [(copy_x, 4), (keep_o, 1), (deviation, 2)])

            @block.gpsimd
            def _(pool):
                gather = tail_on_pool(pool, tail2)
                steps(pool, NT, [(gather, 4), (lambda t, u: spread_values(nc.gpsimd, t, u, 1), 0)])

            @block.vector
            def _(dve):
                def residual(t, u):
                    tile = h[:, ds(t, 1), :].rearrange("p a e -> p (a e)")
                    dve.wait_ge(o_ps, t + 1)
                    nc.vector.tensor_tensor(tile, bank[2 + u][:, 0:E], tile, ALU.add).then_inc(h2, 1)
                    dve.wait_ge(h2, 2 * t + 1)
                    nc.vector.tensor_tensor(tile, tile, bo[:, :], ALU.add).then_inc(h2, 1)
                    moments_of(dve, t, u, tail2["moments"], h2, 2 * t + 2)

                norm, keep_gate = tail_on_dve(dve, tail2)
                steps(dve, NT, [(keep_gate, 5), (norm, 3), (lambda t, u: spread_values(nc.vector, t, u, 0), 0),
                                (residual, 2)])

        r0, sig_done = sem("r0"), sem("sig_done")

        def ranks(link, value, n, lower, rank, eligible=None):
            shape = [P, NT, n, n]
            gt = pairs[:, 0:NT * n * n].rearrange("p (t a b) -> p t a b", a=n, b=n)
            eq = ties[:, 0:NT * n * n].rearrange("p (t a b) -> p t a b", a=n, b=n)
            of_b, of_a = value.unsqueeze(2).broadcast_to(shape), value.unsqueeze(3).broadcast_to(shape)
            nc.vector.tensor_tensor(gt, of_b, of_a, ALU.is_gt)
            link(nc.vector.tensor_tensor(eq, of_b, of_a, ALU.is_equal))
            link(nc.vector.tensor_tensor(eq, eq, lower.rearrange("p (a b) -> p a b", a=n).unsqueeze(1)
                                         .broadcast_to(shape), ALU.mult))
            link(nc.vector.tensor_tensor(gt, gt, eq, ALU.add))
            if eligible is not None:
                link(nc.vector.tensor_tensor(gt, gt, eligible.unsqueeze(2).broadcast_to(shape), ALU.mult))
            link(nc.vector.tensor_reduce(rank, gt, AX.X, ALU.add))

        with nc.Block() as block:
            @block.scalar
            def _(act):
                nc.scalar.activation(logits[:, :, :], logits[:, :, :], ACT.Sigmoid).then_inc(sig_done, 1)

            @block.vector
            def _(dve):
                count = [0]

                def link(ins):
                    count[0] += 1
                    ins.then_inc(r0, 1)
                    dve.wait_ge(r0, count[0])

                s, chosen, rank = rt
                shape8 = [P, NT, NE0]
                dve.wait_ge(sig_done, 1)
                link(nc.vector.tensor_tensor(s[:, :, :], logits[:, :, :],
                                             gbias[:, :].unsqueeze(1).broadcast_to(shape8), ALU.add))
                two = s[:, :, :].rearrange("p t (g k) -> p t g k", k=2)
                group = rank[:, :, 0:GROUPS]
                link(nc.vector.tensor_tensor(group, two[:, :, :, 0], two[:, :, :, 1], ALU.add))
                grank = rank[:, :, GROUPS:2 * GROUPS]
                ranks(link, group, GROUPS, lower4[:, :], grank)
                link(nc.vector.tensor_scalar(grank, grank, 2.0, None, ALU.is_lt))
                link(nc.vector.tensor_copy(chosen[:, :, :].rearrange("p t (g k) -> p t g k", k=2),
                                           grank.unsqueeze(3).broadcast_to([P, NT, GROUPS, 2])))
                ranks(link, s[:, :, :], NE0, lower8[:, :], rank[:, :, :], chosen[:, :, :])
                link(nc.vector.scalar_tensor_tensor(s[:, :, :], rank[:, :, :], 2.0, chosen[:, :, :],
                                                    ALU.is_lt, ALU.mult))
                link(nc.vector.tensor_tensor(s[:, :, :], s[:, :, :], logits[:, :, :], ALU.mult))
                link(nc.vector.tensor_reduce(small[:, :, 0], s[:, :, :], AX.X, ALU.add))
                link(nc.vector.tensor_scalar(small[:, :, 0], small[:, :, 0], 1e-6, None, ALU.add))
                link(nc.vector.reciprocal(small[:, :, 1], small[:, :, 0]))
                link(nc.vector.tensor_tensor(comb[:, :, 0:NE0], s[:, :, :],
                                             small[:, :, 1:2].broadcast_to(shape8), ALU.mult))

        h13_ps, silu_done, hid_done, y_ps, y_done = (sem(n) for n in (
            "h13_ps", "silu_done", "hid_done", "y_ps", "y_done"))
        EXP = NE0 + 1

        with nc.Block() as block:
            @block.tensor
            def _(pe):
                def up(blk, e):
                    n = blk * EXP + e
                    wait(pe, hid_done, n - 2)
                    for w in range(2):
                        for c in range(2):
                            mm = nc.tensor.matmul(bank[2 * (e % 3) + w][:, :], w13[:, w, e, c, :],
                                                  xnT_v[:, c, ds(blk * BLK, BLK)], start=(c == 0), stop=(c == 1))
                    mm.then_inc(h13_ps, 1)

                def down(blk, e):
                    n = blk * EXP + e
                    pe.wait_ge(hid_done, n + 1)
                    for k in range(TPB):
                        wait(pe, y_done, 4 * n - 2 * (1 - k // 2))
                        mm = nc.tensor.matmul(bank[6 + k // 2][:, (k % 2) * E:(k % 2 + 1) * E],
                                              hidden0[:, e % 3, k * P:(k + 1) * P], w2[:, e, :],
                                              start=True, stop=True)
                        mm.then_inc(y_ps, 1)

                def one(blk):
                    up(blk, 0)
                    for e in range(EXP):
                        if e + 1 < EXP:
                            up(blk, e + 1)
                        down(blk, e)

                one(0)
                with pe.Fori(1, NB, 1) as blk:
                    one(blk)

            @block.scalar
            def _(act):
                def one(blk):
                    for e in range(EXP):
                        n = blk * EXP + e
                        act.wait_ge(h13_ps, n + 1)
                        wait(act, hid_done, n - 2)
                        nc.scalar.activation(silu0[:, e % 3, :], bank[2 * (e % 3)][:, :], ACT.Silu)\
                            .then_inc(silu_done, 1)

                one(0)
                with act.Fori(1, NB, 1) as blk:
                    one(blk)

            @block.vector
            def _(dve):
                def gate(blk, e):
                    n = blk * EXP + e
                    dve.wait_ge(silu_done, n + 1)
                    wait(dve, y_ps, 4 * n - 8)
                    nc.vector.tensor_tensor(hidden0[:, e % 3, :], silu0[:, e % 3, :], bank[2 * (e % 3) + 1][:, :],
                                            ALU.mult).then_inc(hid_done, 1)

                def add(blk, e):
                    n = blk * EXP + e
                    for k in range(TPB):
                        tile = h[:, ds(blk * TPB + k, 1), :].rearrange("p a e -> p (a e)")
                        dve.wait_ge(y_ps, 4 * n + 2 * (k // 2) + 2)
                        wait(dve, y_done, 4 * n + k - 3)
                        nc.vector.scalar_tensor_tensor(
                            tile, bank[6 + k // 2][:, (k % 2) * E:(k % 2 + 1) * E],
                            comb[:, ds(blk * TPB + k, 1), e:e + 1].rearrange("p a e -> p (a e)"), tile,
                            ALU.mult, ALU.add).then_inc(y_done, 1)

                def one(blk):
                    gate(blk, 0)
                    for e in range(EXP):
                        if e + 1 < EXP:
                            gate(blk, e + 1)
                        add(blk, e)

                one(0)
                with dve.Fori(1, NB, 1) as blk:
                    one(blk)

        wq1_loaded = sem("wq1_loaded")
        ln3, sdev3, inv3, xn3, am3, rng3, pr3, sc3 = (sem(n) for n in (
            "ln3", "sdev3", "inv3", "xn3", "am3", "rng3", "pr3", "sc3"))

        def absmax(dest, src):
            return nc.vector.tensor_reduce(dest, src, AX.XY if len(src.shape) == 3 else AX.X, ALU.max,
                                           apply_absolute_value=True)

        def scales(dve, pool_done, done, lo, hi, base=0):
            dve.wait_ge(pool_done, 1)
            nc.vector.tensor_scalar(qs[:, lo:hi], peaks[:, lo:hi], 1.0 / QMAX, 1e-8, ALU.mult, ALU.max)\
                .then_inc(done, 1)
            dve.wait_ge(done, base + 1)
            nc.vector.reciprocal(qi[:, lo:hi], qs[:, lo:hi]).then_inc(done, 1)
            dve.wait_ge(done, base + 2)

        X_, WQ_, WP_, Q_, K_, V_, P_, O_ = range(8)

        with nc.Block() as block:
            @block.sync
            def _(sp):
                sp.dma_start(wqkv32, a["L1_attn_w_qkv"]).then_inc(wq1_loaded, 16)
                sp.dma_start(wproj32, a["L1_attn_w_proj"]).then_inc(wq1_loaded, 16)

            @block.scalar
            def _(act):
                steps(act, NT, [(lambda t, u: sdev_of(act, t, u, ln3, sdev3, inv3), 0)])

            @block.vector
            def _(dve):
                def mean(t, u):
                    moments_of(dve, t, u, ln3, y_done, TPB * NB * EXP)

                def norm(t, u):
                    normalise(dve, t, u, sdev3, inv3, xn3,
                              xall[:, ds(t, 1), :].rearrange("p a e -> p (a e)"))

                steps(dve, NT, [(mean, 0), (norm, 1)])
                dve.wait_ge(xn3, NT)
                nc.vector.memset(peak[:, :], 0.0).then_inc(am3, 1)
                dve.wait_ge(am3, 1)
                absmax(peak[:, X_:X_ + 1], xall.rearrange("p n e -> p (n e)")).then_inc(am3, 1)
                dve.wait_ge(wq1_loaded, 32)
                absmax(peak[0:EH, WQ_:WQ_ + 1], wqkv32.rearrange("p c n -> p (c n)")).then_inc(am3, 1)
                absmax(peak[0:EH, WP_:WP_ + 1], wproj32.rearrange("p c n -> p (c n)")).then_inc(am3, 1)
                scales(dve, pr3, sc3, X_, WP_ + 1)
                nc.vector.tensor_scalar(prod[:, 0:1], qs[:, X_:X_ + 1], qs[:, WQ_:WQ_ + 1], None, ALU.mult)\
                    .then_inc(sc3, 1)
                nc.vector.tensor_scalar(wround, wqkv32, qi[0:EH, WQ_:WQ_ + 1], ROUND, ALU.mult, ALU.add)\
                    .then_inc(sc3, 1)
                nc.vector.tensor_scalar(wproj32, wproj32, qi[0:EH, WP_:WP_ + 1], ROUND, ALU.mult, ALU.add)\
                    .then_inc(sc3, 1)
                dve.wait_ge(sc3, 5)
                nc.vector.tensor_scalar(wqkv16, wround, ROUND, QMAX, ALU.subtract, ALU.min).then_inc(sc3, 1)
                nc.vector.tensor_scalar(wproj16, wproj32, ROUND, QMAX, ALU.subtract, ALU.min).then_inc(sc3, 1)

            @block.gpsimd
            def _(pool):
                pool.wait_ge(am3, 4)
                nc.gpsimd.partition_all_reduce(peaks[:, 0:3], peak[:, 0:3], P, RMAX).then_inc(pr3, 1)

        xr4, xi4, tr4, xt4, q_ps4, v_ps4, q_sb4, v_sb4, st4, pr4, am4, sc4 = (sem(n) for n in (
            "xr4", "xi4", "tr4", "xt4", "q_ps4", "v_ps4", "q_sb4", "v_sb4", "st4", "pr4", "am4", "sc4"))
        xt16 = xt[:, :, :, :].rearrange("p u c t -> p u (c t)").bitcast(BF16)

        with nc.Block() as block:
            @block.vector
            def _(dve):
                def quantise(t, u):
                    nc.vector.tensor_scalar(xn[:, u, :], xall[:, ds(t, 1), :].rearrange("p a e -> p (a e)"),
                                            qi[:, X_:X_ + 1], ROUND, ALU.mult, ALU.add).then_inc(xr4, 1)
                    dve.wait_ge(xr4, t + 1)
                    wait(dve, tr4, t - 1)
                    nc.vector.tensor_scalar(x16[:, u, 0:E], xn[:, u, :], ROUND, QMAX, ALU.subtract, ALU.min)\
                        .then_inc(xi4, 1)

                def values(t, u):
                    tile = vall[:, ds(t, 1), :].rearrange("p a e -> p (a e)")
                    dve.wait_ge(v_ps4, t + 1)
                    nc.vector.scalar_tensor_tensor(tile, bank[4 + u][:, 0:E], prod[:, 0:1], bv1[:, :],
                                                   ALU.mult, ALU.add).then_inc(v_sb4, 1)
                    dve.wait_ge(v_sb4, t + 1)
                    absmax(stats[:, V_, ds(t, 1)], tile).then_inc(st4, 1)
                    dve.wait_ge(q_sb4, 4 * t + 4)
                    absmax(stats[0:EH, Q_, ds(t, 1)], qT_v[:, :, ds(t * P, P)]).then_inc(st4, 1)
                    absmax(stats[0:EH, K_, ds(t, 1)], kT_v[:, :, ds(t * P, P)]).then_inc(st4, 1)

                steps(dve, NT, [(quantise, 0), (values, 2)])
                dve.wait_ge(st4, 3 * NT)
                nc.vector.tensor_reduce(peak[:, Q_:V_ + 1], stats[:, Q_:V_ + 1, :], AX.X, ALU.max).then_inc(am4, 1)
                scales(dve, pr4, sc4, Q_, V_ + 1)
                nc.vector.tensor_scalar(prod[:, 1:2], qs[:, Q_:Q_ + 1], qs[:, K_:K_ + 1], SOFT1, ALU.mult, ALU.mult)\
                    .then_inc(sc4, 1)

            @block.gpsimd
            def _(pool):
                pool.wait_ge(am4, 1)
                nc.gpsimd.partition_all_reduce(peaks[:, Q_:V_ + 1], peak[:, Q_:V_ + 1], P, RMAX).then_inc(pr4, 1)

            @block.tensor
            def _(pe):
                def turn(t, u):
                    pe.wait_ge(xi4, t + 1)
                    wait(pe, xt4, t - 1)
                    for c in range(2):
                        mm = nc.tensor.transpose(bank[u][0:EH, c * P // 2:(c + 1) * P // 2].bitcast(BF16),
                                                 x16[:, u, c * EH:(c + 1) * EH], ident16[:, :])
                    mm.then_inc(tr4, 1)

                def project(t, u):
                    pe.wait_ge(xt4, t + 1)
                    wait(pe, q_sb4, 4 * t - 4)
                    for n in range(4):
                        for c in range(2):
                            mm = nc.tensor.matmul(bank[2 + u][0:EH, n * P:(n + 1) * P],
                                                  wqkv16[:, c, n * EH:(n + 1) * EH], xt16[:, u, c * P:(c + 1) * P],
                                                  start=(c == 0), stop=(c == 1))
                    mm.then_inc(q_ps4, 1)
                    wait(pe, v_sb4, t - 1)
                    for c in range(2):
                        mm = nc.tensor.matmul(bank[4 + u][:, 0:E], xt16[:, u, c * P:(c + 1) * P],
                                              wqkv16[:, c, 2 * E:3 * E], start=(c == 0), stop=(c == 1))
                    mm.then_inc(v_ps4, 1)

                steps(pe, NT, [(turn, 0), (project, 1)])

            @block.scalar
            def _(act):
                def copy_x(t, u):
                    act.wait_ge(tr4, t + 1)
                    wait(act, v_ps4, t - 1)
                    nc.scalar.activation(xt16[:, u, 0:2 * P], bank[u][0:EH, 0:P].bitcast(BF16), ACT.Copy)\
                        .then_inc(xt4, 1)

                def copy_qk(t, u):
                    act.wait_ge(q_ps4, t + 1)
                    for n in range(4):
                        dest = (qT_v, kT_v)[n // 2]
                        nc.scalar.activation(dest[:, n % 2, ds(t * P, P)], bank[2 + u][0:EH, n * P:(n + 1) * P],
                                             ACT.Identity, bias=bqk1[:, n // 2, n % 2:n % 2 + 1],
                                             scale=prod[0:EH, 0:1]).then_inc(q_sb4, 1)

                steps(act, NT, [(copy_x, 0), (copy_qk, 1)])

        qr5, q5, k5, v5, kbd5, s_ps5, s_sb5, sc_ps5, sm5, exp5, p5, st5, am5, pr5, sc5 = (sem(n) for n in (
            "qr5", "q5", "k5", "v5", "kbd5", "s_ps5", "s_sb5", "sc_ps5", "sm5", "exp5", "p5", "st5", "am5", "pr5",
            "sc5"))
        vr5 = sem("vr5")
        v_stored16 = [sem(f"v_stored16_{u}") for u in range(2)]
        pall = t2
        st5buf = xt
        qround = ot
        kround = st1

        with nc.Block() as block:
            @block.gpsimd
            def _(pool):
                def store(t, u):
                    pool.wait_ge(v5, t + 1)
                    pool.dma_start(v_scr16[ds(t * P, P), :], v16[:, u, :]).then_inc(v_stored16[u], 16)

                steps(pool, NT, [(store, 0)])
                for u in range(2):
                    pool.wait_ge(v_stored16[u], 8 * NT)
                pool.wait_ge(am5, 1)
                nc.gpsimd.partition_all_reduce(peaks[:, P_:P_ + 1], peak[:, P_:P_ + 1], P, RMAX).then_inc(pr5, 1)

            @block.vector
            def _(dve):
                def by_head(buf):
                    return buf.rearrange("p (m j) -> p m j", j=S)

                def spread(buf):
                    return buf.unsqueeze(2).broadcast_to([P, H, S])

                def keys(t, u):
                    wait(dve, s_ps5, t - 1)
                    nc.vector.tensor_scalar(kround[:, u, :, :], kT_v[:, :, ds(t * P, P)], qi[0:EH, K_:K_ + 1], ROUND,
                                            ALU.mult, ALU.add).then_inc(k5, 1)
                    dve.wait_ge(k5, 2 * t + 1)
                    nc.vector.tensor_scalar(k16[:, u, :, :], kround[:, u, :, :], ROUND, QMAX, ALU.subtract,
                                            ALU.min).then_inc(k5, 1)
                    dve.wait_ge(k5, 2 * t + 2)
                    for g in range(2):
                        nc.vector.tensor_tensor(
                            kbd16[:, u, g * IPT * EH:(g + 1) * IPT * EH]
                            .rearrange("p (b m j) -> p b m j", b=IPT, m=HG),
                            k16[:, u, g, :].rearrange("p (b j) -> p b j", b=IPT).unsqueeze(2)
                            .broadcast_to([EH, IPT, HG, S]),
                            hmask16[:, :].unsqueeze(1).unsqueeze(3).broadcast_to([EH, IPT, HG, S]),
                            ALU.mult).then_inc(kbd5, 1)

                def shift(t, u):
                    dve.wait_ge(sc_ps5, t + 1)
                    nc.vector.tensor_reduce(top[:, u, 0:H], by_head(bank[4 + u][:, 0:E]), AX.X, ALU.max)\
                        .then_inc(sm5, 1)
                    dve.wait_ge(sm5, 4 * t + 1)
                    nc.vector.tensor_tensor(by_head(scores[:, u, 0:E]), by_head(bank[4 + u][:, 0:E]),
                                            spread(top[:, u, 0:H]), ALU.subtract).then_inc(sm5, 1)

                def share(t, u):
                    tile = pall[:, ds(t, 1), :].rearrange("p a e -> p (a e)")
                    dve.wait_ge(exp5, t + 1)
                    nc.vector.tensor_reduce(mass[:, u, 0:H], by_head(scores[:, u, 0:E]), AX.X, ALU.add)\
                        .then_inc(sm5, 1)
                    dve.wait_ge(sm5, 4 * t + 3)
                    nc.vector.reciprocal(top[:, u, H:2 * H], mass[:, u, 0:H]).then_inc(sm5, 1)
                    dve.wait_ge(sm5, 4 * t + 4)
                    nc.vector.tensor_tensor(by_head(tile), by_head(scores[:, u, 0:E]), spread(top[:, u, H:2 * H]),
                                            ALU.mult).then_inc(p5, 1)

                def values(t, u):
                    nc.vector.tensor_scalar(xn[:, u, :], vall[:, ds(t, 1), :].rearrange("p a e -> p (a e)"),
                                            qi[:, V_:V_ + 1], ROUND, ALU.mult, ALU.add).then_inc(vr5, 1)
                    dve.wait_ge(vr5, t + 1)
                    wait(dve, v_stored16[u], in_slot(t, u) - 16)
                    nc.vector.tensor_scalar(v16[:, u, :], xn[:, u, :], ROUND, QMAX, ALU.subtract, ALU.min)\
                        .then_inc(v5, 1)

                steps(dve, NT, [(share, 3), (shift, 2), (keys, 0), (values, 0)])
                dve.wait_ge(p5, NT)
                nc.vector.tensor_reduce(peak[:, P_:P_ + 1], pall.rearrange("p n e -> p (n e)"), AX.X, ALU.max)\
                    .then_inc(am5, 1)
                scales(dve, pr5, sc5, P_, P_ + 1)
                nc.vector.tensor_scalar(prod[:, 2:3], qs[:, P_:P_ + 1], qs[:, V_:V_ + 1], None, ALU.mult)\
                    .then_inc(sc5, 1)

            @block.tensor
            def _(pe):
                def score(t, u):
                    pe.wait_ge(q5, t + 1)
                    pe.wait_ge(kbd5, 2 * t + 2)
                    wait(pe, s_sb5, t - 1)
                    for g in range(2):
                        for b in range(IPT):
                            at = g * IPT * EH + b * EH
                            mm = nc.tensor.matmul(bank[u][0:EH, g * P + b * S:g * P + (b + 1) * S],
                                                  kbd16[:, u, at:at + EH], q16[:, u, g, b * S:(b + 1) * S],
                                                  start=True, stop=True)
                    mm.then_inc(s_ps5, 1)

                def turn(t, u):
                    pe.wait_ge(s_sb5, t + 1)
                    wait(pe, sm5, 4 * t - 6)
                    for g in range(2):
                        mm = nc.tensor.transpose(bank[4 + u][:, g * EH:(g + 1) * EH], st5buf[:, u, g, :],
                                                 ident[0:EH, 0:EH])
                    mm.then_inc(sc_ps5, 1)

                steps(pe, NT, [(score, 0), (turn, 1)])

            @block.scalar
            def _(act):
                def keep_s(t, u):
                    act.wait_ge(s_ps5, t + 1)
                    wait(act, sc_ps5, t - 1)
                    nc.scalar.activation(st5buf[:, u, :, :].rearrange("p g t -> p (g t)"), bank[u][0:EH, 0:2 * P],
                                         ACT.Copy).then_inc(s_sb5, 1)

                def exponent(t, u):
                    act.wait_ge(sm5, 4 * t + 2)
                    nc.scalar.activation(scores[:, u, 0:E], scores[:, u, 0:E], ACT.Exp, scale=prod[:, 1:2])\
                        .then_inc(exp5, 1)

                def queries(t, u):
                    nc.scalar.activation(qround[:, u, :, :], qT_v[:, :, ds(t * P, P)], ACT.Identity,
                                         bias=rounding[0:EH, 0:1], scale=qi[0:EH, Q_:Q_ + 1]).then_inc(qr5, 1)
                    act.wait_ge(qr5, t + 1)
                    wait(act, s_ps5, t - 1)
                    nc.scalar.activation(q16[:, u, :, :], qround[:, u, :, :], ACT.Identity,
                                         bias=rounding[0:EH, 1:2]).then_inc(q5, 1)

                steps(act, NT, [(queries, 0), (exponent, 2), (keep_s, 0)])


        pr6, pi6, tr6, pt6, o_ps6, o_sb6, st6, am6, par6, sc6 = (sem(n) for n in (
            "pr6", "pi6", "tr6", "pt6", "o_ps6", "o_sb6", "st6", "am6", "par6", "sc6"))
        v16_loaded = [sem(f"v16_loaded{u}") for u in range(2)]
        vbd16_done = sem("vbd16_done")
        vrep16 = kT[0:EH, 0:IPT * E].bitcast(BF16).rearrange("p (u b e) -> p u b e", u=2, b=IPT)
        CELLS = IPT * EH

        with nc.Block() as block:
            @block.sync
            def _(sp):
                src = v_scr16.rearrange("(b j) e -> j b e", j=S)

                def load(t, u):
                    wait(sp, vbd16_done, 2 * t - 2)
                    for m in range(HG):
                        sp.dma_start(vrep16[m * S:(m + 1) * S, u, :, :], src[:, ds(t * IPT, IPT), :])\
                            .then_inc(v16_loaded[u], 16)

                steps(sp, NT, [(load, 0)])

            @block.vector
            def _(dve):
                def quantise(t, u):
                    nc.vector.tensor_scalar(xn[:, u, :], pall[:, ds(t, 1), :].rearrange("p a e -> p (a e)"),
                                            qi[:, P_:P_ + 1], ROUND, ALU.mult, ALU.add).then_inc(pr6, 1)
                    dve.wait_ge(pr6, t + 1)
                    wait(dve, tr6, t - 1)
                    nc.vector.tensor_scalar(x16[:, u, 0:E], xn[:, u, :], ROUND, QMAX, ALU.subtract, ALU.min)\
                        .then_inc(pi6, 1)

                def spread_values(t, u):
                    dve.wait_ge(v16_loaded[u], HG * in_slot(t, u))
                    wait(dve, o_ps6, t - 1)
                    shape = [EH, IPT, HG, D]
                    for g in range(2):
                        nc.vector.tensor_tensor(
                            vbd16[:, u, g * CELLS:(g + 1) * CELLS].rearrange("p (b m d) -> p b m d", b=IPT, m=HG),
                            vrep16[:, u, :, g * EH:(g + 1) * EH].rearrange("p b (m d) -> p b m d", m=HG),
                            hmask16[:, :].unsqueeze(1).unsqueeze(3).broadcast_to(shape), ALU.mult)\
                            .then_inc(vbd16_done, 1)

                def range_of(t, u):
                    dve.wait_ge(o_sb6, t + 1)
                    absmax(stats[0:EH, O_, ds(t, 1)], qT_v[:, :, ds(t * P, P)]).then_inc(st6, 1)

                steps(dve, NT, [(range_of, 2), (quantise, 0), (spread_values, 0)])
                dve.wait_ge(st6, NT)
                nc.vector.tensor_reduce(peak[:, O_:O_ + 1], stats[:, O_, :], AX.X, ALU.max).then_inc(am6, 1)
                scales(dve, par6, sc6, O_, O_ + 1)
                nc.vector.tensor_scalar(prod[:, 3:4], qs[:, O_:O_ + 1], qs[:, WP_:WP_ + 1], None, ALU.mult)\
                    .then_inc(sc6, 1)

            @block.gpsimd
            def _(pool):
                pool.wait_ge(am6, 1)
                nc.gpsimd.partition_all_reduce(peaks[:, O_:O_ + 1], peak[:, O_:O_ + 1], P, RMAX).then_inc(par6, 1)

            @block.tensor
            def _(pe):
                def turn(t, u):
                    pe.wait_ge(pi6, t + 1)
                    wait(pe, pt6, t - 1)
                    for c in range(2):
                        mm = nc.tensor.transpose(bank[u][0:EH, c * P // 2:(c + 1) * P // 2].bitcast(BF16),
                                                 x16[:, u, c * EH:(c + 1) * EH], ident16[:, :])
                    mm.then_inc(tr6, 1)

                def attend(t, u):
                    pe.wait_ge(vbd16_done, 2 * t + 2)
                    pe.wait_ge(pt6, t + 1)
                    wait(pe, o_sb6, t - 1)
                    for g in range(2):
                        for b in range(IPT):
                            at = g * CELLS + b * EH
                            mm = nc.tensor.matmul(bank[2 + u][0:EH, g * P + b * S:g * P + (b + 1) * S],
                                                  vbd16[:, u, at:at + EH],
                                                  xt16[:, u, g * P + b * S:g * P + (b + 1) * S],
                                                  start=True, stop=True)
                    mm.then_inc(o_ps6, 1)

                steps(pe, NT, [(attend, 1), (turn, 0)])

            @block.scalar
            def _(act):
                def keep_p(t, u):
                    act.wait_ge(tr6, t + 1)
                    wait(act, o_ps6, t - 1)
                    nc.scalar.activation(xt16[:, u, 0:2 * P], bank[u][0:EH, 0:P].bitcast(BF16), ACT.Copy)\
                        .then_inc(pt6, 1)

                def keep_o(t, u):
                    act.wait_ge(o_ps6, t + 1)
                    nc.scalar.activation(qT_v[:, :, ds(t * P, P)],
                                         bank[2 + u][0:EH, 0:2 * P].rearrange("p (g t) -> p g t", g=2),
                                         ACT.Copy, scale=prod[0:EH, 2:3]).then_inc(o_sb6, 1)

                steps(act, NT, [(keep_o, 1), (keep_p, 0)])

        or7, oi7, w_ps7, h7 = (sem(n) for n in ("or7", "oi7", "w_ps7", "h7"))
        tail7 = tail_sems("7")

        with nc.Block() as block:
            @block.vector
            def _(dve):
                def quantise(t, u):
                    nc.vector.tensor_scalar(ot[:, u, :, :], qT_v[:, :, ds(t * P, P)], qi[0:EH, O_:O_ + 1], ROUND,
                                            ALU.mult, ALU.add).then_inc(or7, 1)
                    dve.wait_ge(or7, t + 1)
                    wait(dve, w_ps7, t - 1)
                    nc.vector.tensor_scalar(x16[0:EH, u, 0:2 * P], ot[:, u, :, :].rearrange("p g t -> p (g t)"),
                                            ROUND, QMAX, ALU.subtract, ALU.min).then_inc(oi7, 1)

                def residual(t, u):
                    tile = h[:, ds(t, 1), :].rearrange("p a e -> p (a e)")
                    dve.wait_ge(w_ps7, t + 1)
                    nc.vector.scalar_tensor_tensor(tile, bank[2 + u][:, 0:E], prod[:, 3:4], tile, ALU.mult, ALU.add)\
                        .then_inc(h7, 1)
                    dve.wait_ge(h7, 2 * t + 1)
                    nc.vector.tensor_tensor(tile, tile, bproj[:, :], ALU.add).then_inc(h7, 1)
                    moments_of(dve, t, u, tail7["moments"], h7, 2 * t + 2)

                norm, keep_gate = tail_on_dve(dve, tail7)
                steps(dve, NT, [(keep_gate, 4), (norm, 2), (quantise, 0), (residual, 1)])

            @block.tensor
            def _(pe):
                def project(t, u):
                    pe.wait_ge(oi7, t + 1)
                    wait(pe, h7, 2 * t - 2)
                    for g in range(2):
                        mm = nc.tensor.matmul(bank[2 + u][:, 0:E], x16[0:EH, u, g * P:(g + 1) * P], wproj16[:, g, :],
                                              start=(g == 0), stop=(g == 1))
                    mm.then_inc(w_ps7, 1)

                turn, gate = tail_on_pe(pe, tail7, gate1)
                steps(pe, NT, [(gate, 4), (turn, 3), (project, 1)])

            @block.scalar
            def _(act):
                copy_x, deviation = tail_on_act(act, tail7)
                steps(act, NT, [(copy_x, 3), (deviation, 1)])

            @block.gpsimd
            def _(pool):
                gather = tail_on_pool(pool, tail7)
                steps(pool, NT, [(gather, 0)])

        cc8 = sem("cc8")
        r8, exp8, comb8, ct_ps8, ct_sb8, b_ps8, b_sb8 = (sem(n) for n in (
            "r8", "exp8", "comb8", "ct_ps8", "ct_sb8", "b_ps8", "b_sb8"))

        with nc.Block() as block:
            @block.vector
            def _(dve):
                count = [0]

                def link(ins):
                    count[0] += 1
                    ins.then_inc(r8, 1)
                    dve.wait_ge(r8, count[0])

                e, chosen, rank = rt
                shape8 = [P, NT, NE1]
                link(nc.vector.tensor_reduce(small[:, :, 0], logits[:, :, :], AX.X, ALU.max))
                link(nc.vector.tensor_tensor(e[:, :, :], logits[:, :, :], small[:, :, 0:1].broadcast_to(shape8),
                                             ALU.subtract))
                ranks(link, logits[:, :, :], NE1, lower8[:, :], rank[:, :, :])
                dve.wait_ge(exp8, 1)
                link(nc.vector.scalar_tensor_tensor(e[:, :, :], rank[:, :, :], 2.0, e[:, :, :],
                                                    ALU.is_lt, ALU.mult))
                link(nc.vector.tensor_reduce(small[:, :, 0], e[:, :, :], AX.X, ALU.add))
                link(nc.vector.reciprocal(small[:, :, 1], small[:, :, 0]))
                nc.vector.tensor_tensor(comb[:, :, 0:NE1], e[:, :, :], small[:, :, 1:2].broadcast_to(shape8),
                                        ALU.mult).then_inc(comb8, 1)

                def add(t, u):
                    tile = h[:, ds(t, 1), :].rearrange("p a e -> p (a e)")
                    dve.wait_ge(b_ps8, t + 1)
                    nc.vector.tensor_tensor(tile, bank[2 + u][:, 0:E], tile, ALU.add).then_inc(b_sb8, 1)

                steps(dve, NT, [(add, 0)])

            @block.scalar
            def _(act):
                act.wait_ge(r8, 2)
                nc.scalar.activation(rt[0][:, :, :], rt[0][:, :, :], ACT.Exp).then_inc(exp8, 1)

                def keep(t, u):
                    act.wait_ge(ct_ps8, t + 1)
                    wait(act, b_ps8, t - 1)
                    nc.scalar.activation(combT[:, u, :], bank[u][0:NE1, 0:P], ACT.Copy).then_inc(ct_sb8, 1)

                steps(act, NT, [(keep, 0)])

            @block.tensor
            def _(pe):
                def turn(t, u):
                    pe.wait_ge(cc8, t + 1)
                    wait(pe, ct_sb8, t - 1)
                    nc.tensor.matmul(bank[u][0:NE1, 0:P], combc[:, u, :], ident[:, :], start=True, stop=True)\
                        .then_inc(ct_ps8, 1)

                def bias(t, u):
                    pe.wait_ge(ct_sb8, t + 1)
                    wait(pe, b_sb8, t - 1)
                    nc.tensor.matmul(bank[2 + u][:, 0:E], combT[:, u, :], b2r[:, :], start=True, stop=True)\
                        .then_inc(b_ps8, 1)

                steps(pe, NT, [(turn, 0), (bias, 1)])

            @block.gpsimd
            def _(pool):
                pool.wait_ge(comb8, 1)

                def fetch(t, u):
                    wait(pool, ct_ps8, t - 1)
                    nc.gpsimd.tensor_copy(combc[:, u, :], comb[:, ds(t, 1), 0:NE1].rearrange("p a e -> p (a e)"))\
                        .then_inc(cc8, 1)

                steps(pool, NT, [(fetch, 0)])

        w_loaded = [sem(f"w_loaded{u}") for u in range(2)]
        up9, ra9, rd9, y9, add9, stored = (sem(n) for n in ("up9", "ra9", "rd9", "y9", "add9", "stored"))

        def experts(eng, begin, one):
            begin(0, 0)
            one(0, 0, 0)
            with eng.Fori(1, NB, 1) as blk:
                one(0, 0, blk)
            begin(1, 1)
            with eng.Fori(0, NB, 1) as blk:
                one(1, 1, blk)
            with eng.Fori(2, NE1 - 1, 2) as e0:
                for u in range(2):
                    begin(e0 + u, u)
                    with eng.Fori(0, NB, 1) as blk:
                        one(e0 + u, u, blk)

        with nc.Block() as block:
            @block.sync
            def _(sp):
                def load(e, u):
                    wait(sp, y9, 4 * NB * (e - 1))
                    sp.dma_start(w1s[:, u, :, :].rearrange("p c f -> p (c f)"),
                                 a["L1_ffn_W1"][ds(e, 1), :, :].rearrange("a p k -> p (a k)"))\
                        .then_inc(w_loaded[u], 16)
                    sp.dma_start(w2s[:, u, :, :].rearrange("p c e -> p (c e)"),
                                 a["L1_ffn_W2"][ds(e, 1), :, :].rearrange("a p k -> p (a k)"))\
                        .then_inc(w_loaded[u], 16)

                for e in range(2):
                    load(e, e)
                with sp.Fori(2, NE1 - 1, 2) as e0:
                    for u in range(2):
                        load(e0 + u, u)
                out_v = out.rearrange("(n p) e -> p n e", p=P)
                for b in range(NB):
                    sp.wait_ge(add9, 4 * ((NE1 - 1) * NB + b + 1))
                    sp.dma_start(out_v[:, b * TPB:(b + 1) * TPB, :], h[:, b * TPB:(b + 1) * TPB, :])\
                        .then_inc(stored, 16)
                sp.wait_ge(stored, 16 * NB)

            @block.tensor
            def _(pe):
                def begin(e, u):
                    wait_alone(pe, w_loaded[u], 2 * in_slot(e, u), passed)

                def one(e, u, blk):
                    n = e * NB + blk
                    for c in range(FC):
                        wait(pe, (ra9, rd9)[c % 2], 3 * n + c // 2 - 2)
                        for k in range(2):
                            mm = nc.tensor.matmul(bank[c][:, :], w1s[:, u, k, c * P:(c + 1) * P],
                                                  xnT_v[:, k, ds(blk * BLK, BLK)], start=(k == 0), stop=(k == 1))
                        mm.then_inc(up9, 1)
                    for k in range(TPB):
                        wait(pe, add9, 4 * n - 2 * (1 - k // 2))
                        for c in range(FC):
                            if k == 0:
                                pe.wait_ge((ra9, rd9)[c % 2], 3 * n + c // 2 + 1)
                            mm = nc.tensor.matmul(bank[6 + k // 2][:, (k % 2) * E:(k % 2 + 1) * E],
                                                  hidden1[:, c, k * P:(k + 1) * P], w2s[:, u, c, :],
                                                  start=(c == 0), stop=(c == FC - 1))
                        mm.then_inc(y9, 1)

                experts(pe, begin, one)

            @block.scalar
            def _(act):
                def one(e, u, blk):
                    n = e * NB + blk
                    wait(act, y9, 4 * n)
                    for c in range(0, FC, 2):
                        act.wait_ge(up9, FC * n + c + 1)
                        nc.scalar.activation(hidden1[:, c, :], bank[c][:, :], ACT.Relu,
                                             bias=b1c[:, ds(e * FC + c, 1)]).then_inc(ra9, 1)

                experts(act, lambda e, u: None, one)

            @block.vector
            def _(dve):
                def one(e, u, blk):
                    n = e * NB + blk
                    wait(dve, y9, 4 * n)
                    for c in range(1, FC, 2):
                        dve.wait_ge(up9, FC * n + c + 1)
                        nc.vector.tensor_scalar(hidden1[:, c, :], bank[c][:, :], b1c[:, ds(e * FC + c, 1)], 0.0,
                                                ALU.add, ALU.max).then_inc(rd9, 1)
                    for k in range(TPB):
                        tile = h[:, ds(blk * TPB + k, 1), :].rearrange("p a e -> p (a e)")
                        dve.wait_ge(y9, 4 * n + 2 * (k // 2) + 2)
                        nc.vector.scalar_tensor_tensor(
                            tile, bank[6 + k // 2][:, (k % 2) * E:(k % 2 + 1) * E],
                            comb[:, ds(blk * TPB + k, 1), ds(e, 1)].rearrange("p a e -> p (a e)"), tile,
                            ALU.mult, ALU.add).then_inc(add9, 1)

                experts(dve, lambda e, u: None, one)


def kernel(**inputs):
    import numpy as np
    import concourse.bacc as bacc
    from concourse import mybir as mb
    from concourse.bass_utils import run_bass_kernel_spmd

    i = {k: np.asarray(v) for k, v in inputs.items()}

    def rows(w):
        return w.reshape(2, EH, -1).transpose(1, 0, 2)

    def column(b):
        return b.reshape(-1, EH).T

    x = i["x"].reshape(IMAGES, CHANS, 4, PATCH, 4, PATCH).transpose(1, 3, 5, 0, 2, 4)
    x = x.reshape(KC, P, NT, P).transpose(2, 1, 0, 3).reshape(NT, P, KC * P)
    near = i["L0_attn_rel_table"][P - 1 - (S - 1):P - 1 + S]
    up = np.stack([np.concatenate([i["L0_ffn_" + w], i["L0_ffn_s" + w][None]]) for w in ("w1", "w3")])
    down = np.concatenate([i["L0_ffn_w2"], i["L0_ffn_sw2"][None]])
    p = np.arange(P)
    arrays = {
        "x": x,
        "L0_tok_pinv": i["L0_tok_pinv"].T.reshape(OC, P, PATCH * PATCH).transpose(1, 0, 2),
        "L0_tok_proj_weight": i["L0_tok_proj_weight"].reshape(E, CHANS, OC, P).transpose(3, 2, 1, 0)
        .reshape(P, OC, CHANS * E),
        "rel": rows(near.T), "rel_reversed": rows(near[::-1].T),
        "L0_attn_columns": np.stack([column(i["L0_attn_b" + n]) for n in ("q", "k", "pk", "pq")], 1),
        "L1_attn_columns": np.stack([column(i["L1_attn_b_qkv"][n * E:(n + 1) * E]) for n in range(2)], 1),
        "L1_attn_b_v": i["L1_attn_b_qkv"][2 * E:],
        "L0_ffn_gate_weight": rows(i["L0_ffn_gate_weight"].T), "L1_ffn_Wr": rows(i["L1_ffn_Wr"]),
        "L0_ffn_w13": up.reshape(2, NE0 + 1, INTER, 2, EH).transpose(4, 0, 1, 3, 2),
        "L0_ffn_w2": down.transpose(2, 0, 1),
        "L1_attn_w_qkv": rows(i["L1_attn_w_qkv"]), "L1_attn_w_proj": rows(i["L1_attn_w_proj"]),
        "L1_ffn_W1": i["L1_ffn_W1"].reshape(NE1, 2, EH, FF).transpose(0, 2, 1, 3).reshape(NE1, EH, 2 * FF),
        "L1_ffn_W2": i["L1_ffn_W2"].reshape(NE1, FC, P, E).transpose(0, 2, 1, 3).reshape(NE1, P, FC * E),
        "L1_ffn_b1": i["L1_ffn_b1"].reshape(NE1 * FC, P).T, "L1_ffn_b2": i["L1_ffn_b2"],
        "ident": np.eye(P, dtype=np.float32),
        "hmask": np.equal(np.arange(EH)[:, None] // D, np.arange(HG)[None]).astype(np.float32),
        "lower4": np.broadcast_to(np.tril(np.ones((GROUPS, GROUPS), np.float32), -1).reshape(1, -1), (P, GROUPS ** 2)),
        "lower8": np.broadcast_to(np.tril(np.ones((NE0, NE0), np.float32), -1).reshape(1, -1), (P, NE0 ** 2)),
    }
    for n in ("Wq", "Wk", "Wv", "Wo", "Wpk", "Wpq"):
        arrays["L0_attn_" + n] = rows(i["L0_attn_" + n])
    for n in ("L0_tok_proj_bias", "L0_attn_bv", "L0_attn_bo", "L1_attn_b_proj", "L0_ffn_gate_bias"):
        arrays[n] = i[n]
    arrays = {k: np.ascontiguousarray(v) for k, v in arrays.items()}

    nc = bacc.Bacc("TRN2", target_bir_lowering=False, num_devices=1)
    aps = {k: nc.dram_tensor("in_" + k, v.shape, mb.dt.from_np(v.dtype), kind="ExternalInput").ap()
           for k, v in arrays.items()}
    out = nc.dram_tensor("out", (T, E), mb.dt.float32, kind="ExternalOutput").ap()
    tower(nc, aps, out)
    r = run_bass_kernel_spmd(nc, [{"in_" + k: v for k, v in arrays.items()}], core_ids=[0])
    return r.results[0]["out"].reshape(IMAGES, S, E)
```

```python
from contextlib import ExitStack

import concourse.bass as bass
from concourse import mybir

F32 = mybir.dt.float32
BF16 = mybir.dt.bfloat16
ALU = mybir.AluOpType
ACT = mybir.ActivationFunctionType
AX = mybir.AxisListType
RMAX = bass.bass_isa.ReduceOp.max

P = 128
IMAGES, CHANS, SIDE, PATCH, OLD = 128, 3, 64, 16, 32
S = (SIDE // PATCH) ** 2
T = IMAGES * S
NT = T // P
IPT = P // S
BLK = 512
NB = T // BLK
TPB = BLK // P
E = 192
EH = E // 2
H, D = 12, 16
HG = H // 2
KC = CHANS * PATCH * PATCH // P
OC = OLD * OLD // P
REL = 2 * S - 1
NE0, INTER = 8, 128
GROUPS = 4
NE1, FF = 8, 768
FC = FF // P
SLOT_TILES = (2 * T + NE1 * (P - 1)) // P
SLOT_TILES += SLOT_TILES % 2
EPS = 1e-5
SOFT0 = 1.0 / (3.0 * D) ** 0.5
SOFT1 = D ** -0.5
QMAX = 127.0
ROUND = 1.5 * 2.0 ** 23


def ds(start, size):
    return bass.ds(start, size)


def wait(eng, semaphore, count):
    if isinstance(count, int) and count <= 0:
        return
    eng.wait_ge(semaphore, count)


def wait_alone(eng, semaphore, count, passed):
    wait(eng, semaphore, count)
    if not isinstance(count, int):
        eng.sem_inc(passed, 1)


def in_slot(t, u):
    return 8 * (t - u) + 16


def steps(eng, n, stages):
    deepest = max(lag for _, lag in stages)
    head = deepest + 2 + deepest % 2

    def fixed(s):
        for stage, lag in stages:
            if 0 <= s - lag < n:
                stage(s - lag, (s - lag) % 2)

    for s in range(head):
        fixed(s)
    with eng.Fori(head, n - 1, 2) as s0:
        for v in range(2):
            for stage, lag in stages:
                stage(s0 + (v - lag), (v - lag) % 2)
    for s in range(n, n + deepest):
        fixed(s)


def tower(nc, a, out):
    ctx = ExitStack()
    with ctx:
        def sb(name, shape, dt=F32):
            return ctx.enter_context(nc.sbuf_tensor(name, shape, dt))

        early = ctx.enter_context(ExitStack())
        early_sems = []

        def sem(name):
            return ctx.enter_context(nc.semaphore(name))

        def early_sem(name):
            early_sems.append(early.enter_context(nc.semaphore(name)))
            return early_sems[-1]

        h = sb("h", [P, NT, E])
        xnT = sb("xnT", [P, 2 * T])
        qks = sb("qks", [P, 3 * 2 * T])
        qT, kT, sT = (qks[:, n * 2 * T:(n + 1) * 2 * T] for n in range(3))
        big = sb("big", [P, 2 * T + S * E])
        ident = sb("ident", [P, P])
        ident16 = sb("ident16", [P, P], BF16)
        hmask = sb("hmask", [EH, HG])
        hmask16 = sb("hmask16", [EH, HG], BF16)
        lower4 = sb("lower4", [P, GROUPS * GROUPS])
        lower8 = sb("lower8", [P, 64])
        upper = sb("upper", [P, P])
        upper16 = sb("upper16", [P, P], BF16)
        ones16 = sb("ones16", [P, P], BF16)
        slot_no = sb("slot_no", [P, SLOT_TILES])
        chosen16 = sb("chosen16", [P, NT * NE1], BF16)
        first = sb("first", [P, 2, NT, NE1])
        weight = sb("weight", [P, 2, NT])
        place = sb("place", [P, 2, NT])
        place_i = sb("place_i", [P, 2, NT], mybir.dt.uint32)
        load_e = sb("load_e", [P, 4, NE1])
        of_tile = sb("of_tile", [P, SLOT_TILES])
        of_tile_i = sb("of_tile_i", [P, SLOT_TILES], mybir.dt.int32)
        tokb = sb("tokb", [P, E])
        wtok = sb("wtok", [P, KC, E])
        wq = sb("wq", [EH, 2, E])
        wk = sb("wk", [EH, 2, E])
        wv = sb("wv", [EH, 2, E])
        wo = sb("wo", [EH, 2, E])
        wpk = sb("wpk", [EH, 2, E])
        wpq = sb("wpq", [EH, 2, E])
        relr = sb("relr", [EH, 2, REL])
        relf = sb("relf", [EH, 2, REL])
        colb = sb("colb", [EH, 4, 2])
        bv = sb("bv", [P, E])
        bo = sb("bo", [P, E])
        bproj = sb("bproj", [P, E])
        bv1 = sb("bv1", [P, E])
        bqk1 = sb("bqk1", [EH, 2, 2])
        gate0 = sb("gate0", [EH, 2, NE0])
        gate1 = sb("gate1", [EH, 2, NE1])
        gbias = sb("gbias", [P, NE0])
        W13, W2 = 2 * (NE0 + 1) * 2 * INTER, (NE0 + 1) * E
        weights = sb("weights", [P, W13 + W2 + 4 * IPT * EH])
        w13 = weights[0:EH, 0:W13].rearrange("p (w e c i) -> p w e c i", w=2, e=NE0 + 1, c=2)
        w2 = weights[:, W13:W13 + W2].rearrange("p (e n) -> p e n", e=NE0 + 1)
        b2r = sb("b2r", [NE1, E])
        pkbd = sb("pkbd", [EH, 2, HG, REL])
        pqbd = sb("pqbd", [EH, 2, HG, REL])
        pos = sb("pos", [EH, 2, 2, REL])
        eps = sb("eps", [P, 1])
        rounding = sb("rounding", [P, 2])
        moments = sb("moments", [P, 2, 6])
        meanvar = sb("meanvar", [P, 2, 2])
        sdev = sb("sdev", [P, 2])
        rstd = sb("rstd", [P, 2])
        xn = sb("xn", [P, 2, E])
        xt = sb("xt", [EH, 2, 2, P])
        vt = sb("vt", [P, 2, E])
        kbd = weights[0:EH, W13 + W2:].rearrange("p (u g k) -> p u g k", u=2, g=2)
        vbd = sb("vbd", [EH, 2, 2, IPT, EH])
        st1 = sb("st1", [EH, 2, 2, P])
        ot = sb("ot", [EH, 2, 2, P])
        scores = sb("scores", [P, 2, 2 * E])
        top = sb("top", [P, 2, 2 * H])
        mass = sb("mass", [P, 2, 2 * H])
        logits = sb("logits", [P, NT, NE0])
        comb = sb("comb", [P, NT, NE0 + 1])
        rt = [sb(f"rt{i}", [P, NT, NE0]) for i in range(3)]
        small = sb("small", [P, NT, 2])
        v16 = sb("v16", [P, 2, E], BF16)
        combc = sb("combc", [P, 2, NE1])
        combT = sb("combT", [NE1, 2, P])
        stats = sb("stats", [P, 8, NT])
        peak = sb("peak", [P, 8])
        peaks = sb("peaks", [P, 8])
        qs = sb("qs", [P, 8])
        qi = sb("qi", [P, 8])
        prod = sb("prod", [P, 4])
        bank = [ctx.enter_context(nc.psum_tensor(f"bank{i}", [P, 512], F32)) for i in range(8)]

        def halves(buf, width=T):
            return buf[0:EH, :].rearrange("p (g t) -> p g t", g=2)

        xnT_v = halves(xnT)
        qT_v, kT_v, sT_v = halves(qT), halves(kT), halves(sT)
        pinv_v = big[:, 0:OC * 256].rearrange("p (o k) -> p o k", o=OC)
        pw_v = big[:, OC * 256:OC * 256 + OC * CHANS * E].rearrange("p (o k) -> p o k", o=OC)
        pT_v = big[0:EH, 0:2 * T].rearrange("p (g t) -> p g t", g=2)
        t2 = big[:, 2 * T:2 * T + S * E].rearrange("p (i k) -> p i k", i=S)
        xall = t2
        vall = sT[:, 0:NT * E].rearrange("p (n e) -> p n e", n=NT)
        q16 = xnT[0:EH, 0:2 * P].bitcast(BF16).rearrange("p (u g t) -> p u g t", u=2, g=2)
        k16 = xnT[0:EH, 2 * P:4 * P].bitcast(BF16).rearrange("p (u g t) -> p u g t", u=2, g=2)
        wqkv32 = big[0:EH, 0:6 * E].rearrange("p (c n) -> p c n", c=2)
        wproj32 = big[0:EH, 6 * E:8 * E].rearrange("p (c n) -> p c n", c=2)
        wqkv16 = big[0:EH, 8 * E:11 * E].bitcast(BF16).rearrange("p (c n) -> p c n", c=2)
        wproj16 = big[0:EH, 11 * E:12 * E].bitcast(BF16).rearrange("p (c n) -> p c n", c=2)
        wround = big[0:EH, 12 * E:18 * E].rearrange("p (c n) -> p c n", c=2)
        w1_all = qks[0:EH + 1, :].rearrange("p (e c f) -> p e c f", e=NE1, c=2)
        w2_all = weights[:, 0:NE1 * FC * E].rearrange("p (e c n) -> p e c n", e=NE1, c=FC)
        hidden = big[:, 0:2 * FF].rearrange("p (u f) -> p u f", u=2)
        hiddenT = big[:, 2 * FF:4 * FF].rearrange("p (u f) -> p u f", u=2)
        y_out = big[:, 4 * FF:4 * FF + 2 * E].rearrange("p (u e) -> p u e", u=2)
        xs = xn
        xsT = big[0:EH + 1, 4 * FF + 2 * E:4 * FF + 2 * E + 4 * P].rearrange("p (u c t) -> p u c t", u=2, c=2)
        y_in = qks[:, 0:2 * NT * E].rearrange("p (k n e) -> p k n e", k=2, n=NT)
        oT_v = xnT_v
        hidden0 = qT[:, 0:3 * 512].rearrange("p (u t) -> p u t", u=3)
        silu0 = qT[:, 3 * 512:6 * 512].rearrange("p (u t) -> p u t", u=3)
        pairs = big[:, 0:NT * 64]
        ties = big[:, NT * 64:2 * NT * 64]
        x16 = scores[:, :, :].bitcast(BF16)
        vbd16 = vbd[:, :, :, :, :].rearrange("p u g b k -> p u (g b k)").bitcast(BF16)
        kbd16 = kbd[:, :, :, :].rearrange("p u g k -> p u (g k)").bitcast(BF16)

        v_scr = nc.dram_tensor("v_scratch", [T, E], F32, kind="Internal").ap()
        x_slots = nc.dram_tensor("x_slots", [SLOT_TILES * P, E], F32, kind="Internal").ap()
        y_slots = nc.dram_tensor("y_slots", [SLOT_TILES * P, E], F32, kind="Internal").ap()
        v_scr16 = nc.dram_tensor("v_scratch16", [T, E], BF16, kind="Internal").ap()

        passed = sem("passed")

        def moments_of(dve, t, u, steps_done, written, written_count):
            wait_alone(dve, written, written_count, passed)
            nc.vector.bn_stats(moments[:, u, :], h[:, ds(t, 1), :].rearrange("p a e -> p (a e)"))\
                .then_inc(steps_done, 1)
            wait_alone(dve, steps_done, 2 * t + 1, passed)
            nc.vector.bn_aggr(meanvar[:, u, :], moments[:, u, :]).then_inc(steps_done, 1)

        def sdev_of(act, t, u, steps_done, sdev_ready, inverted):
            act.wait_ge(steps_done, 2 * t + 2)
            wait(act, inverted, t - 1)
            nc.scalar.activation(sdev[:, u:u + 1], meanvar[:, u, 1:2], ACT.Sqrt, bias=eps[:, 0:1])\
                .then_inc(sdev_ready, 1)

        def normalise(dve, t, u, sdev_ready, inverted, xn_ready, dest):
            dve.wait_ge(sdev_ready, t + 1)
            nc.vector.reciprocal(rstd[:, u:u + 1], sdev[:, u:u + 1]).then_inc(inverted, 1)
            dve.wait_ge(inverted, t + 1)
            nc.vector.tensor_scalar(dest, h[:, ds(t, 1), :].rearrange("p a e -> p (a e)"),
                                    meanvar[:, u, 0:1], rstd[:, u:u + 1], ALU.subtract, ALU.mult)\
                .then_inc(xn_ready, 1)

        consts = early_sem("consts")
        tokw = [early_sem(f"tokw{i}") for i in range(4)]
        wtok_ps = early_sem("wtok_ps")
        wtok_done = early_sem("wtok_done")
        pos_ps = early_sem("pos_ps")
        pos_sb = early_sem("pos_sb")
        pos_bd = early_sem("pos_bd")
        cleared = early_sem("cleared")
        LOADS = [(ident, "ident"), (hmask, "hmask"), (lower4, "lower4"), (lower8, "lower8"),
                 (wpk, "L0_attn_Wpk"), (wpq, "L0_attn_Wpq"), (relr, "rel_reversed"), (relf, "rel"),
                 (colb, "L0_attn_columns"), (wq, "L0_attn_Wq"), (wk, "L0_attn_Wk"), (wv, "L0_attn_Wv"),
                 (wo, "L0_attn_Wo"), (gate0, "L0_ffn_gate_weight"), (gate1, "L1_ffn_Wr"),
                 (bqk1, "L1_attn_columns"), (w13, "L0_ffn_w13"), (w2, "L0_ffn_w2"), (upper, "upper"), (slot_no, "slot_numbers"),
                 (b2r, "L1_ffn_b2")]
        ROWS = [(tokb, "L0_tok_proj_bias"), (bv, "L0_attn_bv"), (bo, "L0_attn_bo"),
                (bproj, "L1_attn_b_proj"), (bv1, "L1_attn_b_v"), (gbias, "L0_ffn_gate_bias")]

        def whole(buf):
            return buf[tuple(slice(None) for _ in buf.shape)]

        with nc.Block() as block:
            @block.sync
            def _(sp):
                pinv_d = a["L0_tok_pinv"]
                pw_d = a["L0_tok_proj_weight"]
                for i in range(4):
                    sp.dma_start(pinv_v[:, 2 * i:2 * i + 2, :], pinv_d[:, 2 * i:2 * i + 2, :]).then_inc(tokw[i], 16)
                    sp.dma_start(pw_v[:, 2 * i:2 * i + 2, :], pw_d[:, 2 * i:2 * i + 2, :]).then_inc(tokw[i], 16)

            @block.gpsimd
            def _(pool):
                nc.gpsimd.memset(eps[:, :], EPS).then_inc(cleared, 1)
                nc.gpsimd.memset(ones16[:, :], 1.0).then_inc(cleared, 1)
                nc.gpsimd.memset(scores[:, 0, 0:E], 0.0).then_inc(cleared, 1)
                nc.gpsimd.memset(rounding[:, 0:1], ROUND).then_inc(cleared, 1)
                nc.gpsimd.memset(rounding[:, 1:2], -ROUND).then_inc(cleared, 1)
                nc.gpsimd.memset(comb[:, :, :], 1.0).then_inc(cleared, 1)
                nc.gpsimd.memset(stats[:, :, :], 0.0).then_inc(cleared, 1)

            @block.scalar
            def _(act):
                for buf, name in LOADS:
                    act.dma_start(whole(buf), a[name]).then_inc(consts, 16)
                for buf, name in ROWS:
                    act.dma_start(buf[:, :], a[name].partition_broadcast(P)).then_inc(consts, 16)
                act.wait_ge(consts, 16 * len(LOADS + ROWS))
                for n in range(4):
                    act.wait_ge(pos_ps, 4)
                    nc.scalar.activation(pos[:, n // 2, n % 2, :], bank[6][0:EH, 32 * n:32 * n + REL],
                                         ACT.Identity, bias=colb[:, 2 + n // 2, n % 2:n % 2 + 1]).then_inc(pos_sb, 1)
                nc.scalar.activation(ident16[:, :], ident[:, :], ACT.Copy).then_inc(pos_sb, 1)
                nc.scalar.activation(hmask16[:, :], hmask[:, :], ACT.Copy).then_inc(pos_sb, 1)
                nc.scalar.activation(upper16[:, :], upper[:, :], ACT.Copy).then_inc(pos_sb, 1)

            @block.tensor
            def _(pe):
                pe.wait_ge(consts, 16 * len(LOADS + ROWS))
                for n, (w, rel) in enumerate(((wpk, relr), (wpk, relr), (wpq, relf), (wpq, relf))):
                    g = n % 2
                    for c in range(2):
                        mm = nc.tensor.matmul(bank[6][0:EH, 32 * n:32 * n + REL], w[:, c, g * EH:(g + 1) * EH],
                                              rel[:, c, :], start=(c == 0), stop=(c == 1))
                    mm.then_inc(pos_ps, 1)
                for o in range(OC):
                    if o % 2 == 0:
                        pe.wait_ge(tokw[o // 2], 32)
                    for k in range(KC):
                        c, half = k // 2, k % 2
                        mm = nc.tensor.matmul(bank[k][:, 0:E], pinv_v[:, o, half * P:(half + 1) * P],
                                              pw_v[:, o, c * E:(c + 1) * E], start=(o == 0), stop=(o == OC - 1))
                        if o == OC - 1:
                            mm.then_inc(wtok_ps, 1)

            @block.vector
            def _(dve):
                for n in range(4):
                    dve.wait_ge(pos_sb, n + 1)
                    dest = (pkbd, pqbd)[n // 2]
                    nc.vector.tensor_tensor(
                        dest[:, n % 2, :, :],
                        pos[:, n // 2, n % 2, :].unsqueeze(1).broadcast_to([EH, HG, REL]),
                        hmask[:, :].unsqueeze(2).broadcast_to([EH, HG, REL]), ALU.mult).then_inc(pos_bd, 1)
                for k in range(KC):
                    dve.wait_ge(wtok_ps, k + 1)
                    nc.vector.tensor_copy(wtok[:, k, :], bank[k][:, 0:E]).then_inc(wtok_done, 1)

        x_loaded = [early_sem(f"x_loaded{u}") for u in range(2)]
        slots_zero = early_sem("slots_zero")
        embedded, h_done, ln1, sdev1, inv1, xn1, tr1, xt1 = (early_sem(n) for n in (
            "embedded", "h_done", "ln1", "sdev1", "inv1", "xn1", "tr1", "xt1"))
        qk_ps, v_ps, qk_sb, v_sb, kbd_done, s_ps, s_sb = (early_sem(n) for n in (
            "qk_ps", "v_ps", "qk_sb", "v_sb", "kbd_done", "s_ps", "s_sb"))
        v_stored = [early_sem(f"v_stored{u}") for u in range(2)]
        xload = ctx.enter_context(nc.sbuf_tensor("xload", [P, 2, KC * P], F32))

        with nc.Block() as block:
            @block.sync
            def _(sp):
                sp.dma_start(x_slots.rearrange("(n p) e -> p n e", p=P),
                             scores[:, 0:1, 0:E].broadcast_to([P, SLOT_TILES, E])).then_inc(slots_zero, 16)

                def load(t, u):
                    wait(sp, embedded, t - 1)
                    sp.dma_start(xload[:, u, :], a["x"][ds(t, 1), :, :].rearrange("a p k -> p (a k)"))\
                        .then_inc(x_loaded[u], 16)

                steps(sp, NT, [(load, 0)])
                sp.wait_ge(slots_zero, 16)

            @block.gpsimd
            def _(pool):
                def store(t, u):
                    pool.wait_ge(v_sb, t + 1)
                    pool.dma_start(v_scr[ds(t * P, P), :], vt[:, u, :]).then_inc(v_stored[u], 16)

                steps(pool, NT, [(store, 0)])
                for u in range(2):
                    pool.wait_ge(v_stored[u], 8 * NT)

            @block.tensor
            def _(pe):
                def transpose(t, u):
                    pe.wait_ge(xn1, t + 1)
                    wait(pe, xt1, t)
                    for c in range(2):
                        mm = nc.tensor.transpose(bank[2][0:EH, c * P:(c + 1) * P], xn[:, u, c * EH:(c + 1) * EH],
                                                 ident[:, :])
                    mm.then_inc(tr1, 1)

                def embed(t, u):
                    pe.wait_ge(x_loaded[u], in_slot(t, u))
                    wait(pe, h_done, t - 1)
                    for k in range(KC):
                        mm = nc.tensor.matmul(bank[u][:, 0:E], xload[:, u, k * P:(k + 1) * P], wtok[:, k, :],
                                              start=(k == 0), stop=(k == KC - 1))
                    mm.then_inc(embedded, 1)

                def project(t, u):
                    pe.wait_ge(xt1, t + 1)
                    wait(pe, qk_sb, 4 * t)
                    for n, w in enumerate((wq, wq, wk, wk)):
                        for c in range(2):
                            mm = nc.tensor.matmul(bank[3][0:EH, n * P:(n + 1) * P],
                                                  w[:, c, (n % 2) * EH:(n % 2 + 1) * EH], xt[:, u, c, :],
                                                  start=(c == 0), stop=(c == 1))
                    mm.then_inc(qk_ps, 1)
                    wait(pe, v_sb, t)
                    for c in range(2):
                        mm = nc.tensor.matmul(bank[4][:, 0:E], xt[:, u, c, :], wv[:, c, :],
                                              start=(c == 0), stop=(c == 1))
                    mm.then_inc(v_ps, 1)

                def score(t, u):
                    pe.wait_ge(kbd_done, 2 * t + 2)
                    pe.wait_ge(qk_sb, 4 * t + 4)
                    wait(pe, s_sb, t - 1)
                    for g in range(2):
                        for b in range(IPT):
                            mm = nc.tensor.matmul(bank[5 + u][0:EH, g * P + b * S:g * P + (b + 1) * S],
                                                  kbd[:, u, g, b * EH:(b + 1) * EH],
                                                  qT_v[:, g, ds(t * P + b * S, S)], start=True, stop=True)
                    mm.then_inc(s_ps, 1)

                steps(pe, NT, [(score, 5), (project, 3), (transpose, 2), (embed, 0)])

            @block.scalar
            def _(act):
                def copy_x(t, u):
                    act.wait_ge(tr1, t + 1)
                    wait(act, v_ps, t - 1)
                    nc.scalar.activation(xt[:, u, :, :].rearrange("p c t -> p (c t)"), bank[2][0:EH, 0:2 * P],
                                         ACT.Copy).then_inc(xt1, 1)

                def deviation(t, u):
                    sdev_of(act, t, u, ln1, sdev1, inv1)

                def copy_qk(t, u):
                    act.wait_ge(qk_ps, t + 1)
                    for n in range(4):
                        dest = (qT_v, kT_v)[n // 2]
                        nc.scalar.activation(dest[:, n % 2, ds(t * P, P)], bank[3][0:EH, n * P:(n + 1) * P],
                                             ACT.Identity, bias=colb[:, n // 2, n % 2:n % 2 + 1]).then_inc(qk_sb, 1)

                def copy_s(t, u):
                    act.wait_ge(s_ps, t + 1)
                    nc.scalar.activation(sT_v[:, :, ds(t * P, P)],
                                         bank[5 + u][0:EH, 0:2 * P].rearrange("p (g t) -> p g t", g=2),
                                         ACT.Copy).then_inc(s_sb, 1)

                steps(act, NT, [(copy_s, 5), (copy_qk, 3), (copy_x, 2), (deviation, 0)])

            @block.vector
            def _(dve):
                def norm(t, u):
                    wait(dve, tr1, t - 1)
                    normalise(dve, t, u, sdev1, inv1, xn1, xn[:, u, :])

                def residual(t, u):
                    dve.wait_ge(embedded, t + 1)
                    nc.vector.tensor_tensor(h[:, ds(t, 1), :].rearrange("p a e -> p (a e)"), bank[u][:, 0:E],
                                            tokb[:, :], ALU.add).then_inc(h_done, 1)
                    moments_of(dve, t, u, ln1, h_done, t + 1)

                def values(t, u):
                    dve.wait_ge(v_ps, t + 1)
                    wait(dve, v_stored[u], in_slot(t, u) - 16)
                    nc.vector.tensor_tensor(vt[:, u, :], bank[4][:, 0:E], bv[:, :], ALU.add).then_inc(v_sb, 1)

                def keys(t, u):
                    wait(dve, s_ps, t - 1)
                    dve.wait_ge(qk_sb, 4 * t + 4)
                    for g in range(2):
                        nc.vector.tensor_tensor(
                            kbd[:, u, g, :].rearrange("p (b m j) -> p b m j", b=IPT, m=HG),
                            kT_v[:, g, ds(t * P, P)].rearrange("p (b j) -> p b j", b=IPT).unsqueeze(2)
                            .broadcast_to([EH, IPT, HG, S]),
                            hmask[:, :].unsqueeze(1).unsqueeze(3).broadcast_to([EH, IPT, HG, S]),
                            ALU.mult).then_inc(kbd_done, 1)

                steps(dve, NT, [(keys, 4), (values, 3), (norm, 1), (residual, 0)])

        ki_done, t2_ps, t2_sb, qs_done, d_ps, p_done, pt_ps, pt_sb, sm = (early_sem(n) for n in (
            "ki_done", "t2_ps", "t2_sb", "qs_done", "d_ps", "p_done", "pt_ps", "pt_sb", "sm"))
        ss_done, exp_done, share_done = early_sem("ss_done"), early_sem("exp_done"), early_sem("share_done")
        stage = kbd[:, :, :, :].rearrange("p u g k -> p (u g k)")[:, 0:16 * P]\
            .rearrange("p (u i k g b) -> p u i k g b", u=2, i=2, k=2, g=2)

        def at_position(buf, i):
            return buf.rearrange("p g (b i) -> p g b i", i=S)[:, :, :, ds(i, 1)].rearrange("p g b i -> p g (b i)")

        with nc.Block() as block:
            @block.gpsimd
            def _(pool):
                def keys(j, u):
                    wait(pool, t2_ps, j - 1)
                    nc.gpsimd.tensor_copy(stage[:, u, 0, 0, :, :], at_position(kT_v, j)).then_inc(ki_done, 1)

                steps(pool, S, [(keys, 0)])

                def queries(n, u):
                    if isinstance(n, int) and n < 2:
                        pool.wait_ge(t2_ps, S)
                    wait(pool, d_ps, n - 1)
                    for i in range(2):
                        nc.gpsimd.tensor_copy(stage[:, u, i, 0, :, :], at_position(qT_v, 2 * n + i))\
                            .then_inc(qs_done, 1)

                steps(pool, S // 2, [(queries, 0)])

            @block.tensor
            def _(pe):
                def key_terms(j, u):
                    pe.wait_ge(ki_done, j + 1)
                    wait_alone(pe, t2_sb, j - 1, passed)
                    for g in range(2):
                        mm = nc.tensor.matmul(bank[u][:, g * EH:(g + 1) * EH], stage[:, u, 0, 0, g, :],
                                              pqbd[:, g, :, ds(S - 1 - j, S)], start=True, stop=True)
                    mm.then_inc(t2_ps, 1)

                steps(pe, S, [(key_terms, 0)])

                def query_terms(n, u):
                    pe.wait_ge(qs_done, 2 * n + 2)
                    pe.wait_ge(ss_done, 2 * n + 2)
                    wait_alone(pe, sm, 4 * n - 7, passed)
                    for i in range(2):
                        for g in range(2):
                            region = bank[2 + u][:, i * E + g * EH:i * E + (g + 1) * EH]
                            nc.tensor.matmul(region, stage[:, u, i, 0, g, :],
                                             pkbd[:, g, :, ds(S - 1 - i - 2 * n, S)], start=True, stop=False)
                            mm = nc.tensor.matmul(region, stage[:, u, i, 1, g, :], ident[0:EH, 0:EH],
                                                  start=False, stop=True)
                    mm.then_inc(d_ps, 1)

                def turn(n, u):
                    pe.wait_ge(p_done, n + 1)
                    wait(pe, pt_sb, n - 1)
                    for m in range(4):
                        mm = nc.tensor.transpose(bank[4 + u][0:EH, m * P:(m + 1) * P],
                                                 scores[:, u, m * EH:(m + 1) * EH], ident[:, :])
                    mm.then_inc(pt_ps, 1)

                steps(pe, S // 2, [(turn, 2), (query_terms, 1)])

            @block.scalar
            def _(act):
                def keep_t2(j, u):
                    act.wait_ge(t2_ps, j + 1)
                    nc.scalar.activation(
                        t2.rearrange("p i (m j) -> p i m j", m=H)[:, :, :, ds(j, 1)].rearrange("p i m j -> p i (m j)"),
                        bank[u][:, 0:E].rearrange("p (m i) -> p i m", m=H), ACT.Copy).then_inc(t2_sb, 1)

                steps(act, S, [(keep_t2, 0)])

                def stage_scores(n, u):
                    wait(act, d_ps, n - 1)
                    for i in range(2):
                        nc.scalar.activation(stage[:, u, i, 1, :, :], at_position(sT_v, 2 * n + i), ACT.Copy)\
                            .then_inc(ss_done, 1)

                def exponent(n, u):
                    act.wait_ge(sm, 4 * n + 3)
                    nc.scalar.activation(scores[:, u, :], scores[:, u, :], ACT.Exp, scale=SOFT0).then_inc(exp_done, 1)

                def keep_p(n, u):
                    act.wait_ge(pt_ps, n + 1)
                    for i in range(2):
                        dest = pT_v.rearrange("p g (b i) -> p g b i", i=S)[:, :, :, ds(2 * n + i, 1)]\
                            .rearrange("p g b i -> p g (b i)")
                        ins = nc.scalar.activation(
                            dest, bank[4 + u][0:EH, i * 2 * P:(i + 1) * 2 * P].rearrange("p (g b) -> p g b", g=2),
                            ACT.Copy)
                    ins.then_inc(pt_sb, 1)

                steps(act, S // 2, [(keep_p, 3), (stage_scores, 0), (exponent, 1)])

            @block.vector
            def _(dve):
                dve.wait_ge(t2_sb, S)

                def by_head(buf):
                    return buf.rearrange("p (m j) -> p m j", j=S)

                def spread(buf):
                    return buf.unsqueeze(2).broadcast_to([P, 2 * H, S])

                def shift(n, u):
                    dve.wait_ge(d_ps, n + 1)
                    wait(dve, pt_ps, n - 1)
                    nc.vector.tensor_tensor(scores[:, u, :], bank[2 + u][:, 0:2 * E],
                                            t2[:, ds(2 * n, 2), :].rearrange("p i k -> p (i k)"),
                                            ALU.add).then_inc(sm, 1)
                    dve.wait_ge(sm, 4 * n + 1)
                    nc.vector.tensor_reduce(top[:, u, :], by_head(scores[:, u, :]), AX.X, ALU.max).then_inc(sm, 1)
                    dve.wait_ge(sm, 4 * n + 2)
                    nc.vector.tensor_tensor(by_head(scores[:, u, :]), by_head(scores[:, u, :]),
                                            spread(top[:, u, :]), ALU.subtract).then_inc(sm, 1)

                def share(n, u):
                    dve.wait_ge(exp_done, n + 1)
                    nc.vector.tensor_reduce(mass[:, u, :], by_head(scores[:, u, :]), AX.X, ALU.add).then_inc(sm, 1)
                    dve.wait_ge(sm, 4 * n + 4)
                    nc.vector.reciprocal(top[:, u, :], mass[:, u, :]).then_inc(share_done, 1)
                    dve.wait_ge(share_done, n + 1)
                    nc.vector.tensor_tensor(by_head(scores[:, u, :]), by_head(scores[:, u, :]),
                                            spread(top[:, u, :]), ALU.mult).then_inc(p_done, 1)

                steps(dve, S // 2, [(share, 2), (shift, 1)])

        def tail_sems(tag):
            return {n: sem(n + tag) for n in (
                "moments", "sdev", "inverse", "xn", "turned", "xt", "gathered", "gate_ps", "gate_sb")}

        def tail_on_pe(pe, s, gate_w):
            def turn(t, u):
                pe.wait_ge(s["xn"], t + 1)
                wait(pe, s["xt"], t - 1)
                for c in range(2):
                    mm = nc.tensor.transpose(bank[4 + u][0:EH, c * P:(c + 1) * P],
                                             xn[:, u, c * EH:(c + 1) * EH], ident[:, :])
                mm.then_inc(s["turned"], 1)

            def gate(t, u):
                pe.wait_ge(s["xt"], t + 1)
                wait(pe, s["gate_sb"], t - 1)
                for c in range(2):
                    mm = nc.tensor.matmul(bank[6 + u][:, 0:NE0], xt[:, u, c, :], gate_w[:, c, :],
                                          start=(c == 0), stop=(c == 1))
                mm.then_inc(s["gate_ps"], 1)

            return turn, gate

        def tail_on_act(act, s):
            def copy_x(t, u):
                act.wait_ge(s["turned"], t + 1)
                wait(act, s["gate_ps"], t - 1)
                if s is tail2:
                    wait(act, s["gathered"], t - 1)
                nc.scalar.activation(xt[:, u, :, :].rearrange("p c t -> p (c t)"), bank[4 + u][0:EH, 0:2 * P],
                                     ACT.Copy).then_inc(s["xt"], 1)

            def deviation(t, u):
                sdev_of(act, t, u, s["moments"], s["sdev"], s["inverse"])

            return copy_x, deviation

        def tail_on_pool(pool, s):
            def gather(t, u):
                pool.wait_ge(s["xt"], t + 1)
                nc.gpsimd.tensor_copy(xnT_v[:, :, ds(t * P, P)], xt[:, u, :, :]).then_inc(s["gathered"], 1)

            return gather

        def tail_on_dve(dve, s):
            def norm(t, u):
                wait(dve, s["turned"], t - 1)
                if s is not tail2:
                    wait(dve, s["gathered"], t - 1)
                normalise(dve, t, u, s["sdev"], s["inverse"], s["xn"], xn[:, u, :])

            def keep_gate(t, u):
                dve.wait_ge(s["gate_ps"], t + 1)
                nc.vector.tensor_copy(logits[:, ds(t, 1), :].rearrange("p a e -> p (a e)"),
                                      bank[6 + u][:, 0:NE0]).then_inc(s["gate_sb"], 1)

            return norm, keep_gate

        tail2 = tail_sems("2")
        pv_ps, ot_sb, o_ps, h2 = (sem(n) for n in ("pv_ps", "ot_sb", "o_ps", "h2"))
        v_loaded = [sem(f"v_loaded{u}") for u in range(2)]
        vbd_done = [sem(f"vbd_done{g}") for g in range(2)]
        vrep = kT[0:EH, 0:2 * IPT * E].rearrange("p (u b e) -> p u b e", u=2, b=IPT)

        def spread_values(eng, t, u, g):
            eng.wait_ge(v_loaded[u], HG * in_slot(t, u))
            wait(eng, pv_ps, t - 1)
            shape = [EH, IPT, HG, D]
            eng.tensor_tensor(vbd[:, u, g, :, :].rearrange("p b (m d) -> p b m d", m=HG),
                              vrep[:, u, :, g * EH:(g + 1) * EH].rearrange("p b (m d) -> p b m d", m=HG),
                              hmask[:, :].unsqueeze(1).unsqueeze(3).broadcast_to(shape), ALU.mult)\
                .then_inc(vbd_done[g], 1)

        with nc.Block() as block:
            @block.sync
            def _(sp):
                src = v_scr.rearrange("(b j) e -> j b e", j=S)

                def load(t, u):
                    wait(sp, vbd_done[0], t - 1)
                    wait(sp, vbd_done[1], t - 1)
                    for m in range(HG):
                        sp.dma_start(vrep[m * S:(m + 1) * S, u, :, :], src[:, ds(t * IPT, IPT), :])\
                            .then_inc(v_loaded[u], 16)

                steps(sp, NT, [(load, 0)])

            @block.tensor
            def _(pe):
                def attend(t, u):
                    pe.wait_ge(vbd_done[0], t + 1)
                    pe.wait_ge(vbd_done[1], t + 1)
                    wait(pe, ot_sb, t - 1)
                    for g in range(2):
                        for b in range(IPT):
                            mm = nc.tensor.matmul(bank[u][0:EH, g * P + b * S:g * P + (b + 1) * S],
                                                  vbd[:, u, g, b, :], pT_v[:, g, ds(t * P + b * S, S)],
                                                  start=True, stop=True)
                    mm.then_inc(pv_ps, 1)

                def project(t, u):
                    pe.wait_ge(ot_sb, t + 1)
                    wait(pe, h2, 2 * t - 2)
                    for g in range(2):
                        mm = nc.tensor.matmul(bank[2 + u][:, 0:E], ot[:, u, g, :], wo[:, g, :],
                                              start=(g == 0), stop=(g == 1))
                    mm.then_inc(o_ps, 1)

                turn, gate = tail_on_pe(pe, tail2, gate0)
                steps(pe, NT, [(gate, 5), (turn, 4), (project, 2), (attend, 1)])

            @block.scalar
            def _(act):
                def keep_o(t, u):
                    act.wait_ge(pv_ps, t + 1)
                    wait(act, o_ps, t - 1)
                    nc.scalar.activation(ot[:, u, :, :].rearrange("p g t -> p (g t)"), bank[u][0:EH, 0:2 * P],
                                         ACT.Copy).then_inc(ot_sb, 1)

                copy_x, deviation = tail_on_act(act, tail2)
                steps(act, NT, [(copy_x, 4), (keep_o, 1), (deviation, 2)])

            @block.gpsimd
            def _(pool):
                gather = tail_on_pool(pool, tail2)
                steps(pool, NT, [(gather, 4), (lambda t, u: spread_values(nc.gpsimd, t, u, 1), 0)])

            @block.vector
            def _(dve):
                def residual(t, u):
                    tile = h[:, ds(t, 1), :].rearrange("p a e -> p (a e)")
                    dve.wait_ge(o_ps, t + 1)
                    nc.vector.tensor_tensor(tile, bank[2 + u][:, 0:E], tile, ALU.add).then_inc(h2, 1)
                    dve.wait_ge(h2, 2 * t + 1)
                    nc.vector.tensor_tensor(tile, tile, bo[:, :], ALU.add).then_inc(h2, 1)
                    moments_of(dve, t, u, tail2["moments"], h2, 2 * t + 2)

                norm, keep_gate = tail_on_dve(dve, tail2)
                steps(dve, NT, [(keep_gate, 5), (norm, 3), (lambda t, u: spread_values(nc.vector, t, u, 0), 0),
                                (residual, 2)])

        r0, sig_done = sem("r0"), sem("sig_done")

        def ranks(link, value, n, lower, rank, eligible=None):
            shape = [P, NT, n, n]
            gt = pairs[:, 0:NT * n * n].rearrange("p (t a b) -> p t a b", a=n, b=n)
            eq = ties[:, 0:NT * n * n].rearrange("p (t a b) -> p t a b", a=n, b=n)
            of_b, of_a = value.unsqueeze(2).broadcast_to(shape), value.unsqueeze(3).broadcast_to(shape)
            nc.vector.tensor_tensor(gt, of_b, of_a, ALU.is_gt)
            link(nc.vector.tensor_tensor(eq, of_b, of_a, ALU.is_equal))
            link(nc.vector.tensor_tensor(eq, eq, lower.rearrange("p (a b) -> p a b", a=n).unsqueeze(1)
                                         .broadcast_to(shape), ALU.mult))
            link(nc.vector.tensor_tensor(gt, gt, eq, ALU.add))
            if eligible is not None:
                link(nc.vector.tensor_tensor(gt, gt, eligible.unsqueeze(2).broadcast_to(shape), ALU.mult))
            link(nc.vector.tensor_reduce(rank, gt, AX.X, ALU.add))

        with nc.Block() as block:
            @block.scalar
            def _(act):
                nc.scalar.activation(logits[:, :, :], logits[:, :, :], ACT.Sigmoid).then_inc(sig_done, 1)

            @block.vector
            def _(dve):
                count = [0]

                def link(ins):
                    count[0] += 1
                    ins.then_inc(r0, 1)
                    dve.wait_ge(r0, count[0])

                s, chosen, rank = rt
                shape8 = [P, NT, NE0]
                dve.wait_ge(sig_done, 1)
                link(nc.vector.tensor_tensor(s[:, :, :], logits[:, :, :],
                                             gbias[:, :].unsqueeze(1).broadcast_to(shape8), ALU.add))
                two = s[:, :, :].rearrange("p t (g k) -> p t g k", k=2)
                group = rank[:, :, 0:GROUPS]
                link(nc.vector.tensor_tensor(group, two[:, :, :, 0], two[:, :, :, 1], ALU.add))
                grank = rank[:, :, GROUPS:2 * GROUPS]
                ranks(link, group, GROUPS, lower4[:, :], grank)
                link(nc.vector.tensor_scalar(grank, grank, 2.0, None, ALU.is_lt))
                link(nc.vector.tensor_copy(chosen[:, :, :].rearrange("p t (g k) -> p t g k", k=2),
                                           grank.unsqueeze(3).broadcast_to([P, NT, GROUPS, 2])))
                ranks(link, s[:, :, :], NE0, lower8[:, :], rank[:, :, :], chosen[:, :, :])
                link(nc.vector.scalar_tensor_tensor(s[:, :, :], rank[:, :, :], 2.0, chosen[:, :, :],
                                                    ALU.is_lt, ALU.mult))
                link(nc.vector.tensor_tensor(s[:, :, :], s[:, :, :], logits[:, :, :], ALU.mult))
                link(nc.vector.tensor_reduce(small[:, :, 0], s[:, :, :], AX.X, ALU.add))
                link(nc.vector.tensor_scalar(small[:, :, 0], small[:, :, 0], 1e-6, None, ALU.add))
                link(nc.vector.reciprocal(small[:, :, 1], small[:, :, 0]))
                link(nc.vector.tensor_tensor(comb[:, :, 0:NE0], s[:, :, :],
                                             small[:, :, 1:2].broadcast_to(shape8), ALU.mult))

        h13_ps, silu_done, hid_done, y_ps, y_done = (sem(n) for n in (
            "h13_ps", "silu_done", "hid_done", "y_ps", "y_done"))
        EXP = NE0 + 1

        with nc.Block() as block:
            @block.tensor
            def _(pe):
                def up(blk, e):
                    n = blk * EXP + e
                    wait(pe, hid_done, n - 2)
                    for w in range(2):
                        for c in range(2):
                            mm = nc.tensor.matmul(bank[2 * (e % 3) + w][:, :], w13[:, w, e, c, :],
                                                  xnT_v[:, c, ds(blk * BLK, BLK)], start=(c == 0), stop=(c == 1))
                    mm.then_inc(h13_ps, 1)

                def down(blk, e):
                    n = blk * EXP + e
                    pe.wait_ge(hid_done, n + 1)
                    for k in range(TPB):
                        wait(pe, y_done, 4 * n - 2 * (1 - k // 2))
                        mm = nc.tensor.matmul(bank[6 + k // 2][:, (k % 2) * E:(k % 2 + 1) * E],
                                              hidden0[:, e % 3, k * P:(k + 1) * P], w2[:, e, :],
                                              start=True, stop=True)
                        mm.then_inc(y_ps, 1)

                def one(blk):
                    up(blk, 0)
                    for e in range(EXP):
                        if e + 1 < EXP:
                            up(blk, e + 1)
                        down(blk, e)

                one(0)
                with pe.Fori(1, NB, 1) as blk:
                    one(blk)

            @block.scalar
            def _(act):
                def one(blk):
                    for e in range(EXP):
                        n = blk * EXP + e
                        act.wait_ge(h13_ps, n + 1)
                        wait(act, hid_done, n - 2)
                        nc.scalar.activation(silu0[:, e % 3, :], bank[2 * (e % 3)][:, :], ACT.Silu)\
                            .then_inc(silu_done, 1)

                one(0)
                with act.Fori(1, NB, 1) as blk:
                    one(blk)

            @block.vector
            def _(dve):
                def gate(blk, e):
                    n = blk * EXP + e
                    dve.wait_ge(silu_done, n + 1)
                    wait(dve, y_ps, 4 * n - 8)
                    nc.vector.tensor_tensor(hidden0[:, e % 3, :], silu0[:, e % 3, :], bank[2 * (e % 3) + 1][:, :],
                                            ALU.mult).then_inc(hid_done, 1)

                def add(blk, e):
                    n = blk * EXP + e
                    for k in range(TPB):
                        tile = h[:, ds(blk * TPB + k, 1), :].rearrange("p a e -> p (a e)")
                        dve.wait_ge(y_ps, 4 * n + 2 * (k // 2) + 2)
                        wait(dve, y_done, 4 * n + k - 3)
                        nc.vector.scalar_tensor_tensor(
                            tile, bank[6 + k // 2][:, (k % 2) * E:(k % 2 + 1) * E],
                            comb[:, ds(blk * TPB + k, 1), e:e + 1].rearrange("p a e -> p (a e)"), tile,
                            ALU.mult, ALU.add).then_inc(y_done, 1)

                def one(blk):
                    gate(blk, 0)
                    for e in range(EXP):
                        if e + 1 < EXP:
                            gate(blk, e + 1)
                        add(blk, e)

                one(0)
                with dve.Fori(1, NB, 1) as blk:
                    one(blk)

        wq1_loaded = sem("wq1_loaded")
        ln3, sdev3, inv3, xn3, am3, rng3, pr3, sc3 = (sem(n) for n in (
            "ln3", "sdev3", "inv3", "xn3", "am3", "rng3", "pr3", "sc3"))

        def absmax(dest, src):
            return nc.vector.tensor_reduce(dest, src, AX.XY if len(src.shape) == 3 else AX.X, ALU.max,
                                           apply_absolute_value=True)

        def scales(dve, pool_done, done, lo, hi, base=0):
            dve.wait_ge(pool_done, 1)
            nc.vector.tensor_scalar(qs[:, lo:hi], peaks[:, lo:hi], 1.0 / QMAX, 1e-8, ALU.mult, ALU.max)\
                .then_inc(done, 1)
            dve.wait_ge(done, base + 1)
            nc.vector.reciprocal(qi[:, lo:hi], qs[:, lo:hi]).then_inc(done, 1)
            dve.wait_ge(done, base + 2)

        X_, WQ_, WP_, Q_, K_, V_, P_, O_ = range(8)

        with nc.Block() as block:
            @block.sync
            def _(sp):
                sp.dma_start(wqkv32, a["L1_attn_w_qkv"]).then_inc(wq1_loaded, 16)
                sp.dma_start(wproj32, a["L1_attn_w_proj"]).then_inc(wq1_loaded, 16)

            @block.scalar
            def _(act):
                steps(act, NT, [(lambda t, u: sdev_of(act, t, u, ln3, sdev3, inv3), 0)])

            @block.vector
            def _(dve):
                def mean(t, u):
                    moments_of(dve, t, u, ln3, y_done, TPB * NB * EXP)

                def norm(t, u):
                    normalise(dve, t, u, sdev3, inv3, xn3,
                              xall[:, ds(t, 1), :].rearrange("p a e -> p (a e)"))

                steps(dve, NT, [(mean, 0), (norm, 1)])
                dve.wait_ge(xn3, NT)
                nc.vector.memset(peak[:, :], 0.0).then_inc(am3, 1)
                dve.wait_ge(am3, 1)
                absmax(peak[:, X_:X_ + 1], xall.rearrange("p n e -> p (n e)")).then_inc(am3, 1)
                dve.wait_ge(wq1_loaded, 32)
                absmax(peak[0:EH, WQ_:WQ_ + 1], wqkv32.rearrange("p c n -> p (c n)")).then_inc(am3, 1)
                absmax(peak[0:EH, WP_:WP_ + 1], wproj32.rearrange("p c n -> p (c n)")).then_inc(am3, 1)
                scales(dve, pr3, sc3, X_, WP_ + 1)
                nc.vector.tensor_scalar(prod[:, 0:1], qs[:, X_:X_ + 1], qs[:, WQ_:WQ_ + 1], None, ALU.mult)\
                    .then_inc(sc3, 1)
                nc.vector.tensor_scalar(wround, wqkv32, qi[0:EH, WQ_:WQ_ + 1], ROUND, ALU.mult, ALU.add)\
                    .then_inc(sc3, 1)
                nc.vector.tensor_scalar(wproj32, wproj32, qi[0:EH, WP_:WP_ + 1], ROUND, ALU.mult, ALU.add)\
                    .then_inc(sc3, 1)
                dve.wait_ge(sc3, 5)
                nc.vector.tensor_scalar(wqkv16, wround, ROUND, QMAX, ALU.subtract, ALU.min).then_inc(sc3, 1)
                nc.vector.tensor_scalar(wproj16, wproj32, ROUND, QMAX, ALU.subtract, ALU.min).then_inc(sc3, 1)

            @block.gpsimd
            def _(pool):
                for used in early_sems:
                    pool.sem_clear(used)

                pool.wait_ge(am3, 4)
                nc.gpsimd.partition_all_reduce(peaks[:, 0:3], peak[:, 0:3], P, RMAX).then_inc(pr3, 1)

        early.close()

        xr4, xi4, tr4, xt4, q_ps4, v_ps4, q_sb4, v_sb4, st4, pr4, am4, sc4 = (sem(n) for n in (
            "xr4", "xi4", "tr4", "xt4", "q_ps4", "v_ps4", "q_sb4", "v_sb4", "st4", "pr4", "am4", "sc4"))
        xt16 = xt[:, :, :, :].rearrange("p u c t -> p u (c t)").bitcast(BF16)

        with nc.Block() as block:
            @block.vector
            def _(dve):
                def quantise(t, u):
                    nc.vector.tensor_scalar(xn[:, u, :], xall[:, ds(t, 1), :].rearrange("p a e -> p (a e)"),
                                            qi[:, X_:X_ + 1], ROUND, ALU.mult, ALU.add).then_inc(xr4, 1)
                    dve.wait_ge(xr4, t + 1)
                    wait(dve, tr4, t - 1)
                    nc.vector.tensor_scalar(x16[:, u, 0:E], xn[:, u, :], ROUND, QMAX, ALU.subtract, ALU.min)\
                        .then_inc(xi4, 1)

                def values(t, u):
                    tile = vall[:, ds(t, 1), :].rearrange("p a e -> p (a e)")
                    dve.wait_ge(v_ps4, t + 1)
                    nc.vector.scalar_tensor_tensor(tile, bank[4 + u][:, 0:E], prod[:, 0:1], bv1[:, :],
                                                   ALU.mult, ALU.add).then_inc(v_sb4, 1)
                    dve.wait_ge(v_sb4, t + 1)
                    absmax(stats[:, V_, ds(t, 1)], tile).then_inc(st4, 1)
                    dve.wait_ge(q_sb4, 4 * t + 4)
                    absmax(stats[0:EH, Q_, ds(t, 1)], qT_v[:, :, ds(t * P, P)]).then_inc(st4, 1)
                    absmax(stats[0:EH, K_, ds(t, 1)], kT_v[:, :, ds(t * P, P)]).then_inc(st4, 1)

                steps(dve, NT, [(quantise, 0), (values, 2)])
                dve.wait_ge(st4, 3 * NT)
                nc.vector.tensor_reduce(peak[:, Q_:V_ + 1], stats[:, Q_:V_ + 1, :], AX.X, ALU.max).then_inc(am4, 1)
                scales(dve, pr4, sc4, Q_, V_ + 1)
                nc.vector.tensor_scalar(prod[:, 1:2], qs[:, Q_:Q_ + 1], qs[:, K_:K_ + 1], SOFT1, ALU.mult, ALU.mult)\
                    .then_inc(sc4, 1)

            @block.gpsimd
            def _(pool):
                pool.wait_ge(am4, 1)
                nc.gpsimd.partition_all_reduce(peaks[:, Q_:V_ + 1], peak[:, Q_:V_ + 1], P, RMAX).then_inc(pr4, 1)

            @block.tensor
            def _(pe):
                def turn(t, u):
                    pe.wait_ge(xi4, t + 1)
                    wait(pe, xt4, t - 1)
                    for c in range(2):
                        mm = nc.tensor.transpose(bank[u][0:EH, c * P // 2:(c + 1) * P // 2].bitcast(BF16),
                                                 x16[:, u, c * EH:(c + 1) * EH], ident16[:, :])
                    mm.then_inc(tr4, 1)

                def project(t, u):
                    pe.wait_ge(xt4, t + 1)
                    wait(pe, q_sb4, 4 * t - 4)
                    for n in range(4):
                        for c in range(2):
                            mm = nc.tensor.matmul(bank[2 + u][0:EH, n * P:(n + 1) * P],
                                                  wqkv16[:, c, n * EH:(n + 1) * EH], xt16[:, u, c * P:(c + 1) * P],
                                                  start=(c == 0), stop=(c == 1))
                    mm.then_inc(q_ps4, 1)
                    wait(pe, v_sb4, t - 1)
                    for c in range(2):
                        mm = nc.tensor.matmul(bank[4 + u][:, 0:E], xt16[:, u, c * P:(c + 1) * P],
                                              wqkv16[:, c, 2 * E:3 * E], start=(c == 0), stop=(c == 1))
                    mm.then_inc(v_ps4, 1)

                steps(pe, NT, [(turn, 0), (project, 1)])

            @block.scalar
            def _(act):
                def copy_x(t, u):
                    act.wait_ge(tr4, t + 1)
                    wait(act, v_ps4, t - 1)
                    nc.scalar.activation(xt16[:, u, 0:2 * P], bank[u][0:EH, 0:P].bitcast(BF16), ACT.Copy)\
                        .then_inc(xt4, 1)

                def copy_qk(t, u):
                    act.wait_ge(q_ps4, t + 1)
                    for n in range(4):
                        dest = (qT_v, kT_v)[n // 2]
                        nc.scalar.activation(dest[:, n % 2, ds(t * P, P)], bank[2 + u][0:EH, n * P:(n + 1) * P],
                                             ACT.Identity, bias=bqk1[:, n // 2, n % 2:n % 2 + 1],
                                             scale=prod[0:EH, 0:1]).then_inc(q_sb4, 1)

                steps(act, NT, [(copy_x, 0), (copy_qk, 1)])

        qr5, q5, k5, v5, kbd5, s_ps5, s_sb5, sc_ps5, sm5, exp5, p5, st5, am5, pr5, sc5 = (sem(n) for n in (
            "qr5", "q5", "k5", "v5", "kbd5", "s_ps5", "s_sb5", "sc_ps5", "sm5", "exp5", "p5", "st5", "am5", "pr5",
            "sc5"))
        vr5 = sem("vr5")
        v_stored16 = [sem(f"v_stored16_{u}") for u in range(2)]
        pall = t2
        st5buf = xt
        qround = ot
        kround = st1

        with nc.Block() as block:
            @block.gpsimd
            def _(pool):
                def store(t, u):
                    pool.wait_ge(v5, t + 1)
                    pool.dma_start(v_scr16[ds(t * P, P), :], v16[:, u, :]).then_inc(v_stored16[u], 16)

                steps(pool, NT, [(store, 0)])
                for u in range(2):
                    pool.wait_ge(v_stored16[u], 8 * NT)
                pool.wait_ge(am5, 1)
                nc.gpsimd.partition_all_reduce(peaks[:, P_:P_ + 1], peak[:, P_:P_ + 1], P, RMAX).then_inc(pr5, 1)

            @block.vector
            def _(dve):
                def by_head(buf):
                    return buf.rearrange("p (m j) -> p m j", j=S)

                def spread(buf):
                    return buf.unsqueeze(2).broadcast_to([P, H, S])

                def keys(t, u):
                    wait(dve, s_ps5, t - 1)
                    nc.vector.tensor_scalar(kround[:, u, :, :], kT_v[:, :, ds(t * P, P)], qi[0:EH, K_:K_ + 1], ROUND,
                                            ALU.mult, ALU.add).then_inc(k5, 1)
                    dve.wait_ge(k5, 2 * t + 1)
                    nc.vector.tensor_scalar(k16[:, u, :, :], kround[:, u, :, :], ROUND, QMAX, ALU.subtract,
                                            ALU.min).then_inc(k5, 1)
                    dve.wait_ge(k5, 2 * t + 2)
                    for g in range(2):
                        nc.vector.tensor_tensor(
                            kbd16[:, u, g * IPT * EH:(g + 1) * IPT * EH]
                            .rearrange("p (b m j) -> p b m j", b=IPT, m=HG),
                            k16[:, u, g, :].rearrange("p (b j) -> p b j", b=IPT).unsqueeze(2)
                            .broadcast_to([EH, IPT, HG, S]),
                            hmask16[:, :].unsqueeze(1).unsqueeze(3).broadcast_to([EH, IPT, HG, S]),
                            ALU.mult).then_inc(kbd5, 1)

                def shift(t, u):
                    dve.wait_ge(sc_ps5, t + 1)
                    nc.vector.tensor_reduce(top[:, u, 0:H], by_head(bank[4 + u][:, 0:E]), AX.X, ALU.max)\
                        .then_inc(sm5, 1)
                    dve.wait_ge(sm5, 4 * t + 1)
                    nc.vector.tensor_tensor(by_head(scores[:, u, 0:E]), by_head(bank[4 + u][:, 0:E]),
                                            spread(top[:, u, 0:H]), ALU.subtract).then_inc(sm5, 1)

                def share(t, u):
                    tile = pall[:, ds(t, 1), :].rearrange("p a e -> p (a e)")
                    dve.wait_ge(exp5, t + 1)
                    nc.vector.tensor_reduce(mass[:, u, 0:H], by_head(scores[:, u, 0:E]), AX.X, ALU.add)\
                        .then_inc(sm5, 1)
                    dve.wait_ge(sm5, 4 * t + 3)
                    nc.vector.reciprocal(top[:, u, H:2 * H], mass[:, u, 0:H]).then_inc(sm5, 1)
                    dve.wait_ge(sm5, 4 * t + 4)
                    nc.vector.tensor_tensor(by_head(tile), by_head(scores[:, u, 0:E]), spread(top[:, u, H:2 * H]),
                                            ALU.mult).then_inc(p5, 1)

                def values(t, u):
                    nc.vector.tensor_scalar(xn[:, u, :], vall[:, ds(t, 1), :].rearrange("p a e -> p (a e)"),
                                            qi[:, V_:V_ + 1], ROUND, ALU.mult, ALU.add).then_inc(vr5, 1)
                    dve.wait_ge(vr5, t + 1)
                    wait(dve, v_stored16[u], in_slot(t, u) - 16)
                    nc.vector.tensor_scalar(v16[:, u, :], xn[:, u, :], ROUND, QMAX, ALU.subtract, ALU.min)\
                        .then_inc(v5, 1)

                steps(dve, NT, [(share, 3), (shift, 2), (keys, 0), (values, 0)])
                dve.wait_ge(p5, NT)
                nc.vector.tensor_reduce(peak[:, P_:P_ + 1], pall.rearrange("p n e -> p (n e)"), AX.X, ALU.max)\
                    .then_inc(am5, 1)
                scales(dve, pr5, sc5, P_, P_ + 1)
                nc.vector.tensor_scalar(prod[:, 2:3], qs[:, P_:P_ + 1], qs[:, V_:V_ + 1], None, ALU.mult)\
                    .then_inc(sc5, 1)

            @block.tensor
            def _(pe):
                def score(t, u):
                    pe.wait_ge(q5, t + 1)
                    pe.wait_ge(kbd5, 2 * t + 2)
                    wait(pe, s_sb5, t - 1)
                    for g in range(2):
                        for b in range(IPT):
                            at = g * IPT * EH + b * EH
                            mm = nc.tensor.matmul(bank[u][0:EH, g * P + b * S:g * P + (b + 1) * S],
                                                  kbd16[:, u, at:at + EH], q16[:, u, g, b * S:(b + 1) * S],
                                                  start=True, stop=True)
                    mm.then_inc(s_ps5, 1)

                def turn(t, u):
                    pe.wait_ge(s_sb5, t + 1)
                    wait(pe, sm5, 4 * t - 6)
                    for g in range(2):
                        mm = nc.tensor.transpose(bank[4 + u][:, g * EH:(g + 1) * EH], st5buf[:, u, g, :],
                                                 ident[0:EH, 0:EH])
                    mm.then_inc(sc_ps5, 1)

                steps(pe, NT, [(score, 0), (turn, 1)])

            @block.scalar
            def _(act):
                def keep_s(t, u):
                    act.wait_ge(s_ps5, t + 1)
                    wait(act, sc_ps5, t - 1)
                    nc.scalar.activation(st5buf[:, u, :, :].rearrange("p g t -> p (g t)"), bank[u][0:EH, 0:2 * P],
                                         ACT.Copy).then_inc(s_sb5, 1)

                def exponent(t, u):
                    act.wait_ge(sm5, 4 * t + 2)
                    nc.scalar.activation(scores[:, u, 0:E], scores[:, u, 0:E], ACT.Exp, scale=prod[:, 1:2])\
                        .then_inc(exp5, 1)

                def queries(t, u):
                    nc.scalar.activation(qround[:, u, :, :], qT_v[:, :, ds(t * P, P)], ACT.Identity,
                                         bias=rounding[0:EH, 0:1], scale=qi[0:EH, Q_:Q_ + 1]).then_inc(qr5, 1)
                    act.wait_ge(qr5, t + 1)
                    wait(act, s_ps5, t - 1)
                    nc.scalar.activation(q16[:, u, :, :], qround[:, u, :, :], ACT.Identity,
                                         bias=rounding[0:EH, 1:2]).then_inc(q5, 1)

                steps(act, NT, [(queries, 0), (exponent, 2), (keep_s, 0)])


        pr6, pi6, tr6, pt6, o_ps6, o_sb6, st6, am6, par6, sc6 = (sem(n) for n in (
            "pr6", "pi6", "tr6", "pt6", "o_ps6", "o_sb6", "st6", "am6", "par6", "sc6"))
        v16_loaded = [sem(f"v16_loaded{u}") for u in range(2)]
        vbd16_done = sem("vbd16_done")
        vrep16 = kT[0:EH, 0:IPT * E].bitcast(BF16).rearrange("p (u b e) -> p u b e", u=2, b=IPT)
        CELLS = IPT * EH
        w1_loaded, w2_loaded = sem("w1_loaded"), sem("w2_loaded")

        with nc.Block() as block:
            @block.sync
            def _(sp):
                src = v_scr16.rearrange("(b j) e -> j b e", j=S)

                def load(t, u):
                    wait(sp, vbd16_done, 2 * t - 2)
                    for m in range(HG):
                        sp.dma_start(vrep16[m * S:(m + 1) * S, u, :, :], src[:, ds(t * IPT, IPT), :])\
                            .then_inc(v16_loaded[u], 16)

                steps(sp, NT, [(load, 0)])

            @block.vector
            def _(dve):
                def quantise(t, u):
                    nc.vector.tensor_scalar(xn[:, u, :], pall[:, ds(t, 1), :].rearrange("p a e -> p (a e)"),
                                            qi[:, P_:P_ + 1], ROUND, ALU.mult, ALU.add).then_inc(pr6, 1)
                    dve.wait_ge(pr6, t + 1)
                    wait(dve, tr6, t - 1)
                    nc.vector.tensor_scalar(x16[:, u, 0:E], xn[:, u, :], ROUND, QMAX, ALU.subtract, ALU.min)\
                        .then_inc(pi6, 1)

                def spread_values(t, u):
                    dve.wait_ge(v16_loaded[u], HG * in_slot(t, u))
                    wait(dve, o_ps6, t - 1)
                    shape = [EH, IPT, HG, D]
                    for g in range(2):
                        nc.vector.tensor_tensor(
                            vbd16[:, u, g * CELLS:(g + 1) * CELLS].rearrange("p (b m d) -> p b m d", b=IPT, m=HG),
                            vrep16[:, u, :, g * EH:(g + 1) * EH].rearrange("p b (m d) -> p b m d", m=HG),
                            hmask16[:, :].unsqueeze(1).unsqueeze(3).broadcast_to(shape), ALU.mult)\
                            .then_inc(vbd16_done, 1)

                def range_of(t, u):
                    dve.wait_ge(o_sb6, t + 1)
                    absmax(stats[0:EH, O_, ds(t, 1)], oT_v[:, :, ds(t * P, P)]).then_inc(st6, 1)

                steps(dve, NT, [(range_of, 2), (quantise, 0), (spread_values, 0)])
                dve.wait_ge(st6, NT)
                nc.vector.tensor_reduce(peak[:, O_:O_ + 1], stats[:, O_, :], AX.X, ALU.max).then_inc(am6, 1)
                scales(dve, par6, sc6, O_, O_ + 1)
                nc.vector.tensor_scalar(prod[:, 3:4], qs[:, O_:O_ + 1], qs[:, WP_:WP_ + 1], None, ALU.mult)\
                    .then_inc(sc6, 1)

            @block.gpsimd
            def _(pool):
                pool.wait_ge(am6, 1)
                nc.gpsimd.partition_all_reduce(peaks[:, O_:O_ + 1], peak[:, O_:O_ + 1], P, RMAX).then_inc(par6, 1)

            @block.tensor
            def _(pe):
                def turn(t, u):
                    pe.wait_ge(pi6, t + 1)
                    wait(pe, pt6, t - 1)
                    for c in range(2):
                        mm = nc.tensor.transpose(bank[u][0:EH, c * P // 2:(c + 1) * P // 2].bitcast(BF16),
                                                 x16[:, u, c * EH:(c + 1) * EH], ident16[:, :])
                    mm.then_inc(tr6, 1)

                def attend(t, u):
                    pe.wait_ge(vbd16_done, 2 * t + 2)
                    pe.wait_ge(pt6, t + 1)
                    wait(pe, o_sb6, t - 1)
                    for g in range(2):
                        for b in range(IPT):
                            at = g * CELLS + b * EH
                            mm = nc.tensor.matmul(bank[2 + u][0:EH, g * P + b * S:g * P + (b + 1) * S],
                                                  vbd16[:, u, at:at + EH],
                                                  xt16[:, u, g * P + b * S:g * P + (b + 1) * S],
                                                  start=True, stop=True)
                    mm.then_inc(o_ps6, 1)

                steps(pe, NT, [(attend, 1), (turn, 0)])

            @block.scalar
            def _(act):
                for e in range(NE1):
                    act.dma_start(w2_all[:, e, :, :].rearrange("p c n -> p (c n)"), a["L1_ffn_W2"][e, :, :])\
                        .then_inc(w2_loaded, 16)

                def keep_p(t, u):
                    act.wait_ge(tr6, t + 1)
                    wait(act, o_ps6, t - 1)
                    nc.scalar.activation(xt16[:, u, 0:2 * P], bank[u][0:EH, 0:P].bitcast(BF16), ACT.Copy)\
                        .then_inc(pt6, 1)

                def keep_o(t, u):
                    act.wait_ge(o_ps6, t + 1)
                    nc.scalar.activation(oT_v[:, :, ds(t * P, P)],
                                         bank[2 + u][0:EH, 0:2 * P].rearrange("p (g t) -> p g t", g=2),
                                         ACT.Copy, scale=prod[0:EH, 2:3]).then_inc(o_sb6, 1)

                steps(act, NT, [(keep_o, 1), (keep_p, 0)])

        or7, oi7, w_ps7, h7 = (sem(n) for n in ("or7", "oi7", "w_ps7", "h7"))
        tail7 = tail_sems("7")

        with nc.Block() as block:
            @block.vector
            def _(dve):
                def quantise(t, u):
                    nc.vector.tensor_scalar(ot[:, u, :, :], oT_v[:, :, ds(t * P, P)], qi[0:EH, O_:O_ + 1], ROUND,
                                            ALU.mult, ALU.add).then_inc(or7, 1)
                    dve.wait_ge(or7, t + 1)
                    wait(dve, w_ps7, t - 1)
                    nc.vector.tensor_scalar(x16[0:EH, u, 0:2 * P], ot[:, u, :, :].rearrange("p g t -> p (g t)"),
                                            ROUND, QMAX, ALU.subtract, ALU.min).then_inc(oi7, 1)

                def residual(t, u):
                    tile = h[:, ds(t, 1), :].rearrange("p a e -> p (a e)")
                    dve.wait_ge(w_ps7, t + 1)
                    nc.vector.scalar_tensor_tensor(tile, bank[2 + u][:, 0:E], prod[:, 3:4], tile, ALU.mult, ALU.add)\
                        .then_inc(h7, 1)
                    dve.wait_ge(h7, 2 * t + 1)
                    nc.vector.tensor_tensor(tile, tile, bproj[:, :], ALU.add).then_inc(h7, 1)
                    moments_of(dve, t, u, tail7["moments"], h7, 2 * t + 2)

                norm, keep_gate = tail_on_dve(dve, tail7)
                steps(dve, NT, [(keep_gate, 4), (norm, 2), (quantise, 0), (residual, 1)])

            @block.tensor
            def _(pe):
                def project(t, u):
                    pe.wait_ge(oi7, t + 1)
                    wait(pe, h7, 2 * t - 2)
                    for g in range(2):
                        mm = nc.tensor.matmul(bank[2 + u][:, 0:E], x16[0:EH, u, g * P:(g + 1) * P], wproj16[:, g, :],
                                              start=(g == 0), stop=(g == 1))
                    mm.then_inc(w_ps7, 1)

                turn, gate = tail_on_pe(pe, tail7, gate1)
                steps(pe, NT, [(gate, 4), (turn, 3), (project, 1)])

            @block.scalar
            def _(act):
                copy_x, deviation = tail_on_act(act, tail7)
                steps(act, NT, [(copy_x, 3), (deviation, 1)])

            @block.gpsimd
            def _(pool):
                def keep_rows(t, u):
                    pool.wait_ge(tail7["xn"], t + 1)
                    nc.gpsimd.tensor_copy(xall[:, ds(t, 1), :].rearrange("p a e -> p (a e)"), xn[:, u, :])\
                        .then_inc(tail7["gathered"], 1)

                steps(pool, NT, [(keep_rows, 0)])

            @block.sync
            def _(sp):
                for e in range(NE1):
                    sp.dma_start(w1_all[0:EH, e, :, :].rearrange("p c f -> p (c f)"), a["L1_ffn_W1"][e, :, :])\
                        .then_inc(w1_loaded, 16)
                sp.dma_start(w1_all[EH:EH + 1, :, 1, :], a["L1_ffn_b1"]).then_inc(w1_loaded, 16)

        cc8, chosen8, prefix8, places, scattered = (sem(n) for n in (
            "cc8", "chosen8", "prefix8", "places", "scattered"))
        r8, exp8, comb8, ct_ps8, ct_sb8, b_ps8, b_sb8 = (sem(n) for n in (
            "r8", "exp8", "comb8", "ct_ps8", "ct_sb8", "b_ps8", "b_sb8"))

        with nc.Block() as block:
            @block.vector
            def _(dve):
                count = [0]

                def link(ins):
                    count[0] += 1
                    ins.then_inc(r8, 1)
                    dve.wait_ge(r8, count[0])

                e, chosen, rank = rt
                shape8 = [P, NT, NE1]
                link(nc.vector.tensor_reduce(small[:, :, 0], logits[:, :, :], AX.X, ALU.max))
                link(nc.vector.tensor_tensor(e[:, :, :], logits[:, :, :], small[:, :, 0:1].broadcast_to(shape8),
                                             ALU.subtract))
                ranks(link, logits[:, :, :], NE1, lower8[:, :], rank[:, :, :])
                dve.wait_ge(exp8, 1)
                link(nc.vector.tensor_scalar(chosen16[:, :].rearrange("p (t e) -> p t e", t=NT), rank[:, :, :], 2.0,
                                             None, ALU.is_lt))
                nc.vector.tensor_copy(small[:, 0, 0:1], small[:, 0, 0:1]).then_inc(chosen8, 1)
                link(nc.vector.scalar_tensor_tensor(e[:, :, :], rank[:, :, :], 2.0, e[:, :, :],
                                                    ALU.is_lt, ALU.mult))
                link(nc.vector.tensor_reduce(small[:, :, 0], e[:, :, :], AX.X, ALU.add))
                link(nc.vector.reciprocal(small[:, :, 1], small[:, :, 0]))
                link(nc.vector.tensor_tensor(comb[:, :, 0:NE1], e[:, :, :], small[:, :, 1:2].broadcast_to(shape8),
                                             ALU.mult))
                nc.vector.tensor_copy(small[:, 0, 0:1], small[:, 0, 0:1]).then_inc(comb8, 1)
                for k in range(2):
                    link(nc.vector.tensor_scalar(first[:, k, :, :], rank[:, :, :], float(k), None, ALU.is_equal))
                    link(nc.vector.tensor_tensor(chosen[:, :, :], first[:, k, :, :], comb[:, :, 0:NE1], ALU.mult))
                    link(nc.vector.tensor_reduce(weight[:, k, :], chosen[:, :, :], AX.X, ALU.add))
                count_e, tiles_e, before_e, end_e = (load_e[:, n, :] for n in range(4))
                dve.wait_ge(prefix8, 2)
                link(nc.vector.tensor_reduce(count_e, bank[5][:, 0:NT * NE1].rearrange("p (t e) -> p e t", t=NT),
                                             AX.X, ALU.add))
                link(nc.vector.tensor_scalar(tiles_e, count_e, P / 2 - 0.5, 1.0 / P, ALU.add, ALU.mult))
                link(nc.vector.tensor_scalar(tiles_e, tiles_e, ROUND, None, ALU.add))
                link(nc.vector.tensor_scalar(tiles_e, tiles_e, ROUND, None, ALU.subtract))
                square = pairs[:, 0:NE1 * NE1].rearrange("p (a b) -> p a b", a=NE1)
                link(nc.vector.tensor_tensor(square, lower8[:, :].rearrange("p (a b) -> p a b", a=NE1),
                                             tiles_e.unsqueeze(1).broadcast_to([P, NE1, NE1]), ALU.mult))
                link(nc.vector.tensor_reduce(before_e, square, AX.X, ALU.add))
                link(nc.vector.tensor_tensor(end_e, before_e, tiles_e, ALU.add))
                link(nc.vector.tensor_scalar(before_e, before_e, float(P), None, ALU.mult))
                link(nc.vector.tensor_tensor(rank[:, :, :], bank[4][:, 0:NT * NE1].rearrange("p (t e) -> p t e", t=NT),
                                             before_e.unsqueeze(1).broadcast_to(shape8), ALU.add))
                for k in range(2):
                    link(nc.vector.tensor_tensor(chosen[:, :, :], first[:, k, :, :], rank[:, :, :], ALU.mult))
                    link(nc.vector.tensor_reduce(place[:, k, :], chosen[:, :, :], AX.X, ALU.add))
                nc.vector.tensor_copy(place_i[:, :, :], place[:, :, :]).then_inc(places, 1)
                over = pairs[:, 0:SLOT_TILES * NE1].rearrange("p (n e) -> p n e", e=NE1)
                grid = [P, SLOT_TILES, NE1]
                link(nc.vector.tensor_tensor(over, end_e.unsqueeze(1).broadcast_to(grid),
                                             slot_no[:, :].unsqueeze(2).broadcast_to(grid), ALU.is_le))
                link(nc.vector.tensor_reduce(of_tile[:, :], over, AX.X, ALU.add))
                link(nc.vector.tensor_scalar(of_tile[:, :], of_tile[:, :], NE1 - 1.0, None, ALU.min))
                link(nc.vector.tensor_copy(of_tile_i[:, :], of_tile[:, :]))

                def add(t, u):
                    tile = h[:, ds(t, 1), :].rearrange("p a e -> p (a e)")
                    dve.wait_ge(b_ps8, t + 1)
                    nc.vector.tensor_tensor(tile, bank[2 + u][:, 0:E], tile, ALU.add).then_inc(b_sb8, 1)

                steps(dve, NT, [(add, 0)])

            @block.scalar
            def _(act):
                act.wait_ge(r8, 2)
                nc.scalar.activation(rt[0][:, :, :], rt[0][:, :, :], ACT.Exp).then_inc(exp8, 1)

                def keep(t, u):
                    act.wait_ge(ct_ps8, t + 1)
                    wait(act, b_ps8, t - 1)
                    nc.scalar.activation(combT[:, u, :], bank[u][0:NE1, 0:P], ACT.Copy).then_inc(ct_sb8, 1)

                steps(act, NT, [(keep, 0)])

            @block.tensor
            def _(pe):
                pe.wait_ge(chosen8, 1)
                for d in range(1, NT):
                    nc.tensor.matmul(bank[4][:, d * NE1:NT * NE1], ones16[:, :], chosen16[:, 0:(NT - d) * NE1],
                                     start=(d == 1), stop=False, skip_group_check=True)
                nc.tensor.matmul(bank[4][:, 0:NT * NE1], upper16[:, :], chosen16[:, :], start=False, stop=True,
                                 skip_group_check=True).then_inc(prefix8, 1)
                nc.tensor.matmul(bank[5][:, 0:NT * NE1], ones16[:, :], chosen16[:, :], start=True, stop=True)\
                    .then_inc(prefix8, 1)

                def turn(t, u):
                    pe.wait_ge(cc8, t + 1)
                    wait(pe, ct_sb8, t - 1)
                    nc.tensor.matmul(bank[u][0:NE1, 0:P], combc[:, u, :], ident[:, :], start=True, stop=True)\
                        .then_inc(ct_ps8, 1)

                def bias(t, u):
                    pe.wait_ge(ct_sb8, t + 1)
                    wait(pe, b_sb8, t - 1)
                    nc.tensor.matmul(bank[2 + u][:, 0:E], combT[:, u, :], b2r[:, :], start=True, stop=True)\
                        .then_inc(b_ps8, 1)

                steps(pe, NT, [(turn, 0), (bias, 1)])

            @block.gpsimd
            def _(pool):
                pool.wait_ge(comb8, 1)

                def fetch(t, u):
                    wait(pool, ct_ps8, t - 1)
                    nc.gpsimd.tensor_copy(combc[:, u, :], comb[:, ds(t, 1), 0:NE1].rearrange("p a e -> p (a e)"))\
                        .then_inc(cc8, 1)

                steps(pool, NT, [(fetch, 0)])
                pool.wait_ge(places, 1)
                for t in range(NT):
                    for k in range(2):
                        pool.indirect_dma_start(
                            out=x_slots, out_offset=bass.IndirectOffsetOnAxis(ap=place_i[:, k, t:t + 1], axis=0),
                            in_=xall[:, t, :], in_offset=None).then_inc(scattered, 16)
                pool.wait_ge(scattered, 16 * 2 * NT)

        xs_loaded = [sem(f"xs_loaded{u}") for u in range(2)]
        y_stored = [sem(f"y_stored{u}") for u in range(2)]
        ones_row, tr9, xt9, up9, ra9, rd9, turn9, ta9, td9, y9, yc9 = (sem(n) for n in (
            "ones_row", "tr9", "xt9", "up9", "ra9", "rd9", "turn9", "ta9", "td9", "y9", "yc9"))
        FH = FF // 2

        with nc.Block() as block:
            @block.sync
            def _(sp):
                def load(t, u):
                    wait(sp, tr9, t - 1)
                    sp.dma_start(xs[:, u, :], x_slots[ds(t * P, P), :]).then_inc(xs_loaded[u], 16)

                def store(t, u):
                    sp.wait_ge(yc9, t + 1)
                    sp.dma_start(y_slots[ds(t * P, P), :], y_out[:, u, :]).then_inc(y_stored[u], 16)

                steps(sp, SLOT_TILES, [(store, 5), (load, 0)])
                for u in range(2):
                    sp.wait_ge(y_stored[u], 8 * SLOT_TILES)

            @block.gpsimd
            def _(pool):
                for u in range(2):
                    nc.gpsimd.memset(xsT[EH:EH + 1, u, :, :], 1.0).then_inc(ones_row, 1)

            @block.tensor
            def _(pe):
                pe.wait_ge(w1_loaded, 16 * (NE1 + 1))
                pe.wait_ge(w2_loaded, 16 * NE1)
                pe.wait_ge(ones_row, 2)

                def turn_x(t, u):
                    pe.wait_ge(xs_loaded[u], in_slot(t, u))
                    wait(pe, xt9, t - 1)
                    for c in range(2):
                        mm = nc.tensor.transpose(bank[4 + u][0:EH, c * P:(c + 1) * P],
                                                 xs[:, u, c * EH:(c + 1) * EH], ident[:, :])
                    mm.then_inc(tr9, 1)

                def up(t, u):
                    expert = pe.value_load(of_tile_i[0:1, ds(t, 1)], min_val=0, max_val=NE1 - 1)
                    wait_alone(pe, xt9, t + 1, passed)
                    for half in range(2):
                        wait(pe, (ra9, rd9)[half], t)
                        for c in range(2):
                            rows = EH + c
                            mm = nc.tensor.matmul(
                                bank[half][:, 0:FH], xsT[0:rows, u, c, :],
                                w1_all[0:rows, ds(expert, 1), c, half * FH:(half + 1) * FH]
                                .rearrange("p a f -> p (a f)"), start=(c == 0), stop=(c == 1))
                        mm.then_inc(up9, 1)

                def turn_h(t, u):
                    for half in range(2):
                        pe.wait_ge((ra9, rd9)[half], t + 1)
                        wait(pe, (ta9, td9)[half], t)
                        for c in range(FC // 2):
                            at = half * FH + c * P
                            mm = nc.tensor.transpose(bank[2 + half][:, c * P:(c + 1) * P],
                                                     hidden[:, u, at:at + P], ident[:, :])
                        mm.then_inc(turn9, 1)

                def down(t, u):
                    expert = pe.value_load(of_tile_i[0:1, ds(t, 1)], min_val=0, max_val=NE1 - 1)
                    wait_alone(pe, ta9, t + 1, passed)
                    wait_alone(pe, td9, t + 1, passed)
                    wait_alone(pe, yc9, t - 1, passed)
                    for c in range(FC):
                        mm = nc.tensor.matmul(bank[6 + u][:, 0:E], hiddenT[:, u, c * P:(c + 1) * P],
                                              w2_all[:, ds(expert, 1), c, :].rearrange("p a n -> p (a n)"),
                                              start=(c == 0), stop=(c == FC - 1))
                    mm.then_inc(y9, 1)

                steps(pe, SLOT_TILES, [(down, 4), (turn_h, 3), (up, 2), (turn_x, 1)])

            @block.scalar
            def _(act):
                def copy_x(t, u):
                    act.wait_ge(tr9, t + 1)
                    wait(act, up9, 2 * t - 2)
                    nc.scalar.activation(xsT[0:EH, u, :, :].rearrange("p c t -> p (c t)"), bank[4 + u][0:EH, 0:2 * P],
                                         ACT.Copy).then_inc(xt9, 1)

                def relu(t, u):
                    act.wait_ge(up9, 2 * t + 1)
                    wait(act, turn9, 2 * t - 2)
                    nc.scalar.activation(hidden[:, u, 0:FH], bank[0][:, 0:FH], ACT.Relu).then_inc(ra9, 1)

                def keep(t, u):
                    act.wait_ge(turn9, 2 * t + 1)
                    wait(act, y9, t - 1)
                    nc.scalar.activation(hiddenT[:, u, 0:FH], bank[2][:, 0:FH], ACT.Copy).then_inc(ta9, 1)

                steps(act, SLOT_TILES, [(keep, 3), (relu, 2), (copy_x, 1)])

            @block.vector
            def _(dve):
                def relu(t, u):
                    dve.wait_ge(up9, 2 * t + 2)
                    wait(dve, turn9, 2 * t - 2)
                    nc.vector.tensor_scalar(hidden[:, u, FH:FF], bank[1][:, 0:FH], 0.0, None, ALU.max)\
                        .then_inc(rd9, 1)

                def keep(t, u):
                    dve.wait_ge(turn9, 2 * t + 2)
                    wait(dve, y9, t - 1)
                    nc.vector.tensor_copy(hiddenT[:, u, FH:FF], bank[3][:, 0:FH]).then_inc(td9, 1)

                def output(t, u):
                    dve.wait_ge(y9, t + 1)
                    wait(dve, y_stored[u], in_slot(t, u) - 16)
                    nc.vector.tensor_copy(y_out[:, u, :], bank[6 + u][:, 0:E]).then_inc(yc9, 1)

                steps(dve, SLOT_TILES, [(output, 4), (keep, 3), (relu, 2)])

        fetched = [sem(f"fetched{b}") for b in range(NB)]
        sum10, out10, stored = sem("sum10"), sem("out10"), sem("stored")

        with nc.Block() as block:
            @block.gpsimd
            def _(pool):
                for t in range(NT):
                    for k in range(2):
                        pool.indirect_dma_start(
                            out=y_in[:, k, t, :], out_offset=None, in_=y_slots,
                            in_offset=bass.IndirectOffsetOnAxis(ap=place_i[:, k, t:t + 1], axis=0))\
                            .then_inc(fetched[t // TPB], 16)

            @block.vector
            def _(dve):
                for t in range(NT):
                    dve.wait_ge(fetched[t // TPB], 16 * 2 * TPB)
                    nc.vector.scalar_tensor_tensor(h[:, t, :], y_in[:, 0, t, :], weight[:, 0, t:t + 1], h[:, t, :],
                                                   ALU.mult, ALU.add).then_inc(sum10, 1)
                    dve.wait_ge(sum10, t + 1)
                    nc.vector.scalar_tensor_tensor(h[:, t, :], y_in[:, 1, t, :], weight[:, 1, t:t + 1], h[:, t, :],
                                                   ALU.mult, ALU.add).then_inc(out10, 1)

            @block.sync
            def _(sp):
                out_v = out.rearrange("(n p) e -> p n e", p=P)
                for b in range(NB):
                    sp.wait_ge(out10, TPB * (b + 1))
                    sp.dma_start(out_v[:, b * TPB:(b + 1) * TPB, :], h[:, b * TPB:(b + 1) * TPB, :])\
                        .then_inc(stored, 16)
                sp.wait_ge(stored, 16 * NB)


def kernel(**inputs):
    import numpy as np
    import concourse.bacc as bacc
    from concourse import mybir as mb
    from concourse.bass_utils import run_bass_kernel_spmd

    i = {k: np.asarray(v) for k, v in inputs.items()}

    def rows(w):
        return w.reshape(2, EH, -1).transpose(1, 0, 2)

    def column(b):
        return b.reshape(-1, EH).T

    x = i["x"].reshape(IMAGES, CHANS, 4, PATCH, 4, PATCH).transpose(1, 3, 5, 0, 2, 4)
    x = x.reshape(KC, P, NT, P).transpose(2, 1, 0, 3).reshape(NT, P, KC * P)
    near = i["L0_attn_rel_table"][P - 1 - (S - 1):P - 1 + S]
    up = np.stack([np.concatenate([i["L0_ffn_" + w], i["L0_ffn_s" + w][None]]) for w in ("w1", "w3")])
    down = np.concatenate([i["L0_ffn_w2"], i["L0_ffn_sw2"][None]])
    p = np.arange(P)
    arrays = {
        "x": x,
        "L0_tok_pinv": i["L0_tok_pinv"].T.reshape(OC, P, PATCH * PATCH).transpose(1, 0, 2),
        "L0_tok_proj_weight": i["L0_tok_proj_weight"].reshape(E, CHANS, OC, P).transpose(3, 2, 1, 0)
        .reshape(P, OC, CHANS * E),
        "rel": rows(near.T), "rel_reversed": rows(near[::-1].T),
        "L0_attn_columns": np.stack([column(i["L0_attn_b" + n]) for n in ("q", "k", "pk", "pq")], 1),
        "L1_attn_columns": np.stack([column(i["L1_attn_b_qkv"][n * E:(n + 1) * E]) for n in range(2)], 1),
        "L1_attn_b_v": i["L1_attn_b_qkv"][2 * E:],
        "L0_ffn_gate_weight": rows(i["L0_ffn_gate_weight"].T), "L1_ffn_Wr": rows(i["L1_ffn_Wr"]),
        "L0_ffn_w13": up.reshape(2, NE0 + 1, INTER, 2, EH).transpose(4, 0, 1, 3, 2),
        "L0_ffn_w2": down.transpose(2, 0, 1),
        "L1_attn_w_qkv": rows(i["L1_attn_w_qkv"]), "L1_attn_w_proj": rows(i["L1_attn_w_proj"]),
        "L1_ffn_W1": i["L1_ffn_W1"].reshape(NE1, 2, EH, FF).transpose(0, 2, 1, 3).reshape(NE1, EH, 2 * FF),
        "L1_ffn_W2": i["L1_ffn_W2"].reshape(NE1, FC, P, E).transpose(0, 2, 1, 3).reshape(NE1, P, FC * E),
        "L1_ffn_b1": i["L1_ffn_b1"][None], "L1_ffn_b2": i["L1_ffn_b2"],
        "upper": np.triu(np.ones((P, P), np.float32), 1),
        "slot_numbers": np.broadcast_to(np.arange(SLOT_TILES, dtype=np.float32), (P, SLOT_TILES)),
        "ident": np.eye(P, dtype=np.float32),
        "hmask": np.equal(np.arange(EH)[:, None] // D, np.arange(HG)[None]).astype(np.float32),
        "lower4": np.broadcast_to(np.tril(np.ones((GROUPS, GROUPS), np.float32), -1).reshape(1, -1), (P, GROUPS ** 2)),
        "lower8": np.broadcast_to(np.tril(np.ones((NE0, NE0), np.float32), -1).reshape(1, -1), (P, NE0 ** 2)),
    }
    for n in ("Wq", "Wk", "Wv", "Wo", "Wpk", "Wpq"):
        arrays["L0_attn_" + n] = rows(i["L0_attn_" + n])
    for n in ("L0_tok_proj_bias", "L0_attn_bv", "L0_attn_bo", "L1_attn_b_proj", "L0_ffn_gate_bias"):
        arrays[n] = i[n]
    arrays = {k: np.ascontiguousarray(v) for k, v in arrays.items()}

    nc = bacc.Bacc("TRN2", target_bir_lowering=False, num_devices=1)
    aps = {k: nc.dram_tensor("in_" + k, v.shape, mb.dt.from_np(v.dtype), kind="ExternalInput").ap()
           for k, v in arrays.items()}
    out = nc.dram_tensor("out", (T, E), mb.dt.float32, kind="ExternalOutput").ap()
    tower(nc, aps, out)
    r = run_bass_kernel_spmd(nc, [{"in_" + k: v for k, v in arrays.items()}], core_ids=[0])
    return r.results[0]["out"].reshape(IMAGES, S, E)
```

```python
from contextlib import ExitStack

import concourse.bass as bass
from concourse import mybir

F32 = mybir.dt.float32
BF16 = mybir.dt.bfloat16
ALU = mybir.AluOpType
ACT = mybir.ActivationFunctionType
AX = mybir.AxisListType
RMAX = bass.bass_isa.ReduceOp.max

P = 128
IMAGES, CHANS, SIDE, PATCH, OLD = 128, 3, 64, 16, 32
S = (SIDE // PATCH) ** 2
T = IMAGES * S
NT = T // P
IPT = P // S
BLK = 512
NB = T // BLK
TPB = BLK // P
E = 192
EH = E // 2
H, D = 12, 16
HG = H // 2
KC = CHANS * PATCH * PATCH // P
OC = OLD * OLD // P
REL = 2 * S - 1
NE0, INTER = 8, 128
GROUPS = 4
NE1, FF = 8, 768
FC = FF // P
SLOT_TILES = (2 * T + NE1 * (P - 1)) // P
SLOT_TILES += SLOT_TILES % 2
EPS = 1e-5
SOFT0 = 1.0 / (3.0 * D) ** 0.5
SOFT1 = D ** -0.5
QMAX = 127.0
ROUND = 1.5 * 2.0 ** 23


def ds(start, size):
    return bass.ds(start, size)


def wait(eng, semaphore, count):
    if isinstance(count, int) and count <= 0:
        return
    eng.wait_ge(semaphore, count)


def wait_alone(eng, semaphore, count, passed):
    wait(eng, semaphore, count)
    if not isinstance(count, int):
        eng.sem_inc(passed, 1)


def in_slot(t, u):
    return 8 * (t - u) + 16


def steps(eng, n, stages):
    deepest = max(lag for _, lag in stages)
    head = deepest + 2 + deepest % 2

    def fixed(s):
        for stage, lag in stages:
            if 0 <= s - lag < n:
                stage(s - lag, (s - lag) % 2)

    for s in range(head):
        fixed(s)
    with eng.Fori(head, n - 1, 2) as s0:
        for v in range(2):
            for stage, lag in stages:
                stage(s0 + (v - lag), (v - lag) % 2)
    for s in range(n, n + deepest):
        fixed(s)


def tower(nc, a, out):
    ctx = ExitStack()
    with ctx:
        def sb(name, shape, dt=F32):
            return ctx.enter_context(nc.sbuf_tensor(name, shape, dt))

        early = ctx.enter_context(ExitStack())
        early_sems = []

        def sem(name):
            return ctx.enter_context(nc.semaphore(name))

        def early_sem(name):
            early_sems.append(early.enter_context(nc.semaphore(name)))
            return early_sems[-1]

        h = sb("h", [P, NT, E])
        xnT = sb("xnT", [P, 2 * T])
        qks = sb("qks", [P, 3 * 2 * T])
        qT, kT, sT = (qks[:, n * 2 * T:(n + 1) * 2 * T] for n in range(3))
        big = sb("big", [P, 2 * T + NT * (E + 1)])
        ident = sb("ident", [P, P])
        ident16 = sb("ident16", [P, P], BF16)
        hmask = sb("hmask", [EH, HG])
        hmask16 = sb("hmask16", [EH, HG], BF16)
        lower4 = sb("lower4", [P, GROUPS * GROUPS])
        lower8 = sb("lower8", [P, 64])
        upper = sb("upper", [P, P])
        upper16 = sb("upper16", [P, P], BF16)
        ones16 = sb("ones16", [P, P], BF16)
        slot_no = sb("slot_no", [P, SLOT_TILES])
        token_no = sb("token_no", [P, NT])
        rows_of = sb("rows_of", [P, SLOT_TILES])
        row_i = sb("row_i", [P, 2], mybir.dt.uint32)
        chosen16 = sb("chosen16", [P, NT * NE1], BF16)
        first = sb("first", [P, 2, NT, NE1])
        weight = sb("weight", [P, 2, NT])
        place = sb("place", [P, 2, NT])
        place_i = sb("place_i", [P, 2, NT], mybir.dt.uint32)
        load_e = sb("load_e", [P, 4, NE1])
        of_tile = sb("of_tile", [P, SLOT_TILES])
        of_tile_i = sb("of_tile_i", [P, SLOT_TILES], mybir.dt.int32)
        tokb = sb("tokb", [P, E])
        wtok = sb("wtok", [P, KC, E])
        wq = sb("wq", [EH, 2, E])
        wk = sb("wk", [EH, 2, E])
        wv = sb("wv", [EH, 2, E])
        wo = sb("wo", [EH, 2, E])
        wpk = sb("wpk", [EH, 2, E])
        wpq = sb("wpq", [EH, 2, E])
        relr = sb("relr", [EH, 2, REL])
        relf = sb("relf", [EH, 2, REL])
        colb = sb("colb", [EH, 4, 2])
        bv = sb("bv", [P, E])
        bo = sb("bo", [P, E])
        bproj = sb("bproj", [P, E])
        bv1 = sb("bv1", [P, E])
        bqk1 = sb("bqk1", [EH, 2, 2])
        gate0 = sb("gate0", [EH, 2, NE0])
        gate1 = sb("gate1", [EH, 2, NE1])
        gbias = sb("gbias", [P, NE0])
        W13, W2 = 2 * (NE0 + 1) * 2 * INTER, (NE0 + 1) * E
        weights = sb("weights", [P, W13 + W2 + 4 * IPT * EH])
        w13 = weights[0:EH, 0:W13].rearrange("p (w e c i) -> p w e c i", w=2, e=NE0 + 1, c=2)
        w2 = weights[:, W13:W13 + W2].rearrange("p (e n) -> p e n", e=NE0 + 1)
        b2r = sb("b2r", [NE1, E])
        pkbd = sb("pkbd", [EH, 2, HG, REL])
        pqbd = sb("pqbd", [EH, 2, HG, REL])
        pos = sb("pos", [EH, 2, 2, REL])
        eps = sb("eps", [P, 1])
        rounding = sb("rounding", [P, 2])
        moments = sb("moments", [P, 2, 6])
        meanvar = sb("meanvar", [P, 2, 2])
        all_moments = sb("all_moments", [P, NT, 6])
        meanvars = sb("meanvars", [P, NT, 2])
        sdevs = sb("sdevs", [P, 2, NT])
        sdev = sb("sdev", [P, 2])
        rstd = sb("rstd", [P, 2])
        xn = sb("xn", [P, 2, E])
        xt = sb("xt", [EH, 2, 2, P])
        vt = sb("vt", [P, 2, E])
        kbd = weights[0:EH, W13 + W2:].rearrange("p (u g k) -> p u g k", u=2, g=2)
        vbd = sb("vbd", [EH, 2, 2, IPT, EH])
        st1 = sb("st1", [EH, 2, 2, P])
        ot = sb("ot", [EH, 2, 2, P])
        scores = sb("scores", [P, 2, 2 * E])
        top = sb("top", [P, 2, 2 * H])
        mass = sb("mass", [P, 2, 2 * H])
        logits = sb("logits", [P, NT, NE0])
        comb = sb("comb", [P, NT, NE0 + 1])
        rt = [sb(f"rt{i}", [P, NT, NE0]) for i in range(3)]
        small = sb("small", [P, NT, 2])
        v16 = sb("v16", [P, 2, E], BF16)
        combc = sb("combc", [P, 2, NE1])
        combT = sb("combT", [NE1, 2, P])
        stats = sb("stats", [P, 8, NT])
        peak = sb("peak", [P, 8])
        peaks = sb("peaks", [P, 8])
        qs = sb("qs", [P, 8])
        qi = sb("qi", [P, 8])
        prod = sb("prod", [P, 4])
        bank = [ctx.enter_context(nc.psum_tensor(f"bank{i}", [P, 512], F32)) for i in range(8)]

        def halves(buf, width=T):
            return buf[0:EH, :].rearrange("p (g t) -> p g t", g=2)

        xnT_v = halves(xnT)
        qT_v, kT_v, sT_v = halves(qT), halves(kT), halves(sT)
        pinv_v = big[:, 0:OC * 256].rearrange("p (o k) -> p o k", o=OC)
        pw_v = big[:, OC * 256:OC * 256 + OC * CHANS * E].rearrange("p (o k) -> p o k", o=OC)
        pT_v = big[0:EH, 0:2 * T].rearrange("p (g t) -> p g t", g=2)
        t2 = big[:, 2 * T:2 * T + S * E].rearrange("p (i k) -> p i k", i=S)
        xall = t2
        rows_x = big[:, 2 * T:2 * T + NT * (E + 1)].rearrange("p (n c) -> p n c", n=NT)
        vall = sT[:, 0:NT * E].rearrange("p (n e) -> p n e", n=NT)
        q16 = xnT[0:EH, 0:2 * P].bitcast(BF16).rearrange("p (u g t) -> p u g t", u=2, g=2)
        k16 = xnT[0:EH, 2 * P:4 * P].bitcast(BF16).rearrange("p (u g t) -> p u g t", u=2, g=2)
        wqkv32 = big[0:EH, 0:6 * E].rearrange("p (c n) -> p c n", c=2)
        wproj32 = big[0:EH, 6 * E:8 * E].rearrange("p (c n) -> p c n", c=2)
        wqkv16 = big[0:EH, 8 * E:11 * E].bitcast(BF16).rearrange("p (c n) -> p c n", c=2)
        wproj16 = big[0:EH, 11 * E:12 * E].bitcast(BF16).rearrange("p (c n) -> p c n", c=2)
        wround = big[0:EH, 12 * E:18 * E].rearrange("p (c n) -> p c n", c=2)
        w1_all = qks[0:EH + 1, :].rearrange("p (e c f) -> p e c f", e=NE1, c=2)
        w2_all = weights[:, 0:NE1 * FC * E].rearrange("p (e c n) -> p e c n", e=NE1, c=FC)
        hidden = big[:, 0:2 * FF].rearrange("p (u f) -> p u f", u=2)
        hiddenT = big[:, 2 * FF:4 * FF].rearrange("p (u f) -> p u f", u=2)
        y_out = big[:, 4 * FF:4 * FF + 2 * E].rearrange("p (u e) -> p u e", u=2)
        xs = sb("xs", [P, 2, E + 1])
        xsT = big[0:EH + 1, 4 * FF + 2 * E:4 * FF + 2 * E + 4 * P].rearrange("p (u c t) -> p u c t", u=2, c=2)
        y_in = qks[:, 0:2 * NT * E].rearrange("p (k n e) -> p k n e", k=2, n=NT)
        oT_v = xnT_v
        hidden0 = qT[:, 0:3 * 512].rearrange("p (u t) -> p u t", u=3)
        silu0 = qT[:, 3 * 512:6 * 512].rearrange("p (u t) -> p u t", u=3)
        pairs = big[:, 0:NT * 64]
        ties = big[:, NT * 64:2 * NT * 64]
        x16 = scores[:, :, :].bitcast(BF16)
        vbd16 = vbd[:, :, :, :, :].rearrange("p u g b k -> p u (g b k)").bitcast(BF16)
        kbd16 = kbd[:, :, :, :].rearrange("p u g k -> p u (g k)").bitcast(BF16)

        v_scr = nc.dram_tensor("v_scratch", [S, IMAGES, E], F32, kind="Internal").ap()
        x_slots = nc.dram_tensor("x_slots", [SLOT_TILES * P, E + 1], F32, kind="Internal").ap()
        y_rows = nc.dram_tensor("y_rows", [2 * T + SLOT_TILES * P, E], F32, kind="Internal").ap()
        v_scr16 = nc.dram_tensor("v_scratch16", [S, IMAGES, E], BF16, kind="Internal").ap()

        def by_key(scratch, t):
            return scratch[:, ds(t * IPT, IPT), :].rearrange("j b e -> b j e")

        passed = sem("passed")

        def moments_of(dve, t, u, steps_done, written, written_count):
            wait_alone(dve, written, written_count, passed)
            nc.vector.bn_stats(moments[:, u, :], h[:, ds(t, 1), :].rearrange("p a e -> p (a e)"))\
                .then_inc(steps_done, 1)
            wait_alone(dve, steps_done, 2 * t + 1, passed)
            nc.vector.bn_aggr(meanvar[:, u, :], moments[:, u, :]).then_inc(steps_done, 1)

        def sdev_of(act, t, u, steps_done, sdev_ready, inverted):
            act.wait_ge(steps_done, 2 * t + 2)
            wait(act, inverted, t - 1)
            nc.scalar.activation(sdev[:, u:u + 1], meanvar[:, u, 1:2], ACT.Sqrt, bias=eps[:, 0:1])\
                .then_inc(sdev_ready, 1)

        def normalise(dve, t, u, sdev_ready, inverted, xn_ready, dest):
            dve.wait_ge(sdev_ready, t + 1)
            nc.vector.reciprocal(rstd[:, u:u + 1], sdev[:, u:u + 1]).then_inc(inverted, 1)
            dve.wait_ge(inverted, t + 1)
            nc.vector.tensor_scalar(dest, h[:, ds(t, 1), :].rearrange("p a e -> p (a e)"),
                                    meanvar[:, u, 0:1], rstd[:, u:u + 1], ALU.subtract, ALU.mult)\
                .then_inc(xn_ready, 1)

        consts = early_sem("consts")
        x_loaded = [early_sem(f"x_loaded{u}") for u in range(2)]
        tokw = [early_sem(f"tokw{i}") for i in range(4)]
        wtok_ps = early_sem("wtok_ps")
        wtok_done = early_sem("wtok_done")
        pos_ps = early_sem("pos_ps")
        pos_sb = early_sem("pos_sb")
        pos_bd = early_sem("pos_bd")
        cleared = early_sem("cleared")
        LOADS = [(ident, "ident"), (hmask, "hmask"), (lower4, "lower4"), (lower8, "lower8"),
                 (wpk, "L0_attn_Wpk"), (wpq, "L0_attn_Wpq"), (relr, "rel_reversed"), (relf, "rel"),
                 (colb, "L0_attn_columns"), (wq, "L0_attn_Wq"), (wk, "L0_attn_Wk"), (wv, "L0_attn_Wv"),
                 (wo, "L0_attn_Wo"), (gate0, "L0_ffn_gate_weight"), (gate1, "L1_ffn_Wr"),
                 (bqk1, "L1_attn_columns"), (w13, "L0_ffn_w13"), (w2, "L0_ffn_w2"), (upper, "upper"), (slot_no, "slot_numbers"),
                 (token_no, "token_numbers"),
                 (b2r, "L1_ffn_b2")]
        ROWS = [(tokb, "L0_tok_proj_bias"), (bv, "L0_attn_bv"), (bo, "L0_attn_bo"),
                (bproj, "L1_attn_b_proj"), (bv1, "L1_attn_b_v"), (gbias, "L0_ffn_gate_bias")]

        xload = ctx.enter_context(nc.sbuf_tensor("xload", [P, 2, KC * P], F32))

        def load_x(sp, t, u):
            sp.dma_start(xload[:, u, :], a["x"][ds(t, 1), :, :].rearrange("a p k -> p (a k)")).then_inc(x_loaded[u], 16)

        def whole(buf):
            return buf[tuple(slice(None) for _ in buf.shape)]

        with nc.Block() as block:
            @block.sync
            def _(sp):
                pinv_d = a["L0_tok_pinv"]
                pw_d = a["L0_tok_proj_weight"]
                for i in range(4):
                    sp.dma_start(pinv_v[:, 2 * i:2 * i + 2, :], pinv_d[:, 2 * i:2 * i + 2, :]).then_inc(tokw[i], 16)
                    sp.dma_start(pw_v[:, 2 * i:2 * i + 2, :], pw_d[:, 2 * i:2 * i + 2, :]).then_inc(tokw[i], 16)
                for t in range(2):
                    load_x(sp, t, t)

            @block.gpsimd
            def _(pool):
                nc.gpsimd.memset(eps[:, :], EPS).then_inc(cleared, 1)
                nc.gpsimd.memset(ones16[:, :], 1.0).then_inc(cleared, 1)
                nc.gpsimd.memset(rounding[:, 0:1], ROUND).then_inc(cleared, 1)
                nc.gpsimd.memset(rounding[:, 1:2], -ROUND).then_inc(cleared, 1)
                nc.gpsimd.memset(comb[:, :, :], 1.0).then_inc(cleared, 1)
                nc.gpsimd.memset(stats[:, :, :], 0.0).then_inc(cleared, 1)

            @block.scalar
            def _(act):
                for buf, name in LOADS:
                    act.dma_start(whole(buf), a[name]).then_inc(consts, 16)
                for buf, name in ROWS:
                    act.dma_start(buf[:, :], a[name].partition_broadcast(P)).then_inc(consts, 16)
                act.wait_ge(consts, 16 * len(LOADS + ROWS))
                for n in range(4):
                    act.wait_ge(pos_ps, 4)
                    nc.scalar.activation(pos[:, n // 2, n % 2, :], bank[6][0:EH, 32 * n:32 * n + REL],
                                         ACT.Identity, bias=colb[:, 2 + n // 2, n % 2:n % 2 + 1]).then_inc(pos_sb, 1)
                nc.scalar.activation(ident16[:, :], ident[:, :], ACT.Copy).then_inc(pos_sb, 1)
                nc.scalar.activation(hmask16[:, :], hmask[:, :], ACT.Copy).then_inc(pos_sb, 1)
                nc.scalar.activation(upper16[:, :], upper[:, :], ACT.Copy).then_inc(pos_sb, 1)

            @block.tensor
            def _(pe):
                for o in range(OC):
                    if o % 2 == 0:
                        pe.wait_ge(tokw[o // 2], 32)
                    for k in range(KC):
                        c, half = k // 2, k % 2
                        mm = nc.tensor.matmul(bank[k][:, 0:E], pinv_v[:, o, half * P:(half + 1) * P],
                                              pw_v[:, o, c * E:(c + 1) * E], start=(o == 0), stop=(o == OC - 1))
                        if o == OC - 1:
                            mm.then_inc(wtok_ps, 1)
                pe.wait_ge(consts, 16 * len(LOADS + ROWS))
                for n, (w, rel) in enumerate(((wpk, relr), (wpk, relr), (wpq, relf), (wpq, relf))):
                    g = n % 2
                    for c in range(2):
                        mm = nc.tensor.matmul(bank[6][0:EH, 32 * n:32 * n + REL], w[:, c, g * EH:(g + 1) * EH],
                                              rel[:, c, :], start=(c == 0), stop=(c == 1))
                    mm.then_inc(pos_ps, 1)

            @block.vector
            def _(dve):
                for k in range(KC):
                    dve.wait_ge(wtok_ps, k + 1)
                    nc.vector.tensor_copy(wtok[:, k, :], bank[k][:, 0:E]).then_inc(wtok_done, 1)
                for n in range(4):
                    dve.wait_ge(pos_sb, n + 1)
                    dest = (pkbd, pqbd)[n // 2]
                    nc.vector.tensor_tensor(
                        dest[:, n % 2, :, :],
                        pos[:, n // 2, n % 2, :].unsqueeze(1).broadcast_to([EH, HG, REL]),
                        hmask[:, :].unsqueeze(2).broadcast_to([EH, HG, REL]), ALU.mult).then_inc(pos_bd, 1)

        slots_zero, zeros_ready = early_sem("slots_zero"), early_sem("zeros_ready")
        embedded, h_done, ln1, sdev1, inv1, xn1, tr1, xt1 = (early_sem(n) for n in (
            "embedded", "h_done", "ln1", "sdev1", "inv1", "xn1", "tr1", "xt1"))
        qk_ps, v_ps, qk_sb, v_sb, kbd_done, s_ps, s_sb = (early_sem(n) for n in (
            "qk_ps", "v_ps", "qk_sb", "v_sb", "kbd_done", "s_ps", "s_sb"))
        v_stored = [sem(f"v_stored{u}") for u in range(2)]

        with nc.Block() as block:
            @block.sync
            def _(sp):
                def load(t, u):
                    wait(sp, embedded, t - 1)
                    load_x(sp, t, u)

                for t in range(2, 4):
                    load(t, t % 2)
                with sp.Fori(4, NT - 1, 2) as t:
                    for u in range(2):
                        load(t + u, u)

            @block.gpsimd
            def _(pool):
                def store(t, u):
                    pool.wait_ge(v_sb, t + 1)
                    pool.dma_start(by_key(v_scr, t), vt[:, u, :]).then_inc(v_stored[u], 16)

                steps(pool, NT, [(store, 0)])
                for u in range(2):
                    pool.wait_ge(v_stored[u], 8 * NT)

            @block.tensor
            def _(pe):
                def transpose(t, u):
                    pe.wait_ge(xn1, t + 1)
                    wait(pe, xt1, t)
                    for c in range(2):
                        mm = nc.tensor.transpose(bank[2][0:EH, c * P:(c + 1) * P], xn[:, u, c * EH:(c + 1) * EH],
                                                 ident[:, :])
                    mm.then_inc(tr1, 1)

                def embed(t, u):
                    pe.wait_ge(x_loaded[u], in_slot(t, u))
                    wait(pe, h_done, t - 1)
                    for k in range(KC):
                        mm = nc.tensor.matmul(bank[u][:, 0:E], xload[:, u, k * P:(k + 1) * P], wtok[:, k, :],
                                              start=(k == 0), stop=(k == KC - 1))
                    mm.then_inc(embedded, 1)

                def project(t, u):
                    pe.wait_ge(xt1, t + 1)
                    wait(pe, qk_sb, 4 * t)
                    for n, w in enumerate((wq, wq, wk, wk)):
                        for c in range(2):
                            mm = nc.tensor.matmul(bank[3][0:EH, n * P:(n + 1) * P],
                                                  w[:, c, (n % 2) * EH:(n % 2 + 1) * EH], xt[:, u, c, :],
                                                  start=(c == 0), stop=(c == 1))
                    mm.then_inc(qk_ps, 1)
                    wait(pe, v_sb, t)
                    for c in range(2):
                        mm = nc.tensor.matmul(bank[4][:, 0:E], xt[:, u, c, :], wv[:, c, :],
                                              start=(c == 0), stop=(c == 1))
                    mm.then_inc(v_ps, 1)

                def score(t, u):
                    pe.wait_ge(kbd_done, 2 * t + 2)
                    pe.wait_ge(qk_sb, 4 * t + 4)
                    wait(pe, s_sb, t - 1)
                    for g in range(2):
                        for b in range(IPT):
                            mm = nc.tensor.matmul(bank[5 + u][0:EH, g * P + b * S:g * P + (b + 1) * S],
                                                  kbd[:, u, g, b * EH:(b + 1) * EH],
                                                  qT_v[:, g, ds(t * P + b * S, S)], start=True, stop=True)
                    mm.then_inc(s_ps, 1)

                steps(pe, NT, [(score, 4), (project, 2), (embed, 0), (transpose, 1)])

            @block.scalar
            def _(act):
                def copy_x(t, u):
                    act.wait_ge(tr1, t + 1)
                    wait(act, v_ps, t - 1)
                    nc.scalar.activation(xt[:, u, :, :].rearrange("p c t -> p (c t)"), bank[2][0:EH, 0:2 * P],
                                         ACT.Copy).then_inc(xt1, 1)

                def deviation(t, u):
                    sdev_of(act, t, u, ln1, sdev1, inv1)

                def copy_qk(t, u):
                    act.wait_ge(qk_ps, t + 1)
                    for n in range(4):
                        dest = (qT_v, kT_v)[n // 2]
                        nc.scalar.activation(dest[:, n % 2, ds(t * P, P)], bank[3][0:EH, n * P:(n + 1) * P],
                                             ACT.Identity, bias=colb[:, n // 2, n % 2:n % 2 + 1]).then_inc(qk_sb, 1)

                def copy_s(t, u):
                    act.wait_ge(s_ps, t + 1)
                    nc.scalar.activation(sT_v[:, :, ds(t * P, P)],
                                         bank[5 + u][0:EH, 0:2 * P].rearrange("p (g t) -> p g t", g=2),
                                         ACT.Copy).then_inc(s_sb, 1)

                steps(act, NT, [(copy_s, 4), (copy_qk, 2), (deviation, 0), (copy_x, 1)])

            @block.vector
            def _(dve):
                def norm(t, u):
                    wait(dve, tr1, t - 1)
                    normalise(dve, t, u, sdev1, inv1, xn1, xn[:, u, :])

                def residual(t, u):
                    dve.wait_ge(embedded, t + 1)
                    nc.vector.tensor_tensor(h[:, ds(t, 1), :].rearrange("p a e -> p (a e)"), bank[u][:, 0:E],
                                            tokb[:, :], ALU.add).then_inc(h_done, 1)
                    moments_of(dve, t, u, ln1, h_done, t + 1)

                def values(t, u):
                    dve.wait_ge(v_ps, t + 1)
                    wait(dve, v_stored[u], in_slot(t, u) - 16)
                    nc.vector.tensor_tensor(vt[:, u, :], bank[4][:, 0:E], bv[:, :], ALU.add).then_inc(v_sb, 1)

                def keys(t, u):
                    wait(dve, s_ps, t - 1)
                    dve.wait_ge(qk_sb, 4 * t + 4)
                    for g in range(2):
                        nc.vector.tensor_tensor(
                            kbd[:, u, g, :].rearrange("p (b m j) -> p b m j", b=IPT, m=HG),
                            kT_v[:, g, ds(t * P, P)].rearrange("p (b j) -> p b j", b=IPT).unsqueeze(2)
                            .broadcast_to([EH, IPT, HG, S]),
                            hmask[:, :].unsqueeze(1).unsqueeze(3).broadcast_to([EH, IPT, HG, S]),
                            ALU.mult).then_inc(kbd_done, 1)

                steps(dve, NT, [(keys, 3), (values, 2), (norm, 1), (residual, 0)])

        ki_done, t2_ps, t2_sb, qs_done, d_ps, p_done, pt_ps, pt_sb, sm = (early_sem(n) for n in (
            "ki_done", "t2_ps", "t2_sb", "qs_done", "d_ps", "p_done", "pt_ps", "pt_sb", "sm"))
        ss_done, exp_done, share_done = early_sem("ss_done"), early_sem("exp_done"), early_sem("share_done")
        stage = kbd[:, :, :, :].rearrange("p u g k -> p (u g k)")[:, 0:16 * P]\
            .rearrange("p (u i k g b) -> p u i k g b", u=2, i=2, k=2, g=2)

        def at_position(buf, i):
            return buf.rearrange("p g (b i) -> p g b i", i=S)[:, :, :, ds(i, 1)].rearrange("p g b i -> p g (b i)")

        with nc.Block() as block:
            @block.sync
            def _(sp):
                sp.wait_ge(zeros_ready, 1)
                sp.dma_start(x_slots[:, 0:E].rearrange("(n p) e -> p n e", p=P),
                             xn[:, 0:1, :].broadcast_to([P, SLOT_TILES, E])).then_inc(slots_zero, 16)
                sp.dma_start(x_slots[:, E:E + 1], a["idle_rows"], allow_slow_non_contiguous=True)\
                    .then_inc(slots_zero, 16)
                sp.wait_ge(slots_zero, 32)

            @block.gpsimd
            def _(pool):
                nc.gpsimd.memset(xn[:, 0, :], 0.0).then_inc(zeros_ready, 1)

                def keys(j, u):
                    wait(pool, t2_ps, j - 1)
                    nc.gpsimd.tensor_copy(stage[:, u, 0, 0, :, :], at_position(kT_v, j)).then_inc(ki_done, 1)

                steps(pool, S, [(keys, 0)])

                def queries(n, u):
                    if isinstance(n, int) and n < 2:
                        pool.wait_ge(t2_ps, S)
                    wait(pool, d_ps, n - 1)
                    for i in range(2):
                        nc.gpsimd.tensor_copy(stage[:, u, i, 0, :, :], at_position(qT_v, 2 * n + i))\
                            .then_inc(qs_done, 1)

                steps(pool, S // 2, [(queries, 0)])

            @block.tensor
            def _(pe):
                def key_terms(j, u):
                    pe.wait_ge(ki_done, j + 1)
                    wait_alone(pe, t2_sb, j - 1, passed)
                    for g in range(2):
                        mm = nc.tensor.matmul(bank[u][:, g * EH:(g + 1) * EH], stage[:, u, 0, 0, g, :],
                                              pqbd[:, g, :, ds(S - 1 - j, S)], start=True, stop=True)
                    mm.then_inc(t2_ps, 1)

                steps(pe, S, [(key_terms, 0)])

                def query_terms(n, u):
                    pe.wait_ge(qs_done, 2 * n + 2)
                    pe.wait_ge(ss_done, 2 * n + 2)
                    wait_alone(pe, sm, 4 * n - 7, passed)
                    for i in range(2):
                        for g in range(2):
                            region = bank[2 + u][:, i * E + g * EH:i * E + (g + 1) * EH]
                            nc.tensor.matmul(region, stage[:, u, i, 0, g, :],
                                             pkbd[:, g, :, ds(S - 1 - i - 2 * n, S)], start=True, stop=False)
                            mm = nc.tensor.matmul(region, stage[:, u, i, 1, g, :], ident[0:EH, 0:EH],
                                                  start=False, stop=True)
                    mm.then_inc(d_ps, 1)

                def turn(n, u):
                    pe.wait_ge(p_done, n + 1)
                    wait(pe, pt_sb, n - 1)
                    for m in range(4):
                        mm = nc.tensor.transpose(bank[4 + u][0:EH, m * P:(m + 1) * P],
                                                 scores[:, u, m * EH:(m + 1) * EH], ident[:, :])
                    mm.then_inc(pt_ps, 1)

                steps(pe, S // 2, [(query_terms, 1), (turn, 2)])

            @block.scalar
            def _(act):
                def keep_t2(j, u):
                    act.wait_ge(t2_ps, j + 1)
                    nc.scalar.activation(
                        t2.rearrange("p i (m j) -> p i m j", m=H)[:, :, :, ds(j, 1)].rearrange("p i m j -> p i (m j)"),
                        bank[u][:, 0:E].rearrange("p (m i) -> p i m", m=H), ACT.Copy).then_inc(t2_sb, 1)

                steps(act, S, [(keep_t2, 0)])

                def stage_scores(n, u):
                    wait(act, d_ps, n - 1)
                    for i in range(2):
                        nc.scalar.activation(stage[:, u, i, 1, :, :], at_position(sT_v, 2 * n + i), ACT.Copy)\
                            .then_inc(ss_done, 1)

                def exponent(n, u):
                    act.wait_ge(sm, 4 * n + 3)
                    nc.scalar.activation(scores[:, u, :], scores[:, u, :], ACT.Exp, scale=SOFT0).then_inc(exp_done, 1)

                def keep_p(n, u):
                    act.wait_ge(pt_ps, n + 1)
                    for i in range(2):
                        dest = pT_v.rearrange("p g (b i) -> p g b i", i=S)[:, :, :, ds(2 * n + i, 1)]\
                            .rearrange("p g b i -> p g (b i)")
                        ins = nc.scalar.activation(
                            dest, bank[4 + u][0:EH, i * 2 * P:(i + 1) * 2 * P].rearrange("p (g b) -> p g b", g=2),
                            ACT.Copy)
                    ins.then_inc(pt_sb, 1)

                steps(act, S // 2, [(keep_p, 3), (stage_scores, 0), (exponent, 1)])

            @block.vector
            def _(dve):
                dve.wait_ge(t2_sb, S)

                def by_head(buf):
                    return buf.rearrange("p (m j) -> p m j", j=S)

                def spread(buf):
                    return buf.unsqueeze(2).broadcast_to([P, 2 * H, S])

                def shift(n, u):
                    dve.wait_ge(d_ps, n + 1)
                    wait(dve, pt_ps, n - 1)
                    nc.vector.tensor_tensor(scores[:, u, :], bank[2 + u][:, 0:2 * E],
                                            t2[:, ds(2 * n, 2), :].rearrange("p i k -> p (i k)"),
                                            ALU.add).then_inc(sm, 1)
                    dve.wait_ge(sm, 4 * n + 1)
                    nc.vector.tensor_reduce(top[:, u, :], by_head(scores[:, u, :]), AX.X, ALU.max).then_inc(sm, 1)
                    dve.wait_ge(sm, 4 * n + 2)
                    nc.vector.tensor_tensor(by_head(scores[:, u, :]), by_head(scores[:, u, :]),
                                            spread(top[:, u, :]), ALU.subtract).then_inc(sm, 1)

                def share(n, u):
                    dve.wait_ge(exp_done, n + 1)
                    nc.vector.tensor_reduce(mass[:, u, :], by_head(scores[:, u, :]), AX.X, ALU.add).then_inc(sm, 1)
                    dve.wait_ge(sm, 4 * n + 4)
                    nc.vector.reciprocal(top[:, u, :], mass[:, u, :]).then_inc(share_done, 1)
                    dve.wait_ge(share_done, n + 1)
                    nc.vector.tensor_tensor(by_head(scores[:, u, :]), by_head(scores[:, u, :]),
                                            spread(top[:, u, :]), ALU.mult).then_inc(p_done, 1)

                steps(dve, S // 2, [(share, 2), (shift, 1)])

        def tail_sems(tag):
            return {n: sem(n + tag) for n in (
                "moments", "sdev", "inverse", "xn", "turned", "xt", "gathered", "gate_ps", "gate_sb")}

        def tail_on_pe(pe, s, gate_w):
            def turn(t, u):
                pe.wait_ge(s["xn"], t + 1)
                wait(pe, s["xt"], t - 1)
                for c in range(2):
                    mm = nc.tensor.transpose(bank[4 + u][0:EH, c * P:(c + 1) * P],
                                             xn[:, u, c * EH:(c + 1) * EH], ident[:, :])
                mm.then_inc(s["turned"], 1)

            def gate(t, u):
                pe.wait_ge(s["xt"], t + 1)
                wait(pe, s["gate_sb"], t - 1)
                for c in range(2):
                    mm = nc.tensor.matmul(bank[6 + u][:, 0:NE0], xt[:, u, c, :], gate_w[:, c, :],
                                          start=(c == 0), stop=(c == 1))
                mm.then_inc(s["gate_ps"], 1)

            return turn, gate

        def tail_on_act(act, s):
            def copy_x(t, u):
                act.wait_ge(s["turned"], t + 1)
                wait(act, s["gate_ps"], t - 1)
                if s is tail2:
                    wait(act, s["gathered"], t - 1)
                nc.scalar.activation(xt[:, u, :, :].rearrange("p c t -> p (c t)"), bank[4 + u][0:EH, 0:2 * P],
                                     ACT.Copy).then_inc(s["xt"], 1)

            def deviation(t, u):
                sdev_of(act, t, u, s["moments"], s["sdev"], s["inverse"])

            return copy_x, deviation

        def tail_on_pool(pool, s):
            def gather(t, u):
                pool.wait_ge(s["xt"], t + 1)
                nc.gpsimd.tensor_copy(xnT_v[:, :, ds(t * P, P)], xt[:, u, :, :]).then_inc(s["gathered"], 1)

            return gather

        def tail_on_dve(dve, s):
            def norm(t, u):
                wait(dve, s["turned"], t - 1)
                if s is not tail2:
                    wait(dve, s["gathered"], t - 1)
                normalise(dve, t, u, s["sdev"], s["inverse"], s["xn"], xn[:, u, :])

            def keep_gate(t, u):
                dve.wait_ge(s["gate_ps"], t + 1)
                nc.vector.tensor_copy(logits[:, ds(t, 1), :].rearrange("p a e -> p (a e)"),
                                      bank[6 + u][:, 0:NE0]).then_inc(s["gate_sb"], 1)

            return norm, keep_gate

        tail2 = tail_sems("2")
        pv_ps, ot_sb, o_ps, h2, p_staged, o_turned = (sem(n) for n in (
            "pv_ps", "ot_sb", "o_ps", "h2", "p_staged", "o_turned"))
        rows_kept = [sem(f"rows_kept{n}") for n in range(2)]
        v_loaded = [sem(f"v_loaded{u}") for u in range(2)]
        vbd_done = [sem(f"vbd_done{g}") for g in range(2)]
        QUARTERS = 4

        def keep_rows_of(u, k):
            return scores[32 * k:32 * k + S, u, :], bank[u][32 * k:32 * k + S, 0:QUARTERS * EH]

        vrep = kT[0:EH, 0:2 * IPT * E].rearrange("p (u b e) -> p u b e", u=2, b=IPT)

        def spread_values(eng, t, u, g):
            eng.wait_ge(v_loaded[u], in_slot(t, u))
            wait(eng, pv_ps, t - 1)
            shape = [EH, IPT, HG, D]
            eng.tensor_tensor(vbd[:, u, g, :, :].rearrange("p b (m d) -> p b m d", m=HG),
                              vrep[:, u, :, g * EH:(g + 1) * EH].rearrange("p b (m d) -> p b m d", m=HG),
                              hmask[:, :].unsqueeze(1).unsqueeze(3).broadcast_to(shape), ALU.mult)\
                .then_inc(vbd_done[g], 1)

        with nc.Block() as block:
            @block.sync
            def _(sp):
                src = v_scr

                def load(t, u):
                    wait(sp, vbd_done[0], t - 1)
                    wait(sp, vbd_done[1], t - 1)
                    sp.dma_start(vrep[:, u, :, :],
                                 src[:, ds(t * IPT, IPT), :].unsqueeze(0).broadcast_to([HG, S, IPT, E]))\
                        .then_inc(v_loaded[u], 16)

                steps(sp, NT, [(load, 0)])

            @block.tensor
            def _(pe):
                def attend(t, u):
                    pe.wait_ge(vbd_done[0], t + 1)
                    pe.wait_ge(vbd_done[1], t + 1)
                    pe.wait_ge(p_staged, t + 1)
                    wait(pe, rows_kept[0], t - 1)
                    wait(pe, rows_kept[1], t - 1)
                    for b in range(IPT):
                        for g in range(2):
                            at, to = 32 * (b % QUARTERS), (b // QUARTERS * 2 + g) * EH
                            mm = nc.tensor.matmul(bank[u][at:at + S, to:to + EH], st1[:, u, g, b * S:(b + 1) * S],
                                                  vbd[:, u, g, b, :], start=True, stop=True)
                    mm.then_inc(pv_ps, 1)

                def turn_o(t, u):
                    pe.wait_ge(rows_kept[0], t + 1)
                    pe.wait_ge(rows_kept[1], t + 1)
                    wait(pe, ot_sb, 2 * t)
                    for c in range(QUARTERS):
                        mm = nc.tensor.transpose(bank[2][0:EH, c * P:(c + 1) * P],
                                                 scores[:, u, c * EH:(c + 1) * EH], ident[:, :])
                    mm.then_inc(o_turned, 1)

                def project(t, u):
                    pe.wait_ge(ot_sb, 2 * t + 2)
                    wait(pe, h2, 2 * t - 1)
                    for g in range(2):
                        mm = nc.tensor.matmul(bank[3][:, 0:E], ot[:, u, g, :], wo[:, g, :],
                                              start=(g == 0), stop=(g == 1))
                    mm.then_inc(o_ps, 1)

                turn, gate = tail_on_pe(pe, tail2, gate0)
                steps(pe, NT, [(gate, 7), (turn, 6), (project, 4), (attend, 1), (turn_o, 3)])

            @block.scalar
            def _(act):
                def stage_p(t, u):
                    wait(act, pv_ps, t - 1)
                    nc.scalar.activation(st1[:, u, :, :], pT_v[:, :, ds(t * P, P)], ACT.Copy).then_inc(p_staged, 1)

                def keep_rows(t, u):
                    act.wait_ge(pv_ps, t + 1)
                    wait(act, o_turned, t - 1)
                    for k in range(2):
                        dest, src = keep_rows_of(u, k)
                        ins = nc.scalar.activation(dest, src, ACT.Copy)
                    ins.then_inc(rows_kept[0], 1)

                def keep_o(t, u):
                    act.wait_ge(o_turned, t + 1)
                    wait(act, o_ps, t - 1)
                    src = bank[2][0:EH, :].rearrange("p (i g k r) -> p g i k r", i=2, g=2, k=QUARTERS)
                    for g in range(2):
                        nc.scalar.activation(ot[:, u, g, :].rearrange("p (i k r) -> p i k r", i=2, k=QUARTERS),
                                             src[:, g, :, :, 0:S], ACT.Copy).then_inc(ot_sb, 1)

                copy_x, deviation = tail_on_act(act, tail2)
                steps(act, NT, [(copy_x, 6), (keep_rows, 2), (stage_p, 0), (deviation, 4), (keep_o, 3)])

            @block.gpsimd
            def _(pool):
                gather = tail_on_pool(pool, tail2)
                steps(pool, NT, [(gather, 6), (lambda t, u: spread_values(nc.gpsimd, t, u, 1), 0)])

            @block.vector
            def _(dve):
                def residual(t, u):
                    tile = h[:, ds(t, 1), :].rearrange("p a e -> p (a e)")
                    dve.wait_ge(o_ps, t + 1)
                    nc.vector.tensor_tensor(tile, bank[3][:, 0:E], tile, ALU.add).then_inc(h2, 1)
                    dve.wait_ge(h2, 2 * t + 1)
                    nc.vector.tensor_tensor(tile, tile, bo[:, :], ALU.add).then_inc(h2, 1)
                    moments_of(dve, t, u, tail2["moments"], h2, 2 * t + 2)

                norm, keep_gate = tail_on_dve(dve, tail2)
                def keep_rows(t, u):
                    dve.wait_ge(pv_ps, t + 1)
                    wait(dve, o_turned, t - 1)
                    for k in range(2, QUARTERS):
                        dest, src = keep_rows_of(u, k)
                        ins = nc.vector.tensor_copy(dest, src)
                    ins.then_inc(rows_kept[1], 1)

                steps(dve, NT, [(keep_gate, 7), (norm, 5), (keep_rows, 2),
                                (lambda t, u: spread_values(nc.vector, t, u, 0), 0), (residual, 4)])

        r0, sig_done, routed = sem("r0"), sem("sig_done"), sem("routed")

        def ranks(link, value, n, lower, rank, eligible=None):
            shape = [P, NT, n, n]
            gt = pairs[:, 0:NT * n * n].rearrange("p (t a b) -> p t a b", a=n, b=n)
            eq = ties[:, 0:NT * n * n].rearrange("p (t a b) -> p t a b", a=n, b=n)
            of_b, of_a = value.unsqueeze(2).broadcast_to(shape), value.unsqueeze(3).broadcast_to(shape)
            nc.vector.tensor_tensor(gt, of_b, of_a, ALU.is_gt)
            link(nc.vector.tensor_tensor(eq, of_b, of_a, ALU.is_equal))
            link(nc.vector.tensor_tensor(eq, eq, lower.rearrange("p (a b) -> p a b", a=n).unsqueeze(1)
                                         .broadcast_to(shape), ALU.mult))
            link(nc.vector.tensor_tensor(gt, gt, eq, ALU.add))
            if eligible is not None:
                link(nc.vector.tensor_tensor(gt, gt, eligible.unsqueeze(2).broadcast_to(shape), ALU.mult))
            link(nc.vector.tensor_reduce(rank, gt, AX.X, ALU.add))

        h13_ps, silu_done, hid_done, y_ps, y_done = (sem(n) for n in (
            "h13_ps", "silu_done", "hid_done", "y_ps", "y_done"))
        EXP = NE0 + 1

        wq1_loaded, amw, prw, ln3 = (sem(n) for n in ("wq1_loaded", "amw", "prw", "ln3"))

        def absmax(dest, src):
            return nc.vector.tensor_reduce(dest, src, AX.XY if len(src.shape) == 3 else AX.X, ALU.max,
                                           apply_absolute_value=True)

        def scales(dve, pool_done, done, lo, hi, base=0):
            dve.wait_ge(pool_done, 1)
            nc.vector.tensor_scalar(qs[:, lo:hi], peaks[:, lo:hi], 1.0 / QMAX, 1e-8, ALU.mult, ALU.max)\
                .then_inc(done, 1)
            dve.wait_ge(done, base + 1)
            nc.vector.reciprocal(qi[:, lo:hi], qs[:, lo:hi]).then_inc(done, 1)
            dve.wait_ge(done, base + 2)

        WQ_, WP_, X_, Q_, K_, V_, P_, O_ = range(8)

        with nc.Block() as block:
            @block.sync
            def _(sp):
                sp.wait_ge(routed, 1)
                sp.dma_start(wqkv32, a["L1_attn_w_qkv"]).then_inc(wq1_loaded, 16)
                sp.dma_start(wproj32, a["L1_attn_w_proj"]).then_inc(wq1_loaded, 16)

            @block.gpsimd
            def _(pool):
                pool.wait_ge(amw, 3)
                nc.gpsimd.partition_all_reduce(peaks[:, WQ_:WP_ + 1], peak[:, WQ_:WP_ + 1], P, RMAX).then_inc(prw, 1)

            @block.tensor
            def _(pe):
                def up(blk, e):
                    n = blk * EXP + e
                    wait(pe, hid_done, n - 2)
                    for w in range(2):
                        for c in range(2):
                            mm = nc.tensor.matmul(bank[2 * (e % 3) + w][:, :], w13[:, w, e, c, :],
                                                  xnT_v[:, c, ds(blk * BLK, BLK)], start=(c == 0), stop=(c == 1))
                    mm.then_inc(h13_ps, 1)

                def down(blk, e):
                    n = blk * EXP + e
                    pe.wait_ge(hid_done, n + 1)
                    for k in range(TPB):
                        wait(pe, y_done, 4 * n - 2 * (1 - k // 2))
                        mm = nc.tensor.matmul(bank[6 + k // 2][:, (k % 2) * E:(k % 2 + 1) * E],
                                              hidden0[:, e % 3, k * P:(k + 1) * P], w2[:, e, :],
                                              start=True, stop=True)
                        mm.then_inc(y_ps, 1)

                def one(blk, last=False):
                    for e in range(EXP):
                        if e + 2 < EXP:
                            up(blk, e + 2)
                        elif not last:
                            up(blk + 1, e + 2 - EXP)
                        down(blk, e)

                up(0, 0)
                up(0, 1)
                one(0)
                with pe.Fori(1, NB - 1, 1) as blk:
                    one(blk)
                one(NB - 1, last=True)

            @block.scalar
            def _(act):
                nc.scalar.activation(logits[:, :, :], logits[:, :, :], ACT.Sigmoid).then_inc(sig_done, 1)

                def one(blk):
                    for e in range(EXP):
                        n = blk * EXP + e
                        act.wait_ge(h13_ps, n + 1)
                        wait(act, hid_done, n - 2)
                        nc.scalar.activation(silu0[:, e % 3, :], bank[2 * (e % 3)][:, :], ACT.Silu)\
                            .then_inc(silu_done, 1)

                one(0)
                with act.Fori(1, NB, 1) as blk:
                    one(blk)

            @block.vector
            def _(dve):
                count = [0]

                def link(ins):
                    count[0] += 1
                    ins.then_inc(r0, 1)
                    dve.wait_ge(r0, count[0])

                s, chosen, rank = rt
                shape8 = [P, NT, NE0]
                dve.wait_ge(sig_done, 1)
                link(nc.vector.tensor_tensor(s[:, :, :], logits[:, :, :],
                                             gbias[:, :].unsqueeze(1).broadcast_to(shape8), ALU.add))
                two = s[:, :, :].rearrange("p t (g k) -> p t g k", k=2)
                group = rank[:, :, 0:GROUPS]
                link(nc.vector.tensor_tensor(group, two[:, :, :, 0], two[:, :, :, 1], ALU.add))
                grank = rank[:, :, GROUPS:2 * GROUPS]
                ranks(link, group, GROUPS, lower4[:, :], grank)
                link(nc.vector.tensor_scalar(grank, grank, 2.0, None, ALU.is_lt))
                link(nc.vector.tensor_copy(chosen[:, :, :].rearrange("p t (g k) -> p t g k", k=2),
                                           grank.unsqueeze(3).broadcast_to([P, NT, GROUPS, 2])))
                ranks(link, s[:, :, :], NE0, lower8[:, :], rank[:, :, :], chosen[:, :, :])
                link(nc.vector.scalar_tensor_tensor(s[:, :, :], rank[:, :, :], 2.0, chosen[:, :, :],
                                                    ALU.is_lt, ALU.mult))
                link(nc.vector.tensor_tensor(s[:, :, :], s[:, :, :], logits[:, :, :], ALU.mult))
                link(nc.vector.tensor_reduce(small[:, :, 0], s[:, :, :], AX.X, ALU.add))
                link(nc.vector.tensor_scalar(small[:, :, 0], small[:, :, 0], 1e-6, None, ALU.add))
                link(nc.vector.reciprocal(small[:, :, 1], small[:, :, 0]))
                link(nc.vector.tensor_tensor(comb[:, :, 0:NE0], s[:, :, :],
                                             small[:, :, 1:2].broadcast_to(shape8), ALU.mult))
                nc.vector.tensor_copy(small[:, 0, 0:1], small[:, 0, 0:1]).then_inc(routed, 1)

                def gate(blk, e):
                    n = blk * EXP + e
                    dve.wait_ge(silu_done, n + 1)
                    wait(dve, y_ps, 4 * n - 8)
                    nc.vector.tensor_tensor(hidden0[:, e % 3, :], silu0[:, e % 3, :], bank[2 * (e % 3) + 1][:, :],
                                            ALU.mult).then_inc(hid_done, 1)

                def add(blk, e):
                    n = blk * EXP + e
                    for k in range(TPB):
                        tile = h[:, ds(blk * TPB + k, 1), :].rearrange("p a e -> p (a e)")
                        dve.wait_ge(y_ps, 4 * n + 2 * (k // 2) + 2)
                        wait(dve, y_done, 4 * n + k - 3)
                        nc.vector.scalar_tensor_tensor(
                            tile, bank[6 + k // 2][:, (k % 2) * E:(k % 2 + 1) * E],
                            comb[:, ds(blk * TPB + k, 1), e:e + 1].rearrange("p a e -> p (a e)"), tile,
                            ALU.mult, ALU.add).then_inc(y_done, 1)

                def one(blk, last=False):
                    for e in range(EXP):
                        if e + 1 < EXP:
                            gate(blk, e + 1)
                        elif not last:
                            gate(blk + 1, 0)
                        add(blk, e)
                    for k in range(TPB):
                        t = blk * TPB + k
                        wait_alone(dve, y_done, 4 * (blk * EXP + EXP - 1) + k + 1, passed)
                        nc.vector.bn_stats(all_moments[:, ds(t, 1), :].rearrange("p a s -> p (a s)"),
                                           h[:, ds(t, 1), :].rearrange("p a e -> p (a e)")).then_inc(ln3, 1)

                nc.vector.memset(peak[:, :], 0.0).then_inc(amw, 1)
                gate(0, 0)
                one(0)
                dve.wait_ge(amw, 1)
                dve.wait_ge(wq1_loaded, 32)
                absmax(peak[0:EH, WQ_:WQ_ + 1], wqkv32.rearrange("p c n -> p (c n)")).then_inc(amw, 1)
                absmax(peak[0:EH, WP_:WP_ + 1], wproj32.rearrange("p c n -> p (c n)")).then_inc(amw, 1)
                with dve.Fori(1, NB - 1, 1) as blk:
                    one(blk)
                one(NB - 1, last=True)

        sdev3, inv3, xn3, am3, pr3, sc3 = (sem(n) for n in ("sdev3", "inv3", "xn3", "am3", "pr3", "sc3"))

        w1_loaded, w2_loaded = sem("w1_loaded"), sem("w2_loaded")
        EARLY_W2 = (W13 + W2) // (FC * E)

        def load_w2(eng, experts):
            for e in experts:
                eng.dma_start(w2_all[:, e, :, :].rearrange("p c n -> p (c n)"), a["L1_ffn_W2"][e, :, :])\
                    .then_inc(w2_loaded, 16)

        with nc.Block() as block:
            @block.scalar
            def _(act):
                load_w2(act, range(EARLY_W2))
                act.wait_ge(ln3, 2 * NT)
                nc.scalar.activation(sdevs[:, 0, :], meanvars[:, :, 1], ACT.Sqrt, bias=eps[:, 0:1]).then_inc(sdev3, 1)

            @block.vector
            def _(dve):
                dve.wait_ge(ln3, NT)
                for t in range(NT):
                    nc.vector.bn_aggr(meanvars[:, t, :], all_moments[:, t, :]).then_inc(ln3, 1)
                scales(dve, prw, sc3, WQ_, WP_ + 1)
                nc.vector.tensor_scalar(wround, wqkv32, qi[0:EH, WQ_:WQ_ + 1], ROUND, ALU.mult, ALU.add)\
                    .then_inc(sc3, 1)
                nc.vector.tensor_scalar(wproj32, wproj32, qi[0:EH, WP_:WP_ + 1], ROUND, ALU.mult, ALU.add)\
                    .then_inc(sc3, 1)
                dve.wait_ge(sdev3, 1)
                nc.vector.reciprocal(sdevs[:, 1, :], sdevs[:, 0, :]).then_inc(inv3, 1)
                dve.wait_ge(sc3, 4)
                nc.vector.tensor_scalar(wqkv16, wround, ROUND, QMAX, ALU.subtract, ALU.min).then_inc(sc3, 1)
                nc.vector.tensor_scalar(wproj16, wproj32, ROUND, QMAX, ALU.subtract, ALU.min).then_inc(sc3, 1)
                dve.wait_ge(inv3, 1)
                for t in range(NT):
                    nc.vector.tensor_scalar(xall[:, t, :], h[:, t, :], meanvars[:, t, 0:1], sdevs[:, 1, t:t + 1],
                                            ALU.subtract, ALU.mult).then_inc(xn3, 1)
                dve.wait_ge(xn3, NT)
                absmax(peak[:, X_:X_ + 1], xall.rearrange("p n e -> p (n e)")).then_inc(am3, 1)
                scales(dve, pr3, sc3, X_, X_ + 1, base=6)
                nc.vector.tensor_scalar(prod[:, 0:1], qs[:, X_:X_ + 1], qs[:, WQ_:WQ_ + 1], None, ALU.mult)\
                    .then_inc(sc3, 1)

            @block.gpsimd
            def _(pool):
                for used in early_sems:
                    pool.sem_clear(used)

                pool.wait_ge(am3, 1)
                nc.gpsimd.partition_all_reduce(peaks[:, X_:X_ + 1], peak[:, X_:X_ + 1], P, RMAX).then_inc(pr3, 1)

        early.close()

        xr4, xi4, tr4, xt4, q_ps4, v_ps4, q_sb4, v_sb4, st4, pr4, am4, sc4 = (sem(n) for n in (
            "xr4", "xi4", "tr4", "xt4", "q_ps4", "v_ps4", "q_sb4", "v_sb4", "st4", "pr4", "am4", "sc4"))
        xt16 = xt[:, :, :, :].rearrange("p u c t -> p u (c t)").bitcast(BF16)

        with nc.Block() as block:
            @block.vector
            def _(dve):
                def quantise(t, u):
                    nc.vector.tensor_scalar(xn[:, u, :], xall[:, ds(t, 1), :].rearrange("p a e -> p (a e)"),
                                            qi[:, X_:X_ + 1], ROUND, ALU.mult, ALU.add).then_inc(xr4, 1)
                    dve.wait_ge(xr4, t + 1)
                    wait(dve, tr4, t - 1)
                    nc.vector.tensor_scalar(x16[:, u, 0:E], xn[:, u, :], ROUND, QMAX, ALU.subtract, ALU.min)\
                        .then_inc(xi4, 1)

                def values(t, u):
                    tile = vall[:, ds(t, 1), :].rearrange("p a e -> p (a e)")
                    dve.wait_ge(v_ps4, t + 1)
                    nc.vector.scalar_tensor_tensor(tile, bank[4 + u][:, 0:E], prod[:, 0:1], bv1[:, :],
                                                   ALU.mult, ALU.add).then_inc(v_sb4, 1)
                    dve.wait_ge(v_sb4, t + 1)
                    absmax(stats[:, V_, ds(t, 1)], tile).then_inc(st4, 1)
                    dve.wait_ge(q_sb4, 4 * t + 4)
                    absmax(stats[0:EH, Q_, ds(t, 1)], qT_v[:, :, ds(t * P, P)]).then_inc(st4, 1)
                    absmax(stats[0:EH, K_, ds(t, 1)], kT_v[:, :, ds(t * P, P)]).then_inc(st4, 1)

                steps(dve, NT, [(quantise, 0), (values, 2)])
                dve.wait_ge(st4, 3 * NT)
                nc.vector.tensor_reduce(peak[:, Q_:V_ + 1], stats[:, Q_:V_ + 1, :], AX.X, ALU.max).then_inc(am4, 1)
                scales(dve, pr4, sc4, Q_, V_ + 1)
                nc.vector.tensor_scalar(prod[:, 1:2], qs[:, Q_:Q_ + 1], qs[:, K_:K_ + 1], SOFT1, ALU.mult, ALU.mult)\
                    .then_inc(sc4, 1)

            @block.gpsimd
            def _(pool):
                pool.wait_ge(am4, 1)
                nc.gpsimd.partition_all_reduce(peaks[:, Q_:V_ + 1], peak[:, Q_:V_ + 1], P, RMAX).then_inc(pr4, 1)

            @block.tensor
            def _(pe):
                def turn(t, u):
                    pe.wait_ge(xi4, t + 1)
                    wait(pe, xt4, t - 1)
                    for c in range(2):
                        mm = nc.tensor.transpose(bank[u][0:EH, c * P // 2:(c + 1) * P // 2].bitcast(BF16),
                                                 x16[:, u, c * EH:(c + 1) * EH], ident16[:, :])
                    mm.then_inc(tr4, 1)

                def project(t, u):
                    pe.wait_ge(xt4, t + 1)
                    wait(pe, q_sb4, 4 * t - 4)
                    for n in range(4):
                        for c in range(2):
                            mm = nc.tensor.matmul(bank[2 + u][0:EH, n * P:(n + 1) * P],
                                                  wqkv16[:, c, n * EH:(n + 1) * EH], xt16[:, u, c * P:(c + 1) * P],
                                                  start=(c == 0), stop=(c == 1))
                    mm.then_inc(q_ps4, 1)
                    wait(pe, v_sb4, t - 1)
                    for c in range(2):
                        mm = nc.tensor.matmul(bank[4 + u][:, 0:E], xt16[:, u, c * P:(c + 1) * P],
                                              wqkv16[:, c, 2 * E:3 * E], start=(c == 0), stop=(c == 1))
                    mm.then_inc(v_ps4, 1)

                steps(pe, NT, [(turn, 0), (project, 1)])

            @block.scalar
            def _(act):
                def copy_x(t, u):
                    act.wait_ge(tr4, t + 1)
                    wait(act, v_ps4, t - 1)
                    nc.scalar.activation(xt16[:, u, 0:2 * P], bank[u][0:EH, 0:P].bitcast(BF16), ACT.Copy)\
                        .then_inc(xt4, 1)

                def copy_qk(t, u):
                    act.wait_ge(q_ps4, t + 1)
                    for n in range(4):
                        dest = (qT_v, kT_v)[n // 2]
                        nc.scalar.activation(dest[:, n % 2, ds(t * P, P)], bank[2 + u][0:EH, n * P:(n + 1) * P],
                                             ACT.Identity, bias=bqk1[:, n // 2, n % 2:n % 2 + 1],
                                             scale=prod[0:EH, 0:1]).then_inc(q_sb4, 1)

                steps(act, NT, [(copy_x, 0), (copy_qk, 1)])

        qr5, q5, kr5, k5, v5, s_ps5, s_sb5, sc_ps5, sm5, exp5, p5, st5, am5, pr5, sc5 = (sem(n) for n in (
            "qr5", "q5", "kr5", "k5", "v5", "s_ps5", "s_sb5", "sc_ps5", "sm5", "exp5", "p5", "st5", "am5", "pr5",
            "sc5"))
        vr5 = sem("vr5")
        v_stored16 = [sem(f"v_stored16_{u}") for u in range(2)]
        pall = t2
        st5buf = xt
        qround = ot
        kround = st1
        kbd5 = [sem(f"kbd5_{g}") for g in range(2)]

        def spread_keys(eng, t, u, g):
            eng.wait_ge(k5, t + 1)
            wait(eng, s_ps5, t - 1)
            eng.tensor_tensor(
                kbd16[:, u, g * IPT * EH:(g + 1) * IPT * EH].rearrange("p (b m j) -> p b m j", b=IPT, m=HG),
                k16[:, u, g, :].rearrange("p (b j) -> p b j", b=IPT).unsqueeze(2).broadcast_to([EH, IPT, HG, S]),
                hmask16[:, :].unsqueeze(1).unsqueeze(3).broadcast_to([EH, IPT, HG, S]), ALU.mult)\
                .then_inc(kbd5[g], 1)

        with nc.Block() as block:
            @block.gpsimd
            def _(pool):
                def store(t, u):
                    pool.wait_ge(v5, t + 1)
                    pool.dma_start(by_key(v_scr16, t), v16[:, u, :]).then_inc(v_stored16[u], 16)

                steps(pool, NT, [(lambda t, u: spread_keys(nc.gpsimd, t, u, 1), 1), (store, 1)])
                for u in range(2):
                    pool.wait_ge(v_stored16[u], 8 * NT)
                pool.wait_ge(am5, 1)
                nc.gpsimd.partition_all_reduce(peaks[:, P_:P_ + 1], peak[:, P_:P_ + 1], P, RMAX).then_inc(pr5, 1)

            @block.vector
            def _(dve):
                def by_head(buf):
                    return buf.rearrange("p (m j) -> p m j", j=S)

                def spread(buf):
                    return buf.unsqueeze(2).broadcast_to([P, H, S])

                def shift(t, u):
                    dve.wait_ge(sc_ps5, t + 1)
                    nc.vector.tensor_reduce(top[:, u, 0:H], by_head(bank[4 + u][:, 0:E]), AX.X, ALU.max)\
                        .then_inc(sm5, 1)
                    dve.wait_ge(sm5, 4 * t + 1)
                    nc.vector.tensor_tensor(by_head(scores[:, u, 0:E]), by_head(bank[4 + u][:, 0:E]),
                                            spread(top[:, u, 0:H]), ALU.subtract).then_inc(sm5, 1)

                def share(t, u):
                    tile = pall[:, ds(t, 1), :].rearrange("p a e -> p (a e)")
                    dve.wait_ge(exp5, t + 1)
                    nc.vector.tensor_reduce(mass[:, u, 0:H], by_head(scores[:, u, 0:E]), AX.X, ALU.add)\
                        .then_inc(sm5, 1)
                    dve.wait_ge(sm5, 4 * t + 3)
                    nc.vector.reciprocal(top[:, u, H:2 * H], mass[:, u, 0:H]).then_inc(sm5, 1)
                    dve.wait_ge(sm5, 4 * t + 4)
                    nc.vector.tensor_tensor(by_head(tile), by_head(scores[:, u, 0:E]), spread(top[:, u, H:2 * H]),
                                            ALU.mult).then_inc(p5, 1)

                def values(t, u):
                    nc.vector.tensor_scalar(xn[:, u, :], vall[:, ds(t, 1), :].rearrange("p a e -> p (a e)"),
                                            qi[:, V_:V_ + 1], ROUND, ALU.mult, ALU.add).then_inc(vr5, 1)
                    dve.wait_ge(vr5, t + 1)
                    wait(dve, v_stored16[u], in_slot(t, u) - 16)
                    nc.vector.tensor_scalar(v16[:, u, :], xn[:, u, :], ROUND, QMAX, ALU.subtract, ALU.min)\
                        .then_inc(v5, 1)

                steps(dve, NT, [(share, 4), (lambda t, u: spread_keys(nc.vector, t, u, 0), 1), (shift, 3), (values, 0)])
                dve.wait_ge(p5, NT)
                nc.vector.tensor_reduce(peak[:, P_:P_ + 1], pall.rearrange("p n e -> p (n e)"), AX.X, ALU.max)\
                    .then_inc(am5, 1)
                scales(dve, pr5, sc5, P_, P_ + 1)
                nc.vector.tensor_scalar(prod[:, 2:3], qs[:, P_:P_ + 1], qs[:, V_:V_ + 1], None, ALU.mult)\
                    .then_inc(sc5, 1)

            @block.tensor
            def _(pe):
                def score(t, u):
                    pe.wait_ge(q5, t + 1)
                    pe.wait_ge(kbd5[0], t + 1)
                    pe.wait_ge(kbd5[1], t + 1)
                    wait(pe, s_sb5, t - 1)
                    for g in range(2):
                        for b in range(IPT):
                            at = g * IPT * EH + b * EH
                            mm = nc.tensor.matmul(bank[u][0:EH, g * P + b * S:g * P + (b + 1) * S],
                                                  kbd16[:, u, at:at + EH], q16[:, u, g, b * S:(b + 1) * S],
                                                  start=True, stop=True)
                    mm.then_inc(s_ps5, 1)

                def turn(t, u):
                    pe.wait_ge(s_sb5, t + 1)
                    wait(pe, sm5, 4 * t - 6)
                    for g in range(2):
                        mm = nc.tensor.transpose(bank[4 + u][:, g * EH:(g + 1) * EH], st5buf[:, u, g, :],
                                                 ident[0:EH, 0:EH])
                    mm.then_inc(sc_ps5, 1)

                steps(pe, NT, [(turn, 2), (score, 1)])

            @block.scalar
            def _(act):
                def keep_s(t, u):
                    act.wait_ge(s_ps5, t + 1)
                    wait(act, sc_ps5, t - 1)
                    nc.scalar.activation(st5buf[:, u, :, :].rearrange("p g t -> p (g t)"), bank[u][0:EH, 0:2 * P],
                                         ACT.Copy).then_inc(s_sb5, 1)

                def exponent(t, u):
                    act.wait_ge(sm5, 4 * t + 2)
                    nc.scalar.activation(scores[:, u, 0:E], scores[:, u, 0:E], ACT.Exp, scale=prod[:, 1:2])\
                        .then_inc(exp5, 1)

                def queries(t, u):
                    nc.scalar.activation(qround[:, u, :, :], qT_v[:, :, ds(t * P, P)], ACT.Identity,
                                         bias=rounding[0:EH, 0:1], scale=qi[0:EH, Q_:Q_ + 1]).then_inc(qr5, 1)
                    act.wait_ge(qr5, t + 1)
                    wait(act, s_ps5, t - 1)
                    nc.scalar.activation(q16[:, u, :, :], qround[:, u, :, :], ACT.Identity,
                                         bias=rounding[0:EH, 1:2]).then_inc(q5, 1)

                def keys(t, u):
                    nc.scalar.activation(kround[:, u, :, :], kT_v[:, :, ds(t * P, P)], ACT.Identity,
                                         bias=rounding[0:EH, 0:1], scale=qi[0:EH, K_:K_ + 1]).then_inc(kr5, 1)
                    act.wait_ge(kr5, t + 1)
                    for eng_done in kbd5:
                        wait(act, eng_done, t - 1)
                    nc.scalar.activation(k16[:, u, :, :], kround[:, u, :, :], ACT.Identity,
                                         bias=rounding[0:EH, 1:2]).then_inc(k5, 1)

                steps(act, NT, [(keep_s, 2), (keys, 0), (exponent, 3), (queries, 0)])


        pr6, pi6, tr6, pt6, o_ps6, o_sb6, st6, am6, par6, sc6 = (sem(n) for n in (
            "pr6", "pi6", "tr6", "pt6", "o_ps6", "o_sb6", "st6", "am6", "par6", "sc6"))
        v16_loaded = [sem(f"v16_loaded{u}") for u in range(2)]
        vbd16_done = [sem(f"vbd16_done{g}") for g in range(2)]
        vrep16 = kT[0:EH, 0:IPT * E].bitcast(BF16).rearrange("p (u b e) -> p u b e", u=2, b=IPT)
        CELLS = IPT * EH
        def spread_values16(eng, t, u, g):
            eng.wait_ge(v16_loaded[u], in_slot(t, u))
            wait(eng, o_ps6, t - 1)
            eng.tensor_tensor(
                vbd16[:, u, g * CELLS:(g + 1) * CELLS].rearrange("p (b m d) -> p b m d", b=IPT, m=HG),
                vrep16[:, u, :, g * EH:(g + 1) * EH].rearrange("p b (m d) -> p b m d", m=HG),
                hmask16[:, :].unsqueeze(1).unsqueeze(3).broadcast_to([EH, IPT, HG, D]), ALU.mult)\
                .then_inc(vbd16_done[g], 1)

        with nc.Block() as block:
            @block.sync
            def _(sp):
                src = v_scr16

                def load(t, u):
                    wait(sp, vbd16_done[0], t - 1)
                    wait(sp, vbd16_done[1], t - 1)
                    sp.dma_start(vrep16[:, u, :, :],
                                 src[:, ds(t * IPT, IPT), :].unsqueeze(0).broadcast_to([HG, S, IPT, E]))\
                        .then_inc(v16_loaded[u], 16)

                steps(sp, NT, [(load, 0)])

            @block.vector
            def _(dve):
                def range_of(t, u):
                    dve.wait_ge(o_sb6, t + 1)
                    absmax(stats[0:EH, O_, ds(t, 1)], oT_v[:, :, ds(t * P, P)]).then_inc(st6, 1)

                steps(dve, NT, [(range_of, 4), (lambda t, u: spread_values16(nc.vector, t, u, 0), 0)])
                dve.wait_ge(st6, NT)
                nc.vector.tensor_reduce(peak[:, O_:O_ + 1], stats[:, O_, :], AX.X, ALU.max).then_inc(am6, 1)
                scales(dve, par6, sc6, O_, O_ + 1)
                nc.vector.tensor_scalar(prod[:, 3:4], qs[:, O_:O_ + 1], qs[:, WP_:WP_ + 1], None, ALU.mult)\
                    .then_inc(sc6, 1)

            @block.gpsimd
            def _(pool):
                steps(pool, NT, [(lambda t, u: spread_values16(nc.gpsimd, t, u, 1), 0)])
                pool.wait_ge(am6, 1)
                nc.gpsimd.partition_all_reduce(peaks[:, O_:O_ + 1], peak[:, O_:O_ + 1], P, RMAX).then_inc(par6, 1)

            @block.tensor
            def _(pe):
                def turn(t, u):
                    pe.wait_ge(pi6, t + 1)
                    wait(pe, pt6, t - 1)
                    for c in range(2):
                        mm = nc.tensor.transpose(bank[u][0:EH, c * P // 2:(c + 1) * P // 2].bitcast(BF16),
                                                 x16[:, u, c * EH:(c + 1) * EH], ident16[:, :])
                    mm.then_inc(tr6, 1)

                def attend(t, u):
                    pe.wait_ge(vbd16_done[0], t + 1)
                    pe.wait_ge(vbd16_done[1], t + 1)
                    pe.wait_ge(pt6, t + 1)
                    wait(pe, o_sb6, t - 1)
                    for g in range(2):
                        for b in range(IPT):
                            at = g * CELLS + b * EH
                            mm = nc.tensor.matmul(bank[2 + u][0:EH, g * P + b * S:g * P + (b + 1) * S],
                                                  vbd16[:, u, at:at + EH],
                                                  xt16[:, u, g * P + b * S:g * P + (b + 1) * S],
                                                  start=True, stop=True)
                    mm.then_inc(o_ps6, 1)

                steps(pe, NT, [(turn, 1), (attend, 2)])

            @block.scalar
            def _(act):
                def quantise(t, u):
                    nc.scalar.activation(xn[:, u, :], pall[:, ds(t, 1), :].rearrange("p a e -> p (a e)"),
                                         ACT.Identity, bias=rounding[:, 0:1], scale=qi[:, P_:P_ + 1]).then_inc(pr6, 1)
                    act.wait_ge(pr6, t + 1)
                    wait(act, tr6, t - 1)
                    nc.scalar.activation(x16[:, u, 0:E], xn[:, u, :], ACT.Identity, bias=rounding[:, 1:2])\
                        .then_inc(pi6, 1)

                def keep_p(t, u):
                    act.wait_ge(tr6, t + 1)
                    wait(act, o_ps6, t - 1)
                    nc.scalar.activation(xt16[:, u, 0:2 * P], bank[u][0:EH, 0:P].bitcast(BF16), ACT.Copy)\
                        .then_inc(pt6, 1)

                def keep_o(t, u):
                    act.wait_ge(o_ps6, t + 1)
                    nc.scalar.activation(oT_v[:, :, ds(t * P, P)],
                                         bank[2 + u][0:EH, 0:2 * P].rearrange("p (g t) -> p g t", g=2),
                                         ACT.Copy, scale=prod[0:EH, 2:3]).then_inc(o_sb6, 1)

                steps(act, NT, [(keep_o, 3), (keep_p, 1), (quantise, 0)])

        or7, oi7, w_ps7, h7 = (sem(n) for n in ("or7", "oi7", "w_ps7", "h7"))
        tail7 = tail_sems("7")

        with nc.Block() as block:
            @block.vector
            def _(dve):
                def residual(t, u):
                    tile = h[:, ds(t, 1), :].rearrange("p a e -> p (a e)")
                    dve.wait_ge(w_ps7, t + 1)
                    nc.vector.scalar_tensor_tensor(tile, bank[2 + u][:, 0:E], prod[:, 3:4], tile, ALU.mult, ALU.add)\
                        .then_inc(h7, 1)
                    dve.wait_ge(h7, 2 * t + 1)
                    nc.vector.tensor_tensor(tile, tile, bproj[:, :], ALU.add).then_inc(h7, 1)
                    moments_of(dve, t, u, tail7["moments"], h7, 2 * t + 2)

                norm, keep_gate = tail_on_dve(dve, tail7)
                steps(dve, NT, [(keep_gate, 6), (norm, 3), (residual, 1)])

            @block.tensor
            def _(pe):
                def project(t, u):
                    pe.wait_ge(oi7, t + 1)
                    wait(pe, h7, 2 * t - 2)
                    for g in range(2):
                        mm = nc.tensor.matmul(bank[2 + u][:, 0:E], x16[0:EH, u, g * P:(g + 1) * P], wproj16[:, g, :],
                                              start=(g == 0), stop=(g == 1))
                    mm.then_inc(w_ps7, 1)

                turn, gate = tail_on_pe(pe, tail7, gate1)
                steps(pe, NT, [(gate, 5), (turn, 4), (project, 1)])

            @block.scalar
            def _(act):
                load_w2(act, range(EARLY_W2, NE1))
                copy_x, deviation = tail_on_act(act, tail7)

                def quantise(t, u):
                    nc.scalar.activation(ot[:, u, :, :], oT_v[:, :, ds(t * P, P)], ACT.Identity,
                                         bias=rounding[0:EH, 0:1], scale=qi[0:EH, O_:O_ + 1]).then_inc(or7, 1)
                    act.wait_ge(or7, t + 1)
                    wait(act, w_ps7, t - 1)
                    nc.scalar.activation(x16[0:EH, u, 0:2 * P], ot[:, u, :, :].rearrange("p g t -> p (g t)"),
                                         ACT.Identity, bias=rounding[0:EH, 1:2]).then_inc(oi7, 1)

                steps(act, NT, [(copy_x, 4), (quantise, 0), (deviation, 2)])

            @block.gpsimd
            def _(pool):
                def keep_rows(t, u):
                    pool.wait_ge(tail7["xn"], t + 1)
                    nc.gpsimd.tensor_copy(rows_x[:, ds(t, 1), 0:E].rearrange("p a e -> p (a e)"), xn[:, u, :])\
                        .then_inc(tail7["gathered"], 1)

                steps(pool, NT, [(keep_rows, 0)])

            @block.sync
            def _(sp):
                for e in range(NE1):
                    sp.dma_start(w1_all[0:EH, e, :, :].rearrange("p c f -> p (c f)"), a["L1_ffn_W1"][e, :, :])\
                        .then_inc(w1_loaded, 16)
                sp.dma_start(w1_all[EH:EH + 1, :, 1, :], a["L1_ffn_b1"]).then_inc(w1_loaded, 16)

        cc8, chosen8, prefix8, places, scattered, numbered = (sem(n) for n in (
            "cc8", "chosen8", "prefix8", "places", "scattered", "numbered"))
        r8, exp8, comb8, ct_ps8, ct_sb8, b_ps8, b_sb8 = (sem(n) for n in (
            "r8", "exp8", "comb8", "ct_ps8", "ct_sb8", "b_ps8", "b_sb8"))

        with nc.Block() as block:
            @block.vector
            def _(dve):
                count = [0]

                def link(ins):
                    count[0] += 1
                    ins.then_inc(r8, 1)
                    dve.wait_ge(r8, count[0])

                e, chosen, rank = rt
                shape8 = [P, NT, NE1]
                link(nc.vector.tensor_reduce(small[:, :, 0], logits[:, :, :], AX.X, ALU.max))
                link(nc.vector.tensor_tensor(e[:, :, :], logits[:, :, :], small[:, :, 0:1].broadcast_to(shape8),
                                             ALU.subtract))
                ranks(link, logits[:, :, :], NE1, lower8[:, :], rank[:, :, :])
                dve.wait_ge(exp8, 1)
                link(nc.vector.tensor_scalar(chosen16[:, :].rearrange("p (t e) -> p t e", t=NT), rank[:, :, :], 2.0,
                                             None, ALU.is_lt))
                nc.vector.tensor_copy(small[:, 0, 0:1], small[:, 0, 0:1]).then_inc(chosen8, 1)
                link(nc.vector.scalar_tensor_tensor(e[:, :, :], rank[:, :, :], 2.0, e[:, :, :],
                                                    ALU.is_lt, ALU.mult))
                link(nc.vector.tensor_reduce(small[:, :, 0], e[:, :, :], AX.X, ALU.add))
                link(nc.vector.reciprocal(small[:, :, 1], small[:, :, 0]))
                link(nc.vector.tensor_tensor(comb[:, :, 0:NE1], e[:, :, :], small[:, :, 1:2].broadcast_to(shape8),
                                             ALU.mult))
                nc.vector.tensor_copy(small[:, 0, 0:1], small[:, 0, 0:1]).then_inc(comb8, 1)
                for k in range(2):
                    link(nc.vector.tensor_scalar(first[:, k, :, :], rank[:, :, :], float(k), None, ALU.is_equal))
                    link(nc.vector.tensor_tensor(chosen[:, :, :], first[:, k, :, :], comb[:, :, 0:NE1], ALU.mult))
                    link(nc.vector.tensor_reduce(weight[:, k, :], chosen[:, :, :], AX.X, ALU.add))
                count_e, tiles_e, before_e, end_e = (load_e[:, n, :] for n in range(4))
                dve.wait_ge(prefix8, 2)
                link(nc.vector.tensor_reduce(count_e, bank[5][:, 0:NT * NE1].rearrange("p (t e) -> p e t", t=NT),
                                             AX.X, ALU.add))
                link(nc.vector.tensor_scalar(tiles_e, count_e, P / 2 - 0.5, 1.0 / P, ALU.add, ALU.mult))
                link(nc.vector.tensor_scalar(tiles_e, tiles_e, ROUND, None, ALU.add))
                link(nc.vector.tensor_scalar(tiles_e, tiles_e, ROUND, None, ALU.subtract))
                square = pairs[:, 0:NE1 * NE1].rearrange("p (a b) -> p a b", a=NE1)
                link(nc.vector.tensor_tensor(square, lower8[:, :].rearrange("p (a b) -> p a b", a=NE1),
                                             tiles_e.unsqueeze(1).broadcast_to([P, NE1, NE1]), ALU.mult))
                link(nc.vector.tensor_reduce(before_e, square, AX.X, ALU.add))
                link(nc.vector.tensor_tensor(end_e, before_e, tiles_e, ALU.add))
                link(nc.vector.tensor_scalar(before_e, before_e, float(P), None, ALU.mult))
                link(nc.vector.tensor_tensor(rank[:, :, :], bank[4][:, 0:NT * NE1].rearrange("p (t e) -> p t e", t=NT),
                                             before_e.unsqueeze(1).broadcast_to(shape8), ALU.add))
                for k in range(2):
                    link(nc.vector.tensor_tensor(chosen[:, :, :], first[:, k, :, :], rank[:, :, :], ALU.mult))
                    link(nc.vector.tensor_reduce(place[:, k, :], chosen[:, :, :], AX.X, ALU.add))
                nc.vector.tensor_copy(place_i[:, :, :], place[:, :, :]).then_inc(places, 1)
                over = pairs[:, 0:SLOT_TILES * NE1].rearrange("p (n e) -> p n e", e=NE1)
                grid = [P, SLOT_TILES, NE1]
                link(nc.vector.tensor_tensor(over, end_e.unsqueeze(1).broadcast_to(grid),
                                             slot_no[:, :].unsqueeze(2).broadcast_to(grid), ALU.is_le))
                link(nc.vector.tensor_reduce(of_tile[:, :], over, AX.X, ALU.add))
                link(nc.vector.tensor_scalar(of_tile[:, :], of_tile[:, :], NE1 - 1.0, None, ALU.min))
                link(nc.vector.tensor_copy(of_tile_i[:, :], of_tile[:, :]))

                def add(t, u):
                    tile = h[:, ds(t, 1), :].rearrange("p a e -> p (a e)")
                    dve.wait_ge(b_ps8, t + 1)
                    nc.vector.tensor_tensor(tile, bank[2 + u][:, 0:E], tile, ALU.add).then_inc(b_sb8, 1)

                steps(dve, NT, [(add, 0)])

            @block.scalar
            def _(act):
                act.wait_ge(r8, 2)
                nc.scalar.activation(rt[0][:, :, :], rt[0][:, :, :], ACT.Exp).then_inc(exp8, 1)

                act.wait_ge(comb8, 1)

                def fetch(t, u):
                    wait(act, ct_ps8, t - 1)
                    nc.scalar.activation(combc[:, u, :], comb[:, ds(t, 1), 0:NE1].rearrange("p a e -> p (a e)"),
                                         ACT.Copy).then_inc(cc8, 1)

                def keep(t, u):
                    act.wait_ge(ct_ps8, t + 1)
                    wait(act, b_ps8, t - 1)
                    nc.scalar.activation(combT[:, u, :], bank[u][0:NE1, 0:P], ACT.Copy).then_inc(ct_sb8, 1)

                steps(act, NT, [(fetch, 0), (keep, 1)])

            @block.tensor
            def _(pe):
                pe.wait_ge(chosen8, 1)
                for d in range(1, NT):
                    nc.tensor.matmul(bank[4][:, d * NE1:NT * NE1], ones16[:, :], chosen16[:, 0:(NT - d) * NE1],
                                     start=(d == 1), stop=False, skip_group_check=True)
                nc.tensor.matmul(bank[4][:, 0:NT * NE1], upper16[:, :], chosen16[:, :], start=False, stop=True,
                                 skip_group_check=True).then_inc(prefix8, 1)
                nc.tensor.matmul(bank[5][:, 0:NT * NE1], ones16[:, :], chosen16[:, :], start=True, stop=True)\
                    .then_inc(prefix8, 1)

                def turn(t, u):
                    pe.wait_ge(cc8, t + 1)
                    wait(pe, ct_sb8, t - 1)
                    nc.tensor.matmul(bank[u][0:NE1, 0:P], combc[:, u, :], ident[:, :], start=True, stop=True)\
                        .then_inc(ct_ps8, 1)

                def bias(t, u):
                    pe.wait_ge(ct_sb8, t + 1)
                    wait(pe, b_sb8, t - 1)
                    nc.tensor.matmul(bank[2 + u][:, 0:E], combT[:, u, :], b2r[:, :], start=True, stop=True)\
                        .then_inc(b_ps8, 1)

                steps(pe, NT, [(turn, 0), (bias, 1)])

            @block.gpsimd
            def _(pool):
                nc.gpsimd.tensor_copy(rows_x[:, :, E], token_no[:, :]).then_inc(numbered, 1)
                pool.wait_ge(places, 1)
                for k in range(2):
                    pool.wait_ge(numbered, k + 1)
                    for t in range(NT):
                        pool.indirect_dma_start(
                            out=x_slots, out_offset=bass.IndirectOffsetOnAxis(ap=place_i[:, k, t:t + 1], axis=0),
                            in_=rows_x[:, t, :], in_offset=None).then_inc(scattered, 16)
                    pool.wait_ge(scattered, 16 * NT * (k + 1))
                    if k == 0:
                        nc.gpsimd.tensor_scalar(rows_x[:, :, E], token_no[:, :], float(T), None, ALU.add)\
                            .then_inc(numbered, 1)

        xs_loaded = [sem(f"xs_loaded{u}") for u in range(2)]
        y_stored = [sem(f"y_stored{u}") for u in range(2)]
        ones_row, tr9, xt9, up9, ra9, rd9, turn9, ta9, td9, y9, yc9 = (sem(n) for n in (
            "ones_row", "tr9", "xt9", "up9", "ra9", "rd9", "turn9", "ta9", "td9", "y9", "yc9"))
        numbers_kept, row_ready = sem("numbers_kept"), sem("row_ready")
        FH = FF // 2

        with nc.Block() as block:
            @block.sync
            def _(sp):
                def load(t, u):
                    wait(sp, tr9, t - 1)
                    wait(sp, numbers_kept, t - 1)
                    sp.dma_start(xs[:, u, :], x_slots[ds(t * P, P), :]).then_inc(xs_loaded[u], 16)

                steps(sp, SLOT_TILES, [(load, 0)])

            @block.gpsimd
            def _(pool):
                for u in range(2):
                    nc.gpsimd.memset(xsT[EH:EH + 1, u, :, :], 1.0).then_inc(ones_row, 1)

                pool.wait_ge(ones_row, 2)

                def keep_numbers(t, u):
                    pool.wait_ge(xs_loaded[u], in_slot(t, u))
                    nc.gpsimd.tensor_copy(rows_of[:, ds(t, 1)], xs[:, u, E:E + 1]).then_inc(numbers_kept, 1)

                def send(t, u):
                    pool.wait_ge(numbers_kept, t + 1)
                    wait(pool, y_stored[u], in_slot(t, u) - 16)
                    nc.gpsimd.tensor_copy(row_i[:, u:u + 1], rows_of[:, ds(t, 1)]).then_inc(row_ready, 1)
                    wait_alone(pool, row_ready, t + 1, passed)
                    wait_alone(pool, yc9, t + 1, passed)
                    pool.indirect_dma_start(
                        out=y_rows, out_offset=bass.IndirectOffsetOnAxis(ap=row_i[:, u:u + 1], axis=0),
                        in_=y_out[:, u, :], in_offset=None).then_inc(y_stored[u], 16)

                steps(pool, SLOT_TILES, [(send, 5), (keep_numbers, 1)])
                for u in range(2):
                    pool.wait_ge(y_stored[u], 8 * SLOT_TILES)

            @block.tensor
            def _(pe):
                pe.wait_ge(w1_loaded, 16 * (NE1 + 1))
                pe.wait_ge(w2_loaded, 16 * NE1)
                pe.wait_ge(ones_row, 2)

                def turn_x(t, u):
                    pe.wait_ge(xs_loaded[u], in_slot(t, u))
                    wait(pe, xt9, t - 1)
                    for c in range(2):
                        mm = nc.tensor.transpose(bank[4 + u][0:EH, c * P:(c + 1) * P],
                                                 xs[:, u, c * EH:(c + 1) * EH], ident[:, :])
                    mm.then_inc(tr9, 1)

                def up(t, u):
                    expert = pe.value_load(of_tile_i[0:1, ds(t, 1)], min_val=0, max_val=NE1 - 1)
                    wait_alone(pe, xt9, t + 1, passed)
                    for half in range(2):
                        wait(pe, (ra9, rd9)[half], t)
                        for c in range(2):
                            rows = EH + c
                            mm = nc.tensor.matmul(
                                bank[half][:, 0:FH], xsT[0:rows, u, c, :],
                                w1_all[0:rows, ds(expert, 1), c, half * FH:(half + 1) * FH]
                                .rearrange("p a f -> p (a f)"), start=(c == 0), stop=(c == 1))
                        mm.then_inc(up9, 1)

                def turn_h(t, u):
                    for half in range(2):
                        pe.wait_ge((ra9, rd9)[half], t + 1)
                        wait(pe, (ta9, td9)[half], t)
                        for c in range(FC // 2):
                            at = half * FH + c * P
                            mm = nc.tensor.transpose(bank[2 + half][:, c * P:(c + 1) * P],
                                                     hidden[:, u, at:at + P], ident[:, :])
                        mm.then_inc(turn9, 1)

                def down(t, u):
                    expert = pe.value_load(of_tile_i[0:1, ds(t, 1)], min_val=0, max_val=NE1 - 1)
                    wait_alone(pe, ta9, t + 1, passed)
                    wait_alone(pe, td9, t + 1, passed)
                    wait_alone(pe, yc9, t - 1, passed)
                    for c in range(FC):
                        mm = nc.tensor.matmul(bank[6 + u][:, 0:E], hiddenT[:, u, c * P:(c + 1) * P],
                                              w2_all[:, ds(expert, 1), c, :].rearrange("p a n -> p (a n)"),
                                              start=(c == 0), stop=(c == FC - 1))
                    mm.then_inc(y9, 1)

                steps(pe, SLOT_TILES, [(down, 4), (turn_h, 3), (up, 2), (turn_x, 1)])

            @block.scalar
            def _(act):
                def copy_x(t, u):
                    act.wait_ge(tr9, t + 1)
                    wait(act, up9, 2 * t - 2)
                    nc.scalar.activation(xsT[0:EH, u, :, :].rearrange("p c t -> p (c t)"), bank[4 + u][0:EH, 0:2 * P],
                                         ACT.Copy).then_inc(xt9, 1)

                def relu(t, u):
                    act.wait_ge(up9, 2 * t + 1)
                    wait(act, turn9, 2 * t - 2)
                    nc.scalar.activation(hidden[:, u, 0:FH], bank[0][:, 0:FH], ACT.Relu).then_inc(ra9, 1)

                def keep(t, u):
                    act.wait_ge(turn9, 2 * t + 1)
                    wait(act, y9, t - 1)
                    nc.scalar.activation(hiddenT[:, u, 0:FH], bank[2][:, 0:FH], ACT.Copy).then_inc(ta9, 1)

                steps(act, SLOT_TILES, [(keep, 3), (relu, 2), (copy_x, 1)])

            @block.vector
            def _(dve):
                def relu(t, u):
                    dve.wait_ge(up9, 2 * t + 2)
                    wait(dve, turn9, 2 * t - 2)
                    nc.vector.tensor_scalar(hidden[:, u, FH:FF], bank[1][:, 0:FH], 0.0, None, ALU.max)\
                        .then_inc(rd9, 1)

                def keep(t, u):
                    dve.wait_ge(turn9, 2 * t + 2)
                    wait(dve, y9, t - 1)
                    nc.vector.tensor_copy(hiddenT[:, u, FH:FF], bank[3][:, 0:FH]).then_inc(td9, 1)

                def output(t, u):
                    dve.wait_ge(y9, t + 1)
                    wait(dve, y_stored[u], in_slot(t, u) - 16)
                    nc.vector.tensor_copy(y_out[:, u, :], bank[6 + u][:, 0:E]).then_inc(yc9, 1)

                steps(dve, SLOT_TILES, [(output, 4), (keep, 3), (relu, 2)])

        fetched = [sem(f"fetched{b}") for b in range(NB)]
        sum10, out10, stored = sem("sum10"), sem("out10"), sem("stored")

        with nc.Block() as block:
            @block.scalar
            def _(act):
                for b in range(NB):
                    for k in range(2):
                        rows = y_rows[k * T + b * BLK:k * T + (b + 1) * BLK, :]
                        act.dma_start(y_in[:, k, b * TPB:(b + 1) * TPB, :], rows.rearrange("(n p) e -> p n e", p=P))\
                            .then_inc(fetched[b], 16)

            @block.vector
            def _(dve):
                for t in range(NT):
                    dve.wait_ge(fetched[t // TPB], 32)
                    nc.vector.scalar_tensor_tensor(h[:, t, :], y_in[:, 0, t, :], weight[:, 0, t:t + 1], h[:, t, :],
                                                   ALU.mult, ALU.add).then_inc(sum10, 1)
                    dve.wait_ge(sum10, t + 1)
                    nc.vector.scalar_tensor_tensor(h[:, t, :], y_in[:, 1, t, :], weight[:, 1, t:t + 1], h[:, t, :],
                                                   ALU.mult, ALU.add).then_inc(out10, 1)

            @block.sync
            def _(sp):
                out_v = out.rearrange("(n p) e -> p n e", p=P)
                for b in range(NB):
                    sp.wait_ge(out10, TPB * (b + 1))
                    sp.dma_start(out_v[:, b * TPB:(b + 1) * TPB, :], h[:, b * TPB:(b + 1) * TPB, :])\
                        .then_inc(stored, 16)
                sp.wait_ge(stored, 16 * NB)


def kernel(**inputs):
    import numpy as np
    import concourse.bacc as bacc
    from concourse import mybir as mb
    from concourse.bass_utils import run_bass_kernel_spmd

    i = {k: np.asarray(v) for k, v in inputs.items()}

    def rows(w):
        return w.reshape(2, EH, -1).transpose(1, 0, 2)

    def column(b):
        return b.reshape(-1, EH).T

    x = i["x"].reshape(IMAGES, CHANS, 4, PATCH, 4, PATCH).transpose(1, 3, 5, 0, 2, 4)
    x = x.reshape(KC, P, NT, P).transpose(2, 1, 0, 3).reshape(NT, P, KC * P)
    near = i["L0_attn_rel_table"][P - 1 - (S - 1):P - 1 + S]
    up = np.stack([np.concatenate([i["L0_ffn_" + w], i["L0_ffn_s" + w][None]]) for w in ("w1", "w3")])
    down = np.concatenate([i["L0_ffn_w2"], i["L0_ffn_sw2"][None]])
    p = np.arange(P)
    arrays = {
        "x": x,
        "L0_tok_pinv": i["L0_tok_pinv"].T.reshape(OC, P, PATCH * PATCH).transpose(1, 0, 2),
        "L0_tok_proj_weight": i["L0_tok_proj_weight"].reshape(E, CHANS, OC, P).transpose(3, 2, 1, 0)
        .reshape(P, OC, CHANS * E),
        "rel": rows(near.T), "rel_reversed": rows(near[::-1].T),
        "L0_attn_columns": np.stack([column(i["L0_attn_b" + n]) for n in ("q", "k", "pk", "pq")], 1),
        "L1_attn_columns": np.stack([column(i["L1_attn_b_qkv"][n * E:(n + 1) * E]) for n in range(2)], 1),
        "L1_attn_b_v": i["L1_attn_b_qkv"][2 * E:],
        "L0_ffn_gate_weight": rows(i["L0_ffn_gate_weight"].T), "L1_ffn_Wr": rows(i["L1_ffn_Wr"]),
        "L0_ffn_w13": up.reshape(2, NE0 + 1, INTER, 2, EH).transpose(4, 0, 1, 3, 2),
        "L0_ffn_w2": down.transpose(2, 0, 1),
        "L1_attn_w_qkv": rows(i["L1_attn_w_qkv"]), "L1_attn_w_proj": rows(i["L1_attn_w_proj"]),
        "L1_ffn_W1": i["L1_ffn_W1"].reshape(NE1, 2, EH, FF).transpose(0, 2, 1, 3).reshape(NE1, EH, 2 * FF),
        "L1_ffn_W2": i["L1_ffn_W2"].reshape(NE1, FC, P, E).transpose(0, 2, 1, 3).reshape(NE1, P, FC * E),
        "L1_ffn_b1": i["L1_ffn_b1"][None], "L1_ffn_b2": i["L1_ffn_b2"],
        "upper": np.triu(np.ones((P, P), np.float32), 1),
        "slot_numbers": np.broadcast_to(np.arange(SLOT_TILES, dtype=np.float32), (P, SLOT_TILES)),
        "token_numbers": np.arange(T, dtype=np.float32).reshape(NT, P).T,
        "idle_rows": np.arange(2 * T, 2 * T + SLOT_TILES * P, dtype=np.float32)[:, None],
        "ident": np.eye(P, dtype=np.float32),
        "hmask": np.equal(np.arange(EH)[:, None] // D, np.arange(HG)[None]).astype(np.float32),
        "lower4": np.broadcast_to(np.tril(np.ones((GROUPS, GROUPS), np.float32), -1).reshape(1, -1), (P, GROUPS ** 2)),
        "lower8": np.broadcast_to(np.tril(np.ones((NE0, NE0), np.float32), -1).reshape(1, -1), (P, NE0 ** 2)),
    }
    for n in ("Wq", "Wk", "Wv", "Wo", "Wpk", "Wpq"):
        arrays["L0_attn_" + n] = rows(i["L0_attn_" + n])
    for n in ("L0_tok_proj_bias", "L0_attn_bv", "L0_attn_bo", "L1_attn_b_proj", "L0_ffn_gate_bias"):
        arrays[n] = i[n]
    arrays = {k: np.ascontiguousarray(v) for k, v in arrays.items()}

    nc = bacc.Bacc("TRN2", target_bir_lowering=False, num_devices=1)
    aps = {k: nc.dram_tensor("in_" + k, v.shape, mb.dt.from_np(v.dtype), kind="ExternalInput").ap()
           for k, v in arrays.items()}
    out = nc.dram_tensor("out", (T, E), mb.dt.float32, kind="ExternalOutput").ap()
    tower(nc, aps, out)
    r = run_bass_kernel_spmd(nc, [{"in_" + k: v for k, v in arrays.items()}], core_ids=[0])
    return r.results[0]["out"].reshape(IMAGES, S, E)
```
